# Optimizing a Trainium2 kernel written in Bass

```python
import numpy as np
import jax
import jax.numpy as jnp

def _softmax(x, axis=-1):
    return jax.nn.softmax(x, axis=axis)

def _gelu(x):
    return jax.nn.gelu(x, approximate=True)

def _silu(x):
    return jax.nn.silu(x)

def _sigmoid(x):
    return jax.nn.sigmoid(x)

def _layernorm(x, axis=-1, eps=1e-05):
    m = jnp.mean(x, axis=axis, keepdims=True)
    v = jnp.var(x, axis=axis, keepdims=True)
    return (x - m) / jnp.sqrt(v + eps)

def _scatter_add(tgt, idx, src, axis=0):
    return tgt.at[idx].add(src)

def _segment_sum(src, seg, n):
    return jax.ops.segment_sum(src, seg, n)
kernel_name = 'mk_recurrent_d2_jaxref_r8_ba669b'

def setup_inputs(seed: int=0):
    np.random.seed(seed)
    _w = jnp.asarray

    def _L0_attn_setup():
        import jax, jax.numpy as jnp
        import numpy as np
        DIM, H, P, N = (256, 32, 64, 128)
        K = 4

        def _causal_conv(u, w):
            T = u.shape[1]
            up = jnp.pad(u, ((0, 0), (K - 1, 0), (0, 0), (0, 0)))
            out = jnp.zeros_like(u)
            for k in range(K):
                out = out + up[:, k:k + T] * w[:, :, k]
            return out
        key = jax.random.key(seed)
        ks = jax.random.split(key, 8)
        proj_dim = 2 * H * P + 2 * H * N + H
        x = jax.random.normal(ks[0], (2, 256, DIM), dtype=jnp.float32)
        Win = jax.random.normal(ks[1], (proj_dim, DIM), dtype=jnp.float32) * 0.02
        Wout = jax.random.normal(ks[2], (DIM, H * P), dtype=jnp.float32) * 0.02
        A_log = jnp.linspace(-3.0, -1.0, H, dtype=jnp.float32)
        dt_bias = jnp.zeros((H,), dtype=jnp.float32)
        conv_w_x = jax.random.normal(ks[3], (H, P, K), dtype=jnp.float32) * 0.1
        conv_w_b = jax.random.normal(ks[4], (H, N, K), dtype=jnp.float32) * 0.1
        conv_w_c = jax.random.normal(ks[5], (H, N, K), dtype=jnp.float32) * 0.1
        return {'x': x, 'Win': Win, 'Wout': Wout, 'A_log': A_log, 'dt_bias': dt_bias, 'conv_w_x': conv_w_x, 'conv_w_b': conv_w_b, 'conv_w_c': conv_w_c}
    _L0_attn_in = _L0_attn_setup()

    def _L0_ffn_setup():
        import jax, jax.numpy as jnp
        import numpy as np
        EPS = 1e-06
        K_STEPS = 4
        USE_GATING = True

        def layer_norm(x, gamma, beta):
            mu = jnp.mean(x, axis=-1, keepdims=True)
            var = jnp.mean(jnp.square(x - mu), axis=-1, keepdims=True)
            return (x - mu) * jax.lax.rsqrt(var + EPS) * gamma + beta
        key = jax.random.key(seed)
        B, L, D, H = (4, 512, 256, 1024)
        ks = jax.random.split(key, 16)
        s = 0.02
        return {'x': jax.random.normal(ks[0], (B, L, D), dtype=jnp.float32), 'in_gamma': jnp.ones((D,), jnp.float32), 'in_beta': jnp.zeros((D,), jnp.float32), 'agg_w': jax.random.normal(ks[1], (D, D), jnp.float32) * s, 'agg_b': jnp.zeros((D,), jnp.float32), 'pn_gamma': jnp.ones((D,), jnp.float32), 'pn_beta': jnp.zeros((D,), jnp.float32), 'd1_w': jax.random.normal(ks[2], (D, H), jnp.float32) * s, 'd1_b': jnp.zeros((H,), jnp.float32), 'd2_w': jax.random.normal(ks[3], (H, D), jnp.float32) * s, 'd2_b': jnp.zeros((D,), jnp.float32), 'bc_w': jax.random.normal(ks[4], (D, D), jnp.float32) * s, 'bc_b': jnp.zeros((D,), jnp.float32), 'gate_w': jax.random.normal(ks[5], (D, D), jnp.float32) * s, 'gate_b': jnp.zeros((D,), jnp.float32), 'out_gamma': jnp.ones((D,), jnp.float32), 'out_beta': jnp.zeros((D,), jnp.float32)}
    _L0_ffn_in = _L0_ffn_setup()

    def _L1_attn_setup():
        import jax, jax.numpy as jnp
        import numpy as np
        import math
        B, S, DIM = (2, 256, 256)
        H, NOPE, ROPE, VDIM = (16, 128, 64, 128)
        Q_RANK, KV_RANK = (128, 64)
        EPS = 1e-06
        ROPE_THETA = 10000.0

        def _rmsnorm(x, w, eps=EPS):
            return x * jax.lax.rsqrt(jnp.mean(x * x, axis=-1, keepdims=True) + eps) * w

        def _rope_cos_sin(seq_len, head_dim, dtype=jnp.float32):
            inv_freq = 1.0 / ROPE_THETA ** (jnp.arange(0, head_dim, 2, dtype=jnp.float32) / head_dim)
            t = jnp.arange(seq_len, dtype=jnp.float32)
            freqs = jnp.outer(t, inv_freq)
            return (jnp.cos(freqs).astype(dtype), jnp.sin(freqs).astype(dtype))

        def _apply_rope(x, cos, sin):
            x1, x2 = (x[..., 0::2], x[..., 1::2])
            c = cos[None, :, None, :]
            s = sin[None, :, None, :]
            o1 = x1 * c - x2 * s
            o2 = x1 * s + x2 * c
            return jnp.stack([o1, o2], axis=-1).reshape(x.shape)
        key = jax.random.key(seed)
        ks = jax.random.split(key, 9)
        s = 0.02
        return {'x': jax.random.normal(ks[0], (B, S, DIM), jnp.float32), 'wq_down': jax.random.normal(ks[1], (Q_RANK, DIM), jnp.float32) * s, 'q_norm_w': jnp.ones((Q_RANK,), jnp.float32), 'wq_up': jax.random.normal(ks[2], (H * NOPE, Q_RANK), jnp.float32) * s, 'wq_rope': jax.random.normal(ks[3], (H * ROPE, Q_RANK), jnp.float32) * s, 'wkv_down': jax.random.normal(ks[4], (KV_RANK, DIM), jnp.float32) * s, 'kv_norm_w': jnp.ones((KV_RANK,), jnp.float32), 'wkv_up': jax.random.normal(ks[5], (H * (NOPE + VDIM), KV_RANK), jnp.float32) * s, 'wk_rope': jax.random.normal(ks[6], (ROPE, DIM), jnp.float32) * s, 'wo': jax.random.normal(ks[7], (DIM, H * VDIM), jnp.float32) * s}
    _L1_attn_in = _L1_attn_setup()

    def _L1_ffn_setup():
        import jax, jax.numpy as jnp
        import numpy as np
        B, S, D, E, TOPK = (4, 256, 256, 8, 2)
        key = jax.random.key(seed)
        k1, k2, k3 = jax.random.split(key, 3)
        x = jax.random.normal(k1, (B, S, D), dtype=jnp.float32)
        gate_w = jax.random.normal(k2, (E, D), dtype=jnp.float32) * 0.02
        expert_w = jax.random.normal(k3, (E, D, D), dtype=jnp.float32) / np.sqrt(D)
        expert_b = jnp.zeros((E, D), dtype=jnp.float32)
        return {'x': x, 'gate_w': gate_w, 'expert_w': expert_w, 'expert_b': expert_b}
    _L1_ffn_in = _L1_ffn_setup()
    _d = {'L0_attn_x': _L0_attn_in['x'], 'L0_attn_Win': _L0_attn_in['Win'], 'L0_attn_Wout': _L0_attn_in['Wout'], 'L0_attn_A_log': _L0_attn_in['A_log'], 'L0_attn_dt_bias': _L0_attn_in['dt_bias'], 'L0_attn_conv_w_x': _L0_attn_in['conv_w_x'], 'L0_attn_conv_w_b': _L0_attn_in['conv_w_b'], 'L0_attn_conv_w_c': _L0_attn_in['conv_w_c'], 'L0_ffn_in_gamma': _L0_ffn_in['in_gamma'], 'L0_ffn_in_beta': _L0_ffn_in['in_beta'], 'L0_ffn_agg_w': _L0_ffn_in['agg_w'], 'L0_ffn_agg_b': _L0_ffn_in['agg_b'], 'L0_ffn_pn_gamma': _L0_ffn_in['pn_gamma'], 'L0_ffn_pn_beta': _L0_ffn_in['pn_beta'], 'L0_ffn_d1_w': _L0_ffn_in['d1_w'], 'L0_ffn_d1_b': _L0_ffn_in['d1_b'], 'L0_ffn_d2_w': _L0_ffn_in['d2_w'], 'L0_ffn_d2_b': _L0_ffn_in['d2_b'], 'L0_ffn_bc_w': _L0_ffn_in['bc_w'], 'L0_ffn_bc_b': _L0_ffn_in['bc_b'], 'L0_ffn_gate_w': _L0_ffn_in['gate_w'], 'L0_ffn_gate_b': _L0_ffn_in['gate_b'], 'L0_ffn_out_gamma': _L0_ffn_in['out_gamma'], 'L0_ffn_out_beta': _L0_ffn_in['out_beta'], 'L1_attn_wq_down': _L1_attn_in['wq_down'], 'L1_attn_q_norm_w': _L1_attn_in['q_norm_w'], 'L1_attn_wq_up': _L1_attn_in['wq_up'], 'L1_attn_wq_rope': _L1_attn_in['wq_rope'], 'L1_attn_wkv_down': _L1_attn_in['wkv_down'], 'L1_attn_kv_norm_w': _L1_attn_in['kv_norm_w'], 'L1_attn_wkv_up': _L1_attn_in['wkv_up'], 'L1_attn_wk_rope': _L1_attn_in['wk_rope'], 'L1_attn_wo': _L1_attn_in['wo'], 'L1_ffn_gate_w': _L1_ffn_in['gate_w'], 'L1_ffn_expert_w': _L1_ffn_in['expert_w'], 'L1_ffn_expert_b': _L1_ffn_in['expert_b']}
    _x0 = _d['L0_attn_x']
    _d['L0_attn_x'] = jax.random.normal(jax.random.fold_in(jax.random.key(seed), 1), (4, 512, 256), dtype=_x0.dtype)
    del _x0
    return _d

def reference(L0_attn_x, L0_attn_Win, L0_attn_Wout, L0_attn_A_log, L0_attn_dt_bias, L0_attn_conv_w_x, L0_attn_conv_w_b, L0_attn_conv_w_c, L0_ffn_in_gamma, L0_ffn_in_beta, L0_ffn_agg_w, L0_ffn_agg_b, L0_ffn_pn_gamma, L0_ffn_pn_beta, L0_ffn_d1_w, L0_ffn_d1_b, L0_ffn_d2_w, L0_ffn_d2_b, L0_ffn_bc_w, L0_ffn_bc_b, L0_ffn_gate_w, L0_ffn_gate_b, L0_ffn_out_gamma, L0_ffn_out_beta, L1_attn_wq_down, L1_attn_q_norm_w, L1_attn_wq_up, L1_attn_wq_rope, L1_attn_wkv_down, L1_attn_kv_norm_w, L1_attn_wkv_up, L1_attn_wk_rope, L1_attn_wo, L1_ffn_gate_w, L1_ffn_expert_w, L1_ffn_expert_b):

    def _L0_attn_ref(x, Win, Wout, A_log, dt_bias, conv_w_x, conv_w_b, conv_w_c):
        import jax, jax.numpy as jnp
        import numpy as np
        DIM, H, P, N = (256, 32, 64, 128)
        K = 4

        def _causal_conv(u, w):
            T = u.shape[1]
            up = jnp.pad(u, ((0, 0), (K - 1, 0), (0, 0), (0, 0)))
            out = jnp.zeros_like(u)
            for k in range(K):
                out = out + up[:, k:k + T] * w[:, :, k]
            return out
        B, T, _ = x.shape
        proj = x @ Win.T
        x_ssm = proj[..., :H * P].reshape(B, T, H, P)
        z = proj[..., H * P:2 * H * P].reshape(B, T, H, P)
        Bm = proj[..., 2 * H * P:2 * H * P + H * N].reshape(B, T, H, N)
        Cm = proj[..., 2 * H * P + H * N:2 * H * P + 2 * H * N].reshape(B, T, H, N)
        dt_raw = proj[..., 2 * H * P + 2 * H * N:]
        dt = jax.nn.softplus(dt_raw + dt_bias)
        xc = jax.nn.silu(_causal_conv(x_ssm, conv_w_x))
        Bc = jax.nn.silu(_causal_conv(Bm, conv_w_b))
        Cc = jax.nn.silu(_causal_conv(Cm, conv_w_c))
        A = -jnp.exp(A_log)
        decay = jnp.exp(dt * A)
        dtx = dt[..., None] * xc

        def step(h, inp):
            dec_t, dtx_t, B_t, C_t = inp
            h = dec_t[..., None, None] * h + dtx_t[..., None] * B_t[:, :, None, :]
            y = jnp.einsum('bhpn,bhn->bhp', h, C_t)
            return (h, y)
        h0 = jnp.zeros((B, H, P, N), dtype=x.dtype)
        xs = (jnp.moveaxis(decay, 1, 0), jnp.moveaxis(dtx, 1, 0), jnp.moveaxis(Bc, 1, 0), jnp.moveaxis(Cc, 1, 0))
        _, ys = jax.lax.scan(step, h0, xs)
        y = jnp.moveaxis(ys, 0, 1)
        y = y * jax.lax.rsqrt(jnp.mean(y * y, axis=-1, keepdims=True) + 1e-06)
        y = y * jax.nn.silu(z)
        return y.reshape(B, T, H * P) @ Wout.T

    def _L0_ffn_ref(x, in_gamma, in_beta, agg_w, agg_b, pn_gamma, pn_beta, d1_w, d1_b, d2_w, d2_b, bc_w, bc_b, gate_w, gate_b, out_gamma, out_beta):
        import jax, jax.numpy as jnp
        import numpy as np
        EPS = 1e-06
        K_STEPS = 4
        USE_GATING = True

        def layer_norm(x, gamma, beta):
            mu = jnp.mean(x, axis=-1, keepdims=True)
            var = jnp.mean(jnp.square(x - mu), axis=-1, keepdims=True)
            return (x - mu) * jax.lax.rsqrt(var + EPS) * gamma + beta
        x_norm = layer_norm(x, in_gamma, in_beta)
        thought = x_norm[:, -1, :] @ agg_w + agg_b
        for _ in range(K_STEPS):
            t = layer_norm(thought, pn_gamma, pn_beta)
            t = jax.nn.gelu(t @ d1_w + d1_b, approximate=False)
            thought = thought + (t @ d2_w + d2_b)
        broadcast = (thought @ bc_w + bc_b)[:, None, :]
        if USE_GATING:
            gate = jax.nn.sigmoid(x @ gate_w + gate_b)
            out = x + gate * broadcast
        else:
            out = x + broadcast
        return layer_norm(out, out_gamma, out_beta)

    def _L1_attn_ref(x, wq_down, q_norm_w, wq_up, wq_rope, wkv_down, kv_norm_w, wkv_up, wk_rope, wo):
        import jax, jax.numpy as jnp
        import numpy as np
        import math
        B, S, DIM = (2, 256, 256)
        H, NOPE, ROPE, VDIM = (16, 128, 64, 128)
        Q_RANK, KV_RANK = (128, 64)
        EPS = 1e-06
        ROPE_THETA = 10000.0

        def _rmsnorm(x, w, eps=EPS):
            return x * jax.lax.rsqrt(jnp.mean(x * x, axis=-1, keepdims=True) + eps) * w

        def _rope_cos_sin(seq_len, head_dim, dtype=jnp.float32):
            inv_freq = 1.0 / ROPE_THETA ** (jnp.arange(0, head_dim, 2, dtype=jnp.float32) / head_dim)
            t = jnp.arange(seq_len, dtype=jnp.float32)
            freqs = jnp.outer(t, inv_freq)
            return (jnp.cos(freqs).astype(dtype), jnp.sin(freqs).astype(dtype))

        def _apply_rope(x, cos, sin):
            x1, x2 = (x[..., 0::2], x[..., 1::2])
            c = cos[None, :, None, :]
            s = sin[None, :, None, :]
            o1 = x1 * c - x2 * s
            o2 = x1 * s + x2 * c
            return jnp.stack([o1, o2], axis=-1).reshape(x.shape)
        bs, seq_len, _ = x.shape
        q_c = _rmsnorm(x @ wq_down.T, q_norm_w)
        q_nope = (q_c @ wq_up.T).reshape(bs, seq_len, H, NOPE)
        q_pe = (q_c @ wq_rope.T).reshape(bs, seq_len, H, ROPE)
        kv_c = _rmsnorm(x @ wkv_down.T, kv_norm_w)
        kv_up = (x_kv := (kv_c @ wkv_up.T)).reshape(bs, seq_len, H, NOPE + VDIM)
        k_nope, v = (kv_up[..., :NOPE], kv_up[..., NOPE:])
        k_rope_shared = (x @ wk_rope.T).reshape(bs, seq_len, 1, ROPE)
        cos, sin = _rope_cos_sin(seq_len, ROPE, x.dtype)
        q_pe = _apply_rope(q_pe, cos, sin)
        k_rope_shared = _apply_rope(k_rope_shared, cos, sin)
        k_rope = jnp.broadcast_to(k_rope_shared, (bs, seq_len, H, ROPE))
        q = jnp.concatenate([q_nope, q_pe], axis=-1)
        k = jnp.concatenate([k_nope, k_rope], axis=-1)
        scale = 1.0 / math.sqrt(NOPE + ROPE)
        scores = jnp.einsum('bqhd,bkhd->bhqk', q, k) * scale
        causal = jnp.tril(jnp.ones((seq_len, seq_len), bool))
        scores = jnp.where(causal[None, None], scores, -jnp.inf)
        probs = jax.nn.softmax(scores.astype(jnp.float32), axis=-1).astype(q.dtype)
        out = jnp.einsum('bhqk,bkhv->bqhv', probs, v).reshape(bs, seq_len, H * VDIM)
        return out @ wo.T

    def _L1_ffn_ref(x, gate_w, expert_w, expert_b):
        import jax, jax.numpy as jnp
        import numpy as np
        B, S, D, E, TOPK = (4, 256, 256, 8, 2)
        batch_shape = x.shape[:-1]
        xf = x.reshape(-1, x.shape[-1])
        T = xf.shape[0]
        logits = jnp.einsum('td,ed->te', xf, gate_w)
        top_w, top_i = jax.lax.top_k(logits, TOPK)
        top_w = jax.nn.softmax(top_w.astype(jnp.float32), axis=-1).astype(x.dtype)
        gates = jnp.zeros((T, logits.shape[-1]), dtype=x.dtype)
        gates = gates.at[jnp.arange(T)[:, None], top_i].set(top_w)
        y = jnp.einsum('td,edo->eto', xf, expert_w) + expert_b[:, None, :]
        out = jnp.einsum('te,eto->to', gates, y)
        return out.reshape(*batch_shape, -1)
    x = L0_attn_x
    xn = _layernorm(x, axis=-1)
    s = _L0_attn_ref(xn, L0_attn_Win, L0_attn_Wout, L0_attn_A_log, L0_attn_dt_bias, L0_attn_conv_w_x, L0_attn_conv_w_b, L0_attn_conv_w_c)
    g = _silu(_L0_ffn_ref(xn, L0_ffn_in_gamma, L0_ffn_in_beta, L0_ffn_agg_w, L0_ffn_agg_b, L0_ffn_pn_gamma, L0_ffn_pn_beta, L0_ffn_d1_w, L0_ffn_d1_b, L0_ffn_d2_w, L0_ffn_d2_b, L0_ffn_bc_w, L0_ffn_bc_b, L0_ffn_gate_w, L0_ffn_gate_b, L0_ffn_out_gamma, L0_ffn_out_beta))
    x = x + s * g
    xn = _layernorm(x, axis=-1)
    s = _L1_attn_ref(xn, L1_attn_wq_down, L1_attn_q_norm_w, L1_attn_wq_up, L1_attn_wq_rope, L1_attn_wkv_down, L1_attn_kv_norm_w, L1_attn_wkv_up, L1_attn_wk_rope, L1_attn_wo)
    g = _silu(_L1_ffn_ref(xn, L1_ffn_gate_w, L1_ffn_expert_w, L1_ffn_expert_b))
    x = x + s * g
    return x

_drawn_inputs = setup_inputs


def setup_inputs(seed=0):
    import zlib

    import numpy as np

    out = dict(_drawn_inputs(seed))
    spreads = {'L0_attn_dt_bias': (0.0, 0.8),
     'L0_ffn_in_gamma': (1.0, 0.6),
     'L0_ffn_in_beta': (0.0, 0.8),
     'L0_ffn_agg_b': (0.0, 0.8),
     'L0_ffn_pn_gamma': (1.0, 0.6),
     'L0_ffn_pn_beta': (0.0, 0.8),
     'L0_ffn_d1_b': (0.0, 0.8),
     'L0_ffn_d2_b': (0.0, 0.8),
     'L0_ffn_bc_b': (0.0, 0.8),
     'L0_ffn_gate_b': (0.0, 0.8),
     'L0_ffn_out_gamma': (1.0, 0.6),
     'L0_ffn_out_beta': (0.0, 0.8),
     'L1_attn_q_norm_w': (1.0, 0.6),
     'L1_attn_kv_norm_w': (1.0, 0.6),
     'L1_ffn_expert_b': (0.0, 0.8)}
    factors = {'L0_attn_A_log': 2.862,
     'L0_ffn_agg_w': 8.0,
     'L0_ffn_d1_w': 8.0,
     'L0_ffn_d2_w': 8.0,
     'L0_ffn_bc_w': 8.0,
     'L0_ffn_gate_w': 8.0,
     'L1_attn_wq_down': 8.0,
     'L1_attn_wq_up': 8.0,
     'L1_attn_wq_rope': 8.0,
     'L1_attn_wkv_down': 7.961,
     'L1_attn_wkv_up': 8.0,
     'L1_attn_wk_rope': 8.0,
     'L1_attn_wo': 8.0,
     'L1_ffn_gate_w': 8.0,
     'L1_ffn_expert_w': 8.0}
    for name, (base, spread) in spreads.items():
        noise = np.random.default_rng([zlib.crc32(name.encode()), seed]).standard_normal(out[name].shape)
        drawn = base * np.exp(spread * noise) if base else spread * noise
        out[name] = jnp.asarray(drawn.astype(out[name].dtype))
    for name, factor in factors.items():
        out[name] = (out[name] * factor).astype(out[name].dtype)
    return out
```

```python
from collections import namedtuple
from contextlib import ExitStack

import concourse.bass as bass
import numpy as np
from concourse import mybir

F32 = mybir.dt.float32
BF16 = mybir.dt.bfloat16
ACT = mybir.ActivationFunctionType
ALU = mybir.AluOpType
AX = mybir.AxisListType.X

B, T, D = 4, 512, 256
TOK = B * T
TILES = TOK // 128
KD = D // 128
H, P, N, TAPS = 32, 64, 128, 4
PAIRS = H // 2
CH = T // 128
CHANNELS = 2 * P * 2 + 4 * N
CONVS = 5
PACK_CONV = KD * CHANNELS
PACK = PACK_CONV + CONVS * TAPS
HID = 1024
K_STEPS = 4
AH, NOPE, ROPE, VDIM, QR, KVR = 16, 128, 64, 128, 128, 64
APAIRS = AH // 2
E, TOPK = 8, 2
DOWN = QR + KVR + 2 * ROPE + E
MASKED = -1e30


class Buffers:
    pass


def sems(nc, ctx, *names):
    return namedtuple("Sems", names)(*[ctx.enter_context(nc.semaphore(n)) for n in names])


def wait(eng, sem, value):
    if value.__class__ is not int or value > 0:
        eng.wait_ge(sem, value)


def rsqrt_small(pool, out, x, scale, eps, minus_half, chain, base):
    pool.tensor_scalar(out, x, scale, eps, ALU.mult, ALU.add).then_inc(chain, 1)
    pool.wait_ge(chain, base + 1)
    return pool.tensor_tensor(out, out, minus_half, ALU.pow)


def shared(m, sb):
    m.ident = sb("ident", [128, 128])
    m.identb = sb("identb", [128, 128], BF16)
    m.maskb = sb("maskb", [128, 2, 128], BF16)
    m.minus_half = sb("minus_half", [128, TILES])
    m.acc = sb("acc", [128, TILES, D])
    m.mean = sb("mean", [128, TILES])
    m.rstd = sb("rstd", [128, TILES])
    m.half_bc = sb("half_bc", [128, B, D])


def mixer_buffers(m, sb):
    m.triu = sb("triu", [128, 128])
    m.ones = sb("ones", [128, 128])
    m.onehot = sb("onehot", [96, H], BF16)
    m.inv_P = sb("inv_P", [128, 2 * B])
    m.eps6 = sb("eps6", [128, 2 * B])
    m.w_dt = sb("w_dt", [128, KD, H])
    m.tab = sb("tab", [128, 4, TILES, H])
    m.cs = sb("cs", [96, TOK], BF16)
    m.ncs = sb("ncs", [96, TOK], BF16)
    m.xnT = sb("xnT", [128, KD, TOK])
    m.w = [sb(f"w{u}", [128, PACK]) for u in range(2)]
    m.wo = sb("wo", [128, 2, D])
    m.ynT = [sb(f"ynT{u}", [128, B, CH, 128]) for u in range(2)]
    conv = [sb(f"conv{u}", [128, 6, B, T]) for u in range(2)]
    m.conv = [[conv[u][:, ch, :, :] for ch in range(6)] for u in range(2)]
    flat = conv[1][:, :, :, :].rearrange("p c b t -> p (c b t)")
    m.stage_x = flat[:, 0:TILES * D].rearrange("p (t d) -> p t d", d=D)
    m.work = flat[:, TILES * D:TILES * D + 4096]
    w = flat[:, TILES * D:]
    at = 0
    m.thought_w = {}
    for name, shape in (("agg", (KD, D)), ("d1", (KD, HID)), ("d2", (HID // 128, D)), ("bc", (KD, D)), ("rows", (6, D))):
        size = shape[0] * shape[1]
        m.thought_w[name] = w[:, at:at + size].rearrange("p (a b) -> p a b", a=shape[0])
        at += size
    m.thought_w["d1b"] = w[:, at:at + HID // 128]
    m.stage_rows = flat[:, TILES * D + 4096:TILES * D + 4096 + TOK]


def norm_and_decay(nc, m, io):
    xt = m.stage_x
    with ExitStack() as ctx:
        stats = ctx.enter_context(nc.sbuf_tensor("stats", [128, TILES, 6], F32))
        mv = ctx.enter_context(nc.sbuf_tensor("mv", [128, TILES, 2], F32))
        bank = [ctx.enter_context(nc.psum_tensor(f"na{i}", [128, 512], F32)) for i in range(8)]
        s = sems(nc, ctx, "na_const", "na_const2", "na_x0", "na_x1", "na_x2", "na_x3", "na_half", "na_stats", "na_aggr", "na_eps", "na_rstd",
                 "na_xn", "na_turned", "na_even", "na_odd", "na_dtraw", "na_biased", "na_abs", "na_exp", "na_eA",
                 "na_ln", "na_relu", "na_dt", "na_da", "na_da3", "na_cs", "na_tot", "na_tot_copied", "na_csd",
                 "na_tabs", "na_rows", "na_part", "na_zero")
        m.old_sems = list(s)
        x_loaded = [s.na_x0, s.na_x1, s.na_x2, s.na_x3]
        raw, ab, relu, tot = (m.work[:, i * 512:(i + 1) * 512] for i in range(4))
        da3 = m.work[:, 2048:2048 + TILES * 96].rearrange("p (t g h) -> p t g h", g=3, h=H)
        r1 = m.stage_rows[0:96, 0:TOK]
        ex_A = m.work[:, 3600:3600 + H]
        A_row = m.work[:, 3632:3632 + H]
        dtb_row = m.work[:, 3664:3664 + H]
        block = ctx.enter_context(nc.Block())

        def tiles_of(ap, h=H):
            return ap.rearrange("p (t h) -> p t h", h=h)

        @block.sync
        def _(sp):
            for b in range(B):
                sp.dma_start(xt[:, b * CH:(b + 1) * CH, :],
                             io.x[b].rearrange("(c p) d -> p c d", p=128)).then_inc(x_loaded[b], 16)
            sp.dma_start(m.ident[:, :], io.c_ident).then_inc(s.na_const, 16)
            sp.dma_start(m.triu[:, :], io.c_triu).then_inc(s.na_const, 16)
            sp.dma_start(m.w_dt[:, :, :], io.w_dt.rearrange("(k p) h -> p k h", p=128)).then_inc(s.na_const, 16)
            sp.dma_start(A_row, io.A_log.partition_broadcast(128)).then_inc(s.na_const2, 16)
            sp.dma_start(dtb_row, io.dt_bias.partition_broadcast(128)).then_inc(s.na_const2, 16)
            sp.dma_start(m.identb[:, :], io.c_identb).then_inc(s.na_const2, 16)
            sp.dma_start(m.maskb[:, :, :], io.c_maskb).then_inc(s.na_const2, 16)
            sp.dma_start(m.onehot[:, :], io.c_onehot).then_inc(s.na_const2, 16)
            sp.wait_ge(s.na_const2, 80)

        @block.vector
        def _(dve):
            for t in range(TILES):
                dve.wait_ge(x_loaded[t // CH], 16)
                dve.bn_stats(stats[:, t, :], xt[:, t, :]).then_inc(s.na_stats, 1)
            for t in range(TILES):
                dve.wait_ge(s.na_stats, t + 1)
                dve.bn_aggr(mv[:, t, :], stats[:, t, :]).then_inc(s.na_aggr, 1)
            dve.wait_ge(s.na_rstd, 1)
            for t in range(TILES):
                dve.tensor_scalar(xt[:, t, :], xt[:, t, :], mv[:, t, 0:1], m.rstd[:, t:t + 1],
                                  ALU.subtract, ALU.mult).then_inc(s.na_xn, 1)
            dve.tensor_copy(m.mean[:, :], mv[:, :, 0]).then_inc(s.na_xn, 1)
            for g in range(0, 8, 2):
                dve.wait_ge(s.na_turned, g + 1)
                dve.tensor_copy(m.xnT[:, g % 2, g // 2 * 512:(g // 2 + 1) * 512], bank[g][:, :]).then_inc(s.na_even, 1)
            dve.wait_ge(s.na_dtraw, 1)
            dve.wait_ge(s.na_const2, 80)
            dve.tensor_tensor(tiles_of(raw), tiles_of(bank[0][:, :]),
                              dtb_row[:, None, :].to_broadcast([128, TILES, H]), ALU.add).then_inc(s.na_biased, 1)
            dve.wait_ge(s.na_biased, 1)
            dve.tensor_scalar(relu, raw, 0.0, None, ALU.max).then_inc(s.na_relu, 1)
            dve.wait_ge(s.na_relu, 1)
            dve.wait_ge(s.na_ln, 1)
            dt = m.tab[:, 0, :, :]
            dve.tensor_tensor(dt, tiles_of(relu), tiles_of(ab), ALU.add).then_inc(s.na_dt, 1)
            dve.wait_ge(s.na_dt, 1)
            dve.wait_ge(s.na_eA, 1)
            dve.scalar_tensor_tensor(tiles_of(raw), dt, -1.0,
                                     ex_A[:, None, :].to_broadcast([128, TILES, H]), ALU.mult, ALU.mult).then_inc(s.na_da, 1)
            dve.wait_ge(s.na_da, 1)
            for g in range(3):
                dve.tensor_copy(da3[:, :, g, :], tiles_of(raw)).then_inc(s.na_da3, 1)
            dve.wait_ge(s.na_tot, 1)
            dve.tensor_copy(tot, bank[2][:, :]).then_inc(s.na_tot_copied, 1)
            dve.wait_ge(s.na_tot_copied, 1)
            dve.wait_ge(s.na_tabs, 1)
            dve.tensor_tensor(relu, tot, bank[1][:, :], ALU.subtract).then_inc(s.na_csd, 1)
            n = 0
            for q in range(4):
                dve.wait_ge(s.na_rows, q + 1)
                at = slice(q * 512, (q + 1) * 512)
                rows = bank[3 + q][0:96, :]
                dve.tensor_copy(m.cs[:, at], rows).then_inc(s.na_part, 1)
                dve.wait_ge(s.na_part, n + 1)
                dve.tensor_tensor(r1[:, at], rows, m.cs[:, at], ALU.subtract).then_inc(s.na_part, 1)
                dve.wait_ge(s.na_part, n + 2)
                dve.tensor_copy(m.cs[0:64, at], r1[0:64, at]).then_inc(s.na_part, 1)
                dve.wait_ge(s.na_part, n + 3)
                dve.tensor_tensor(r1[0:32, at], r1[0:32, at], m.cs[0:32, at], ALU.subtract).then_inc(s.na_part, 1)
                dve.wait_ge(s.na_part, n + 4)
                dve.tensor_copy(m.cs[0:32, at], r1[0:32, at]).then_inc(s.na_part, 1)
                dve.wait_ge(s.na_part, n + 5)
                dve.tensor_scalar(m.ncs[:, at], m.cs[:, at], -1.0, None, ALU.mult).then_inc(s.na_part, 1)
                n += 6

        @block.gpsimd
        def _(pool):
            pool.memset(m.minus_half[:, :], -0.5).then_inc(s.na_half, 1)
            pool.memset(m.ones[:, :], 1.0).then_inc(s.na_half, 1)
            pool.memset(m.inv_P[:, :], 1.0 / P).then_inc(s.na_zero, 1)
            pool.memset(m.eps6[:, :], 1e-6).then_inc(s.na_zero, 1)
            pool.memset(m.acc[:, :, :], 0.0).then_inc(s.na_zero, 1)
            pool.wait_ge(s.na_half, 1)
            pool.wait_ge(s.na_aggr, TILES)
            rsqrt_small(pool, m.rstd[:, :], mv[:, :, 1], 1.0, 1e-5, m.minus_half[:, 0:TILES], s.na_eps, 0)\
                .then_inc(s.na_rstd, 1)

        @block.tensor
        def _(pe):
            pe.wait_ge(s.na_const, 48)
            for g in range(8):
                b, k = g // 2, g % 2
                pe.wait_ge(s.na_xn, CH * (b + 1))
                for c in range(CH):
                    mm = pe.transpose(bank[g][:, c * 128:(c + 1) * 128], xt[:, b * CH + c, k * 128:(k + 1) * 128],
                                      m.ident[:, :])
                mm.then_inc(s.na_turned, 1)
            pe.wait_ge(s.na_even, 4)
            pe.wait_ge(s.na_odd, 4)
            for t in range(TILES):
                for k in range(KD):
                    mm = pe.matmul(bank[0][:, t * H:(t + 1) * H], m.xnT[:, k, t * 128:(t + 1) * 128],
                                   m.w_dt[:, k, :], start=(k == 0), stop=(k == KD - 1))
            mm.then_inc(s.na_dtraw, 1)
            pe.wait_ge(s.na_da, 1)
            pe.wait_ge(s.na_half, 2)
            pe.matmul(bank[1][:, :], m.triu[:, :], raw, start=True, stop=True).then_inc(s.na_cs, 1)
            pe.matmul(bank[2][:, :], m.ones[:, :], raw, start=True, stop=True).then_inc(s.na_tot, 1)
            pe.wait_ge(s.na_da3, 3)
            for q in range(4):
                for c in range(4):
                    t = 4 * q + c
                    mm = pe.matmul(bank[3 + q][0:96, c * 128:(c + 1) * 128],
                                   da3[:, t, :, :].rearrange("p g h -> p (g h)"), m.triu[:, :], start=True, stop=True)
                mm.then_inc(s.na_rows, 1)

        @block.scalar
        def _(act):
            for g in range(1, 8, 2):
                act.wait_ge(s.na_turned, g + 1)
                act.activation(m.xnT[:, g % 2, g // 2 * 512:(g // 2 + 1) * 512], bank[g][:, :], ACT.Copy)\
                    .then_inc(s.na_odd, 1)
            act.wait_ge(s.na_const2, 80)
            act.activation(ex_A, A_row, ACT.Exp).then_inc(s.na_eA, 1)
            act.wait_ge(s.na_biased, 1)
            act.activation(ab, raw, ACT.Abs).then_inc(s.na_abs, 1)
            act.wait_ge(s.na_abs, 1)
            act.activation(ab, ab, ACT.Exp, scale=-1.0).then_inc(s.na_exp, 1)
            act.wait_ge(s.na_exp, 1)
            act.activation(ab, ab, ACT.Ln, bias=1.0).then_inc(s.na_ln, 1)
            act.wait_ge(s.na_cs, 1)
            act.activation(m.tab[:, 1, :, :], tiles_of(bank[1][:, :]), ACT.Exp).then_inc(s.na_tabs, 1)
            act.wait_ge(s.na_csd, 1)
            act.activation(m.tab[:, 2, :, :], tiles_of(relu), ACT.Exp).then_inc(s.na_tabs, 1)
            act.activation(m.tab[:, 3, :, :], tiles_of(tot), ACT.Exp).then_inc(s.na_tabs, 1)


BX, BZ, BB0, BC0, BB1, BC1 = range(6)
PIECES = [(ch, half) for ch in (BB0, BC0, BB1, BC1, BX, BZ) for half in range(2)]
NP = len(PIECES)
NC = 2 * CONVS
CONV_OF = {BX: 0, BB0: 1, BC0: 2, BB1: 3, BC1: 4}
PER_STEP = NP // CH
OUTS = CH
PER_TRIP = 2 * NP + OUTS


def mixer(nc, m, io):
    with ExitStack() as ctx:
        def sb(name, shape, dt=F32):
            return ctx.enter_context(nc.sbuf_tensor(name, shape, dt))

        L = [sb(f"L{h}", [128, B, 128]) for h in range(2)]
        BT = [sb(f"BT{h}", [128, B, 128]) for h in range(2)]
        dtx, dtx2, y, sq, tmp, S, Sdl = (sb(n, [128, B, 2, P]) for n in ("dtx", "dtx2", "y", "sq", "tmp", "S", "Sdl"))
        ss = sb("ss", [128, B, 2])
        rs = sb("rs", [128, B, 2])
        tabp = [sb(f"tabp{u}", [128, 4, TILES, 2]) for u in range(2)]
        hot = [sb(f"hot{u}", [96, 2, 128], BF16) for u in range(2)]
        piece = [ctx.enter_context(nc.psum_tensor(f"piece{i}", [128, 2, 512], F32)) for i in range(2)]
        bank = [ctx.enter_context(nc.psum_tensor(f"scan{i}", [128, 512], F32)) for i in range(4)]
        s = sems(nc, ctx, "w_loaded0", "w_loaded1", "wo_loaded", "piece_ready", "piece_read0", "piece_read1", "tap_done", "conv_chain",
                 "piece_final", "pair_tabs", "diff_ready", "exp_done", "scores_ready", "masked_done", "xT_ready",
                 "dtx_done", "dtx2_done", "BT_ready", "BT_done", "intra_ready", "inter_ready", "inter_read",
                 "y_done", "sadd_ready", "sdl_done", "S_done", "sq_done", "ss_done", "eps_done", "rs_done",
                 "ysc_done", "yT_ready", "yn_done", "out_added")
        w_loaded = [s.w_loaded0, s.w_loaded1]
        piece_read = [s.piece_read0, s.piece_read1]
        block = ctx.enter_context(nc.Block())
        LAST = PAIRS // 2 - 1

        def w_of(u, k, ch):
            return m.w[u][:, k * CHANNELS + ch * 128:k * CHANNELS + (ch + 1) * 128]

        def tap_w(u, ch, k):
            at = PACK_CONV + CONV_OF[ch] * TAPS + k
            return m.w[u][:, at:at + 1]

        def row4(ap):
            return ap.rearrange("p b h d -> p (b h) d")

        def tab_of(u, kind, c):
            return tabp[u][:, kind, c::CH, :]

        def spread(ap):
            return ap[:, :, :, None].to_broadcast([128, B, 2, P])

        def first_piece(it):
            return NP + it * PER_TRIP

        def pieces_of_step(u, c, more):
            per = PER_STEP if more else 0
            outs = max(c - 1, 0) if u else 0
            at = (NP if u else 0) + per * c + outs
            return [(at + i, c * PER_STEP + i) for i in range(per)], (at + per if u and c > 0 else None)

        def tail_piece(more):
            return NP + (NP + OUTS - 1 if more else OUTS - 1)

        @block.tensor
        def _(pe):
            def proj(u, n, i, slot, first=False):
                ch, half = PIECES[i]
                if not first:
                    wait(pe, piece_read[slot], n)
                for b in range(2):
                    for k in range(KD):
                        at = (2 * half + b) * T
                        mm = pe.matmul(piece[slot][:, b, :], w_of(u, k, ch), m.xnT[:, k, at:at + T],
                                       start=(k == 0), stop=(k == KD - 1))
                mm.then_inc(s.piece_ready, 1)

            def out_piece(it, n, c, slot):
                wait(pe, piece_read[slot], n)
                wait(pe, s.yn_done, (2 * it + 1) * CH + c + 1)
                wait(pe, s.wo_loaded, 16 * (it + 1))
                for b in range(B):
                    for u in range(2):
                        mm = pe.matmul(piece[slot][:, b // 2, b % 2 * D:(b % 2 + 1) * D], m.ynT[u][:, b, c, :],
                                       m.wo[:, u, :], start=(u == 0), stop=(u == 1))
                mm.then_inc(s.piece_ready, 1)

            def uses(it, n):
                return (NP + n) // 2 + it * (PER_TRIP // 2)

            def turn_y(p, u, c):
                wait(pe, s.ysc_done, p * CH + c + 1)
                for b in range(B):
                    mm = pe.transpose(bank[3][:, b * 128:(b + 1) * 128],
                                      y[:, b, :, :].rearrange("p h d -> p (h d)"), m.ident[:, :])
                mm.then_inc(s.yT_ready, 1)

            def step(it, p, u, c, more):
                buf = m.conv[u]
                todo, out = pieces_of_step(u, c, more)
                if c == 0:
                    wait(pe, s.pair_tabs, 2 * (p + 1))
                for h in range(2):
                    if h == 0:
                        wait(pe, s.y_done, p * CH + c)
                    elif c == 1:
                        wait(pe, s.BT_done, p * 2 * (CH - 1) + 1)
                    else:
                        wait(pe, s.inter_read, p * (CH - 1) + max(c - 1, 0))
                    for b in range(B):
                        q = slice(b * T + c * 128, b * T + (c + 1) * 128)
                        o = bank[h][:, b * 128:(b + 1) * 128]
                        pe.matmul(o, m.ncs[:, q], hot[u][:, h, :], start=True, stop=False)
                        pe.matmul(o, hot[u][:, h, :], m.cs[:, q], start=False, stop=False)
                        mm = pe.matmul(o, m.identb[:, :], m.maskb[:, 0, :], start=False, stop=True)
                    mm.then_inc(s.diff_ready, 1)
                for h in range(2):
                    if c == 0:
                        wait(pe, s.piece_final, p * NC + 4 * (h + 1))
                    if h == 0:
                        wait(pe, s.S_done, p * (CH - 1) + c)
                    else:
                        wait(pe, s.yn_done, p * CH + max(c - 1, 0))
                        if c == 1:
                            wait(pe, s.masked_done, (p * CH + c) * 2)
                    for b in range(B):
                        q = slice(c * 128, (c + 1) * 128)
                        mm = pe.matmul(bank[2 + h][:, b * 128:(b + 1) * 128], buf[BB0 + 2 * h][:, b, q],
                                       buf[BC0 + 2 * h][:, b, q], start=True, stop=True)
                    mm.then_inc(s.scores_ready, 1)
                for n, i in todo[0:1]:
                    proj(1 - u, uses(it, n), i, n % 2)
                if c == 0:
                    wait(pe, s.piece_final, p * NC + 10)
                wait(pe, s.exp_done, (p * CH + c) * 2 + 1)
                for b in range(B):
                    mm = pe.transpose(bank[0][:, b * 128:(b + 1) * 128], buf[BX][:, b, c * 128:(c + 1) * 128], m.ident[:, :])
                mm.then_inc(s.xT_ready, 1)
                if c < CH - 1:
                    for h in range(2):
                        if h == 0:
                            wait(pe, s.exp_done, (p * CH + c) * 2 + 2)
                        else:
                            wait(pe, s.masked_done, (p * CH + c) * 2 + 1)
                        for b in range(B):
                            mm = pe.transpose(bank[1 + h][:, b * 128:(b + 1) * 128],
                                              buf[BB0 + 2 * h][:, b, c * 128:(c + 1) * 128], m.ident[:, :])
                        mm.then_inc(s.BT_ready, 1)
                if c > 0:
                    wait(pe, s.masked_done, (p * CH + c) * 2 + 2)
                    turn_y(p, u, c - 1)
                for n, i in todo[1:2]:
                    proj(1 - u, uses(it, n), i, n % 2)
                wait(pe, s.masked_done, (p * CH + c) * 2 + 2)
                wait(pe, s.dtx_done, p * CH + c + 1)
                for b in range(B):
                    for h in range(2):
                        at = (b * 2 + h) * P
                        mm = pe.matmul(bank[0][:, at:at + P], L[h][:, b, :], dtx[:, b, h, :], start=True, stop=True)
                mm.then_inc(s.intra_ready, 1)
                if c > 0:
                    wait(pe, s.S_done, p * (CH - 1) + c)
                    if c < CH - 1:
                        wait(pe, s.BT_done, (p * (CH - 1) + c) * 2 + 1)
                    else:
                        wait(pe, s.exp_done, (p * CH + c) * 2 + 2)
                    for b in range(B):
                        for h in range(2):
                            at = (b * 2 + h) * P
                            mm = pe.matmul(bank[1][:, at:at + P], buf[BC0 + 2 * h][:, b, c * 128:(c + 1) * 128],
                                           S[:, b, h, :], start=True, stop=True)
                    mm.then_inc(s.inter_ready, 1)
                if c < CH - 1:
                    wait(pe, s.BT_done, (p * (CH - 1) + c) * 2 + 2)
                    wait(pe, s.dtx2_done, p * (CH - 1) + c + 1)
                    for b in range(B):
                        for h in range(2):
                            at = (b * 2 + h) * P
                            mm = pe.matmul(bank[2][:, at:at + P], BT[h][:, b, :], dtx2[:, b, h, :], start=True, stop=True)
                    mm.then_inc(s.sadd_ready, 1)
                for n, i in todo[2:]:
                    proj(1 - u, uses(it, n), i, n % 2)
                if out is not None:
                    out_piece(it, uses(it, out), c - 1, out % 2)

            def trip(it, last=False):
                for u in range(2):
                    p = 2 * it + u
                    more = not (last and u)
                    if more:
                        wait(pe, w_loaded[1 - u], 16 * (it + 1 + u))
                    for c in range(CH):
                        step(it, p, u, c, more)
                    turn_y(p, u, CH - 1)
                    if u:
                        n = tail_piece(more)
                        out_piece(it, uses(it, n), CH - 1, n % 2)

            wait(pe, w_loaded[0], 16)
            for i in range(NP):
                proj(0, i // 2, i, i % 2, first=i < 2)
            trip(0)
            with pe.Fori(1, LAST) as it:
                trip(it)
            trip(LAST, last=True)

        @block.scalar
        def _(act):
            def tap(u, n, i, slot):
                ch, half = PIECES[i]
                if ch == BZ:
                    return
                wait(act, s.piece_ready, n + 1)
                act.activation(m.conv[u][ch][:, 2 * half:2 * half + 2, :], piece[slot][:, :, :], ACT.Copy,
                               scale=tap_w(u, ch, TAPS - 1)).then_inc(s.tap_done, 1)

            def fin(u, n, i, slot, uses):
                ch, half = PIECES[i]
                dst = m.conv[u][ch][:, 2 * half:2 * half + 2, :]
                if ch == BZ:
                    wait(act, s.piece_ready, n + 1)
                    act.activation(dst, piece[slot][:, :, :], ACT.Silu).then_inc(piece_read[slot], 1)
                else:
                    wait(act, piece_read[slot], uses + 1)
                    act.activation(dst, dst, ACT.Silu).then_inc(s.piece_final, 1)

            def step(it, p, u, c, more):
                todo, _ = pieces_of_step(u, c, more)
                for h in range(2):
                    wait(act, s.diff_ready, (p * CH + c) * 2 + h + 1)
                    act.activation(L[h][:, :, :].rearrange("p b q -> p (b q)"), bank[h][:, :], ACT.Exp).then_inc(s.exp_done, 1)

                def args(k):
                    n, i = todo[k]
                    return first_piece(it) + n, i, n % 2, (NP + n) // 2 + it * (PER_TRIP // 2)

                if more:
                    n, i, slot, uses = args(0)
                    tap(1 - u, n, i, slot)
                if c < CH - 1:
                    for h in range(2):
                        wait(act, s.BT_ready, (p * (CH - 1) + c) * 2 + h + 1)
                        act.activation(BT[h][:, :, :].rearrange("p b q -> p (b q)"), bank[1 + h][:, :], ACT.Copy)\
                            .then_inc(s.BT_done, 1)
                for k in (1, 2):
                    if more:
                        n, i, slot, uses = args(k)
                        tap(1 - u, n, i, slot)
                        n, i, slot, uses = args(k - 1)
                        fin(1 - u, n, i, slot, uses)
                wait(act, s.y_done, p * CH + c + 1)
                act.activation(sq[:, :, :, :], y[:, :, :, :], ACT.Square).then_inc(s.sq_done, 1)
                if more:
                    n, i, slot, uses = args(2)
                    fin(1 - u, n, i, slot, uses)

            def trip(it, last=False):
                for u in range(2):
                    for c in range(CH):
                        step(it, 2 * it + u, u, c, not (last and u))

            wait(act, w_loaded[0], 16)
            for i in range(NP + 1):
                if i < NP:
                    tap(0, i, i, i % 2)
                if i > 0:
                    fin(0, i - 1, i - 1, (i - 1) % 2, (i - 1) // 2)
            trip(0)
            with act.Fori(1, LAST) as it:
                trip(it)
            trip(LAST, last=True)

        @block.vector
        def _(dve):
            def conv(u, i, slot, j):
                ch, half = PIECES[i]
                if ch == BZ:
                    return
                wait(dve, s.tap_done, j + 1)
                for k in range(1, TAPS):
                    dst = m.conv[u][ch][:, 2 * half:2 * half + 2, k:T]
                    if k > 1:
                        wait(dve, s.conv_chain, 2 * j + k - 1)
                    dve.scalar_tensor_tensor(dst, piece[slot][:, :, 0:T - k], tap_w(u, ch, TAPS - 1 - k), dst,
                                             ALU.mult, ALU.add)\
                        .then_inc(s.conv_chain if k < TAPS - 1 else piece_read[slot], 1)

            def add_out(n, c, slot):
                wait(dve, s.piece_ready, n + 1)
                for b2 in range(2):
                    a = m.acc[:, (2 * b2) * CH + c:(2 * b2 + 1) * CH + c + 1:CH, :]
                    i = dve.tensor_tensor(a, a, piece[slot][:, b2, :].rearrange("p (b d) -> p b d", b=2), ALU.add)
                i.then_inc(piece_read[slot], 1)

            def norm_y(p, u, c):
                wait(dve, s.yT_ready, p * CH + c + 1)
                dve.tensor_tensor(m.ynT[u][:, :, c, :], bank[3][:, :].rearrange("p (b q) -> p b q", b=B),
                                  m.conv[u][BZ][:, :, c * 128:(c + 1) * 128], ALU.mult).then_inc(s.yn_done, 1)

            def step(it, p, u, c, more):
                todo, out = pieces_of_step(u, c, more)
                bk = [b[:, :].rearrange("p (b h d) -> p b h d", h=2, d=P) for b in bank]
                for h in range(2):
                    wait(dve, s.exp_done, (p * CH + c) * 2 + h + 1)
                    wait(dve, s.scores_ready, (p * CH + c) * 2 + h + 1)
                    flat = L[h][:, :, :].rearrange("p b q -> p (b q)")
                    dve.tensor_tensor(flat, bank[2 + h][:, :], flat, ALU.mult).then_inc(s.masked_done, 1)
                for n, i in todo[0:1]:
                    conv(1 - u, i, n % 2, (p + 1) * NC + i)
                wait(dve, s.xT_ready, p * CH + c + 1)
                if c == 0:
                    wait(dve, s.pair_tabs, 2 * (p + 1))
                wait(dve, s.dtx2_done, p * (CH - 1) + c)
                dve.tensor_tensor(dtx[:, :, :, :], bk[0], spread(tab_of(u, 0, c)), ALU.mult).then_inc(s.dtx_done, 1)
                if c > 0:
                    norm_y(p, u, c - 1)
                for n, i in todo[1:2]:
                    conv(1 - u, i, n % 2, (p + 1) * NC + i)
                if c > 0:
                    wait(dve, s.inter_ready, p * (CH - 1) + c)
                    dve.tensor_tensor(tmp[:, :, :, :], bk[1], spread(tab_of(u, 1, c)), ALU.mult).then_inc(s.inter_read, 1)
                    wait(dve, s.intra_ready, p * CH + c + 1)
                    wait(dve, s.inter_read, p * (CH - 1) + c)
                    dve.tensor_tensor(row4(y[:, :, :, :]), row4(bk[0]), row4(tmp[:, :, :, :]), ALU.add).then_inc(s.y_done, 1)
                else:
                    wait(dve, s.intra_ready, p * CH + c + 1)
                    dve.tensor_copy(row4(y[:, :, :, :]), row4(bk[0])).then_inc(s.y_done, 1)
                if c < CH - 1:
                    wait(dve, s.sadd_ready, p * (CH - 1) + c + 1)
                    if c > 0:
                        wait(dve, s.sdl_done, p * (CH - 2) + c)
                        dve.tensor_tensor(row4(S[:, :, :, :]), row4(bk[2]), row4(Sdl[:, :, :, :]), ALU.add).then_inc(s.S_done, 1)
                    else:
                        dve.tensor_copy(row4(S[:, :, :, :]), row4(bk[2])).then_inc(s.S_done, 1)
                for n, i in todo[2:3]:
                    conv(1 - u, i, n % 2, (p + 1) * NC + i)
                wait(dve, s.sq_done, p * CH + c + 1)
                dve.tensor_reduce(ss[:, :, :], sq[:, :, :, :], AX, ALU.add).then_inc(s.ss_done, 1)
                if out is not None:
                    add_out(first_piece(it) + out, c - 1, out % 2)

            def trip(it, last=False):
                for u in range(2):
                    p = 2 * it + u
                    more = not (last and u)
                    for c in range(CH):
                        step(it, p, u, c, more)
                    norm_y(p, u, CH - 1)
                    if u:
                        n = tail_piece(more)
                        add_out(first_piece(it) + n, CH - 1, n % 2)

            wait(dve, w_loaded[0], 16)
            for i in range(NP):
                conv(0, i, i % 2, i)
            trip(0)
            with dve.Fori(1, LAST) as it:
                trip(it)
            trip(LAST, last=True)

        @block.gpsimd
        def _(pool):
            def tabs(p, u, head):
                pool.tensor_copy(tabp[u][:, :, :, :].rearrange("p k t h -> p (k t) h"),
                                 m.tab[:, :, :, bass.ds(head, 2)].rearrange("p k t h -> p (k t) h")).then_inc(s.pair_tabs, 1)
                pool.tensor_copy(hot[u][:, :, :], m.onehot[:, bass.ds(head, 2)][:, :, None].to_broadcast([96, 2, 128]))\
                    .then_inc(s.pair_tabs, 1)

            def step(p, u, c):
                if c < CH - 1:
                    wait(pool, s.dtx_done, p * CH + c + 1)
                    pool.tensor_tensor(dtx2[:, :, :, :], dtx[:, :, :, :], spread(tab_of(u, 2, c)), ALU.mult)\
                        .then_inc(s.dtx2_done, 1)
                if 0 < c < CH - 1:
                    wait(pool, s.S_done, p * (CH - 1) + c)
                    pool.tensor_tensor(Sdl[:, :, :, :], S[:, :, :, :], spread(tab_of(u, 3, c)), ALU.mult)\
                        .then_inc(s.sdl_done, 1)
                e = (p * CH + c) * 2
                wait(pool, s.ss_done, p * CH + c + 1)
                pool.tensor_tensor(rs[:, :, :], ss[:, :, :], m.inv_P[:, :].rearrange("p (b h) -> p b h", b=B), ALU.mult).then_inc(s.eps_done, 1)
                wait(pool, s.eps_done, e + 1)
                pool.tensor_tensor(rs[:, :, :], rs[:, :, :], m.eps6[:, :].rearrange("p (b h) -> p b h", b=B), ALU.add).then_inc(s.eps_done, 1)
                wait(pool, s.eps_done, e + 2)
                pool.tensor_tensor(rs[:, :, :], rs[:, :, :], m.minus_half[:, 0:8].rearrange("p (b h) -> p b h", b=B), ALU.pow).then_inc(s.rs_done, 1)
                wait(pool, s.rs_done, p * CH + c + 1)
                pool.tensor_tensor(y[:, :, :, :], y[:, :, :, :], spread(rs[:, :, :]), ALU.mult).then_inc(s.ysc_done, 1)

            def trip(it, last=False):
                for u in range(2):
                    p = 2 * it + u
                    for c in range(CH):
                        step(p, u, c)
                        if c == 1 and not (last and u):
                            tabs(p + 1, 1 - u, 4 * it + 2 * (u + 1))

            for old in m.old_sems:
                pool.sem_clear(old)
            tabs(0, 0, 0)
            trip(0)
            with pool.Fori(1, LAST) as it:
                trip(it)
            trip(LAST, last=True)

        @block.sync
        def _(sp):
            def load_out(p):
                sp.dma_start(m.wo[:, :, :], io.w_out[p:p + 2].rearrange("u p n -> p u n")).then_inc(s.wo_loaded, 16)

            for u in range(2):
                sp.dma_start(m.w[u][:, :], io.w_pack[u]).then_inc(w_loaded[u], 16)
            load_out(0)
            for it in range(LAST):
                for u in range(2):
                    sp.wait_ge(s.piece_ready, it * PER_TRIP + NP * (u + 1))
                    sp.wait_ge(s.piece_final, (2 * it + u + 1) * NC)
                    sp.dma_start(m.w[u][:, :], io.w_pack[2 * it + 2 + u]).then_inc(w_loaded[u], 16)
                sp.wait_ge(s.piece_ready, first_piece(it + 1))
                load_out(2 * it + 2)
            for u in range(2):
                sp.wait_ge(w_loaded[u], 16 * (LAST + 1))


def thought(nc, m, io):
    w = m.thought_w
    agg, d1, d2, bcw = w["agg"], w["d1"], w["d2"], w["bc"]
    rows, d1b = w["rows"], w["d1b"]
    HT = HID // 128
    with ExitStack() as ctx:
        def sb(name, shape):
            return ctx.enter_context(nc.sbuf_tensor(name, shape, F32))

        x4, normed, state = (sb(f"th_{n}", [4, D]) for n in ("x4", "normed", "state"))
        stats, mv, rstd = sb("th_st", [4, 6]), sb("th_mv", [4, 2]), sb("th_rs", [4, 1])
        xT, hT = sb("th_xT", [128, KD, B]), sb("th_hT", [128, HT, B])
        spreadT = sb("th_spreadT", [128, KD, B, 128])
        bcb = sb("th_bcb", [128, D])
        ps_row, ps_T, ps_h = (ctx.enter_context(nc.psum_tensor(f"th_{n}", [128, 512], F32)) for n in ("row", "T", "h"))
        ps_bc = ctx.enter_context(nc.psum_tensor("th_bc", [128, B, D], F32))
        s = sems(nc, ctx, "th_loaded", "th_row_ready", "th_state", "th_stats", "th_aggr", "th_eps", "th_rstd", "th_hat",
                 "th_scaled", "th_normed", "th_turned", "th_T", "th_h_ready", "th_h_biased", "th_gelu", "th_added",
                 "th_spread", "th_bc_ready", "th_bc_sum", "th_bc_done")
        block = ctx.enter_context(nc.Block())
        LNS = K_STEPS + 1
        LOADS = 12

        @block.sync
        def _(sp):
            for i, v in enumerate((io.in_gamma, io.in_beta, io.agg_b, io.pn_gamma, io.pn_beta, io.d2_b)):
                sp.dma_start(rows[0:B, i, :], v.partition_broadcast(B)).then_inc(s.th_loaded, 16)
            sp.dma_start(agg, io.agg_w.rearrange("(k p) n -> p k n", p=128)).then_inc(s.th_loaded, 16)
            sp.dma_start(d1, io.d1_w.rearrange("(k p) n -> p k n", p=128)).then_inc(s.th_loaded, 16)
            sp.dma_start(d2, io.d2_w.rearrange("(k p) n -> p k n", p=128)).then_inc(s.th_loaded, 16)
            sp.dma_start(bcw, io.bc_w.rearrange("(k p) n -> p k n", p=128)).then_inc(s.th_loaded, 16)
            sp.dma_start(d1b, io.d1_b).then_inc(s.th_loaded, 16)
            sp.dma_start(bcb[:, :], io.bc_b.partition_broadcast(128)).then_inc(s.th_loaded, 16)

        @block.tensor
        def _(pe):
            def turn(n, src):
                for k in range(KD):
                    mm = pe.transpose(ps_T[:, k * B:(k + 1) * B], src[:, k * 128:(k + 1) * 128], m.ident[0:B, 0:B])
                mm.then_inc(s.th_turned, 1)

            for k in range(KD):
                mm = pe.matmul(ps_row[0:B, k * 128:(k + 1) * 128], m.xnT[:, k, T - 1::T], m.ident[:, :], start=True, stop=True)
            mm.then_inc(s.th_row_ready, 1)
            pe.wait_ge(s.th_loaded, 16 * LOADS)
            for n in range(LNS):
                pe.wait_ge(s.th_normed, n + 1)
                turn(n, normed)
                pe.wait_ge(s.th_T, n + 1)
                if n == 0:
                    for k in range(KD):
                        mm = pe.matmul(ps_row[0:B, 0:D], xT[:, k, :], agg[:, k, :], start=(k == 0), stop=(k == KD - 1))
                    mm.then_inc(s.th_row_ready, 1)
                    continue
                for j in range(HT):
                    for k in range(KD):
                        mm = pe.matmul(ps_h[:, j * B:(j + 1) * B], d1[:, k, j * 128:(j + 1) * 128], xT[:, k, :],
                                       start=(k == 0), stop=(k == KD - 1))
                mm.then_inc(s.th_h_ready, 1)
                pe.wait_ge(s.th_gelu, n)
                for j in range(HT):
                    mm = pe.matmul(ps_row[0:B, 0:D], hT[:, j, :], d2[:, j, :], start=(j == 0), stop=(j == HT - 1))
                mm.then_inc(s.th_row_ready, 1)
            pe.wait_ge(s.th_state, LNS)
            turn(LNS, state)
            pe.wait_ge(s.th_spread, KD)
            for b in range(B):
                for k in range(KD):
                    mm = pe.matmul(ps_bc[:, b, :], spreadT[:, k, b, :], bcw[:, k, :], start=(k == 0), stop=(k == KD - 1))
            mm.then_inc(s.th_bc_ready, 1)

        @block.vector
        def _(dve):
            def layer_norm(n, src, gamma, beta):
                dve.bn_stats(stats[:, :], src[:, :]).then_inc(s.th_stats, 1)
                dve.wait_ge(s.th_stats, n + 1)
                dve.bn_aggr(mv[:, :], stats[:, :]).then_inc(s.th_aggr, 1)
                dve.wait_ge(s.th_rstd, n + 1)
                dve.tensor_scalar(normed[:, :], src[:, :], mv[:, 0:1], rstd[:, 0:1], ALU.subtract, ALU.mult).then_inc(s.th_hat, 1)
                dve.wait_ge(s.th_hat, n + 1)
                dve.tensor_tensor(normed[:, :], normed[:, :], rows[0:B, gamma, :], ALU.mult).then_inc(s.th_scaled, 1)
                dve.wait_ge(s.th_scaled, n + 1)
                dve.tensor_tensor(normed[:, :], normed[:, :], rows[0:B, beta, :], ALU.add).then_inc(s.th_normed, 1)

            dve.wait_ge(s.th_loaded, 16 * LOADS)
            dve.wait_ge(s.th_row_ready, 1)
            dve.tensor_copy(x4[:, :], ps_row[0:B, 0:D]).then_inc(s.th_added, 1)
            dve.wait_ge(s.th_added, 1)
            for n in range(LNS):
                layer_norm(n, x4 if n == 0 else state, 0 if n == 0 else 3, 1 if n == 0 else 4)
                dve.wait_ge(s.th_turned, n + 1)
                dve.tensor_copy(xT[:, :, :].rearrange("p k b -> p (k b)"), ps_T[:, 0:KD * B]).then_inc(s.th_T, 1)
                if n == 0:
                    dve.wait_ge(s.th_row_ready, 2)
                    dve.tensor_tensor(state[:, :], ps_row[0:B, 0:D], rows[0:B, 2, :], ALU.add).then_inc(s.th_state, 1)
                    dve.wait_ge(s.th_state, 1)
                    continue
                dve.wait_ge(s.th_h_ready, n)
                dve.tensor_tensor(hT[:, :, :], ps_h[:, 0:HT * B].rearrange("p (j b) -> p j b", b=B),
                                  d1b[:, :, None].to_broadcast([128, HT, B]), ALU.add).then_inc(s.th_h_biased, 1)
                dve.wait_ge(s.th_row_ready, n + 2)
                dve.tensor_tensor(state[:, :], ps_row[0:B, 0:D], state[:, :], ALU.add).then_inc(s.th_added, 1)
                dve.wait_ge(s.th_added, n + 1)
                dve.tensor_tensor(state[:, :], state[:, :], rows[0:B, 5, :], ALU.add).then_inc(s.th_state, 1)
                dve.wait_ge(s.th_state, n + 1)
            dve.wait_ge(s.th_turned, LNS + 1)
            for k in range(KD):
                dve.tensor_copy(spreadT[:, k, :, :], ps_T[:, k * B:(k + 1) * B][:, :, None].to_broadcast([128, B, 128]))\
                    .then_inc(s.th_spread, 1)
            dve.wait_ge(s.th_bc_ready, 1)
            for b in range(B):
                dve.tensor_tensor(m.half_bc[:, b, :], ps_bc[:, b, :], bcb[:, :], ALU.add).then_inc(s.th_bc_sum, 1)
            dve.wait_ge(s.th_bc_sum, B)
            dve.tensor_scalar(m.half_bc[:, :, :], m.half_bc[:, :, :], 0.5, None, ALU.mult).then_inc(s.th_bc_done, 1)

        @block.gpsimd
        def _(pool):
            for n in range(LNS):
                pool.wait_ge(s.th_aggr, n + 1)
                rsqrt_small(pool, rstd[:, :], mv[:, 1:2], 1.0, 1e-6, m.minus_half[0:B, 0:1], s.th_eps, n).then_inc(s.th_rstd, 1)

        @block.scalar
        def _(act):
            for n in range(1, LNS):
                act.wait_ge(s.th_h_biased, n)
                act.activation(hT[:, :, :], hT[:, :, :], ACT.Gelu).then_inc(s.th_gelu, 1)


def middle(nc, m, io):
    with ExitStack() as ctx:
        def sb(name, shape, dt=F32):
            return ctx.enter_context(nc.sbuf_tensor(name, shape, dt))

        x = sb("mi_x", [128, TILES, D])
        gate_w, gate_b = sb("mi_gw", [128, KD, D]), sb("mi_gb", [128, D])
        out_g, out_b = sb("mi_og", [128, D]), sb("mi_ob", [128, D])
        down_w = sb("mi_dw", [128, KD, DOWN])
        ew = sb("mi_ew", [128, E, KD, D])
        eb = sb("mi_eb", [E, D])
        norm_w = sb("mi_nw", [128, QR + KVR])
        kcos, ksin = sb("mi_cos", [128, CH, ROPE]), sb("mi_sin", [128, CH, ROPE])
        before = sb("mi_before", [128, E, E])
        inv = sb("mi_inv", [128, 2])
        eps = sb("mi_eps", [128, 2])
        xn0, out, hat, xn1 = (sb(f"mi_{n}", [128, D]) for n in ("xn0", "out", "hat", "xn1"))
        th, sg = sb("mi_th", [128, D]), sb("mi_sg", [128, D])
        x1, idle = sb("mi_x1", [128, D]), sb("mi_idle", [128, 1])
        T0, T1 = sb("mi_T0", [128, KD, 128]), sb("mi_T1", [128, KD, 128])
        st, mv, rs = sb("mi_st", [128, 6]), sb("mi_mv", [128, 2]), sb("mi_rs", [128, 1])
        st1, mv1, rs1 = sb("mi_st1", [128, 6]), sb("mi_mv1", [128, 2]), sb("mi_rs1", [128, 1])
        dn, sqd, ssd, rsd = sb("mi_dn", [128, DOWN]), sb("mi_sqd", [128, QR]), sb("mi_ssd", [128, 2]), sb("mi_rsd", [128, 2])
        gt, eq = sb("mi_gt", [128, E, E]), sb("mi_eq", [128, E, E])
        rank, sel, sl, hsum, garg, gates = (sb(f"mi_{n}", [128, E]) for n in ("rank", "sel", "sl", "hsum", "garg", "gates"))
        qn, kcat = sb("mi_qn", [128, QR]), sb("mi_kcat", [128, KVR + ROPE])
        kr = sb("mi_kr", [128, ROPE])
        gT = sb("mi_gT", [E, 128])
        moe = sb("mi_moe", [128, D])
        pT, pG, pD, pK = (ctx.enter_context(nc.psum_tensor(f"mi_p{n}", [128, 512], F32)) for n in "TGDK")
        pE = [ctx.enter_context(nc.psum_tensor(f"mi_e{i}", [128, 2, D], F32)) for i in range(4)]
        s = sems(nc, ctx, "mi_loaded", "mi_consts", "mi_xn0", "mi_turned0", "mi_T0", "mi_gate_ready", "mi_gate_biased",
                 "mi_tanh", "mi_gated", "mi_out", "mi_stats", "mi_aggr", "mi_eps", "mi_rstd", "mi_hat", "mi_hat2",
                 "mi_hat3", "mi_silu", "mi_sg", "mi_x1", "mi_stats1", "mi_aggr1", "mi_eps1", "mi_rstd1", "mi_xn1",
                 "mi_turned1", "mi_T1", "mi_down_ready", "mi_dn", "mi_ssd", "mi_rsd_chain", "mi_rsd", "mi_route",
                 "mi_route_arg", "mi_route_tanh", "mi_gates", "mi_kv_done", "mi_qn", "mi_rope", "mi_kcat",
                 "mi_qk_turned", "mi_qk_done", "mi_gates_turned", "mi_gT", "mi_bias_ready", "mi_experts_ready",
                 "mi_expert_added", "mi_moe", "mi_route_arg2", "mi_const")
        block = ctx.enter_context(nc.Block())
        NCONST = 3
        LOADS = 14

        def order(stage_a, stage_b, t, has_next, nxt):
            if has_next:
                stage_a(nxt, 1)
            stage_b(t, 1)
            if has_next:
                stage_a(nxt, 2)
            stage_b(t, 2)
            if has_next:
                stage_a(nxt, 3)
            stage_b(t, 3)
            if has_next:
                stage_a(nxt, 4)

        def run(eng, stage_a, stage_b):
            for n in range(1, 5):
                stage_a((0, 0), n)
            for c in range(CH):
                order(stage_a, stage_b, (0, c), True, (0, c + 1))
            with eng.Fori(1, B - 1) as b:
                for c in range(CH):
                    order(stage_a, stage_b, (b, c), True, (b, c + 1))
            for c in range(CH):
                order(stage_a, stage_b, (B - 1, c), c < CH - 1, (B - 1, c + 1))

        def num(t):
            return t[0] * CH + t[1]

        @block.sync
        def _(sp):
            for b in range(B):
                sp.dma_start(x[:, b * CH:(b + 1) * CH, :], io.x[b].rearrange("(c p) d -> p c d", p=128)).then_inc(s.mi_loaded, 16)
            sp.dma_start(gate_w[:, :, :], io.gate_w.rearrange("(k p) n -> p k n", p=128)).then_inc(s.mi_loaded, 16)
            sp.dma_start(gate_b[:, :], io.gate_b.partition_broadcast(128)).then_inc(s.mi_loaded, 16)
            sp.dma_start(out_g[:, :], io.out_gamma.partition_broadcast(128)).then_inc(s.mi_loaded, 16)
            sp.dma_start(out_b[:, :], io.out_beta.partition_broadcast(128)).then_inc(s.mi_loaded, 16)
            sp.dma_start(down_w[:, :, :], io.w_down.rearrange("(k p) n -> p k n", p=128)).then_inc(s.mi_loaded, 16)
            sp.dma_start(norm_w[:, 0:QR], io.q_norm_w.partition_broadcast(128)).then_inc(s.mi_loaded, 16)
            sp.dma_start(norm_w[:, QR:], io.kv_norm_w.partition_broadcast(128)).then_inc(s.mi_loaded, 16)
            sp.dma_start(kcos[:, :, :], io.c_kcos).then_inc(s.mi_loaded, 16)
            sp.dma_start(ksin[:, :, :], io.c_ksin).then_inc(s.mi_loaded, 16)
            sp.dma_start(before[:, :, :], io.c_before).then_inc(s.mi_loaded, 16)
            sp.dma_start(ew[:, :, :, :], io.expert_w.rearrange("e (k p) n -> p e k n", p=128)).then_inc(s.mi_consts, 16)
            sp.dma_start(eb[:, :], io.expert_b).then_inc(s.mi_consts, 16)

        @block.tensor
        def _(pe):
            def a(t, n):
                i = num(t)
                if n == 2:
                    wait(pe, s.mi_xn0, i + 1)
                    for k in range(KD):
                        mm = pe.transpose(pT[:, k * 128:(k + 1) * 128], xn0[:, k * 128:(k + 1) * 128], m.ident[:, :])
                    mm.then_inc(s.mi_turned0, 1)
                    wait(pe, s.mi_T0, i + 1)
                    for k in range(KD):
                        mm = pe.matmul(pG[:, 0:D], T0[:, k, :], gate_w[:, k, :], start=(k == 0), stop=(k == KD - 1))
                    mm.then_inc(s.mi_gate_ready, 1)

            def b(t, n):
                i = num(t)
                if n == 1:
                    wait(pe, s.mi_xn1, i + 1)
                    for k in range(KD):
                        mm = pe.transpose(pT[:, 256 + k * 128:256 + (k + 1) * 128], xn1[:, k * 128:(k + 1) * 128], m.ident[:, :])
                    mm.then_inc(s.mi_turned1, 1)
                    wait(pe, s.mi_T1, i + 1)
                    for k in range(KD):
                        mm = pe.matmul(pD[:, 0:DOWN], T1[:, k, :], down_w[:, k, :], start=(k == 0), stop=(k == KD - 1))
                    mm.then_inc(s.mi_down_ready, 1)
                    wait(pe, s.mi_expert_added, i * E)
                    for e in range(E):
                        for k in range(KD):
                            mm = pe.matmul(pE[e // 2][:, e % 2, :], T1[:, k, :], ew[:, e, k, :], start=(k == 0), stop=(k == KD - 1))
                    mm.then_inc(s.mi_experts_ready, 1)
                if n == 2:
                    wait(pe, s.mi_gates, i + 1)
                    wait(pe, s.mi_moe, i)
                    pe.transpose(pK[0:E, 256:384], gates[:, :], m.ident[:, :]).then_inc(s.mi_gates_turned, 1)
                    wait(pe, s.mi_qn, i + 1)
                    wait(pe, s.mi_kcat, i + 1)
                    wait(pe, s.mi_gT, i + 1)
                    pe.transpose(pK[:, 0:128], qn[:, :], m.ident[:, :])
                    pe.transpose(pK[:, 128:256], kcat[:, :], m.ident[:, :]).then_inc(s.mi_qk_turned, 1)
                    pe.matmul(pG[:, 256:512], gT[:, :], eb[:, :], start=True, stop=True).then_inc(s.mi_bias_ready, 1)

            wait(pe, s.mi_loaded, 16 * LOADS)
            wait(pe, s.mi_consts, 32)
            run(pe, a, b)

        @block.scalar
        def _(act):
            def a(t, n):
                i = num(t)
                if n == 2:
                    wait(act, s.mi_turned0, i + 1)
                    act.activation(T0[:, :, :].rearrange("p k n -> p (k n)"), pT[:, 0:256], ACT.Copy).then_inc(s.mi_T0, 1)
                    wait(act, s.mi_gate_biased, i + 1)
                    act.activation(th[:, :], th[:, :], ACT.Tanh, scale=0.5).then_inc(s.mi_tanh, 1)
                if n == 3:
                    wait(act, s.mi_hat3, i + 1)
                    act.activation(hat[:, :], hat[:, :], ACT.Silu).then_inc(s.mi_silu, 1)

            def b(t, n):
                i = num(t)
                if n == 1:
                    wait(act, s.mi_turned1, i + 1)
                    act.activation(T1[:, :, :].rearrange("p k n -> p (k n)"), pT[:, 256:512], ACT.Copy).then_inc(s.mi_T1, 1)
                    wait(act, s.mi_down_ready, i + 1)
                    act.activation(dn[:, :], pD[:, 0:DOWN], ACT.Copy).then_inc(s.mi_dn, 1)
                    wait(act, s.mi_dn, i + 1)
                    act.activation(sqd[:, 0:QR], dn[:, 0:QR], ACT.Square, accum_out=ssd[:, 0:1]).then_inc(s.mi_ssd, 1)
                    wait(act, s.mi_ssd, 2 * i + 1)
                    act.activation(sqd[:, 0:KVR], dn[:, QR:QR + KVR], ACT.Square, accum_out=ssd[:, 1:2]).then_inc(s.mi_ssd, 1)
                    wait(act, s.mi_route_arg, i + 1)
                    act.activation(garg[:, :], garg[:, :], ACT.Tanh).then_inc(s.mi_route_tanh, 1)
                if n == 2:
                    wait(act, s.mi_gates_turned, i + 1)
                    act.activation(gT[:, :], pK[0:E, 256:384], ACT.Copy).then_inc(s.mi_gT, 1)

            run(act, a, b)

        @block.vector
        def _(dve):
            def a(t, n):
                i = num(t)
                tile = slice(i, i + 1) if t[0].__class__ is int else bass.ds(i, 1)
                if n == 1:
                    dve.tensor_scalar(xn0[:, :], x[:, tile, :].rearrange("p o d -> p (o d)"), m.mean[:, tile], m.rstd[:, tile],
                                      ALU.subtract, ALU.mult).then_inc(s.mi_xn0, 1)
                if n == 2:
                    row = slice(t[0], t[0] + 1) if t[0].__class__ is int else bass.ds(t[0], 1)
                    wait(dve, s.mi_gate_ready, i + 1)
                    dve.tensor_tensor(th[:, :], pG[:, 0:D], gate_b[:, :], ALU.add).then_inc(s.mi_gate_biased, 1)
                    wait(dve, s.mi_tanh, i + 1)
                    if t[1] == CH:
                        row = slice(t[0] + 1, t[0] + 2) if t[0].__class__ is int else bass.ds(t[0] + 1, 1)
                    dve.scalar_tensor_tensor(th[:, :], th[:, :], 1.0, m.half_bc[:, row, :].rearrange("p o d -> p (o d)"),
                                             ALU.add, ALU.mult).then_inc(s.mi_gated, 1)
                    wait(dve, s.mi_gated, i + 1)
                    dve.tensor_tensor(out[:, :], xn0[:, :], th[:, :], ALU.add).then_inc(s.mi_out, 1)
                    wait(dve, s.mi_out, i + 1)
                    dve.bn_stats(st[:, :], out[:, :]).then_inc(s.mi_stats, 1)
                    wait(dve, s.mi_stats, i + 1)
                    dve.tensor_copy(idle[:, :], m.minus_half[:, 0:1])
                    dve.bn_aggr(mv[:, :], st[:, :]).then_inc(s.mi_aggr, 1)
                if n == 3:
                    wait(dve, s.mi_rstd, i + 1)
                    dve.tensor_scalar(hat[:, :], out[:, :], mv[:, 0:1], rs[:, :], ALU.subtract, ALU.mult).then_inc(s.mi_hat, 1)
                    wait(dve, s.mi_hat, i + 1)
                    dve.tensor_tensor(hat[:, :], hat[:, :], out_g[:, :], ALU.mult).then_inc(s.mi_hat2, 1)
                    wait(dve, s.mi_hat2, i + 1)
                    dve.tensor_tensor(hat[:, :], hat[:, :], out_b[:, :], ALU.add).then_inc(s.mi_hat3, 1)
                    wait(dve, s.mi_silu, i + 1)
                    acc = m.acc[:, tile, :].rearrange("p o d -> p (o d)")
                    dve.tensor_tensor(sg[:, :], acc, hat[:, :], ALU.mult).then_inc(s.mi_sg, 1)
                    wait(dve, s.mi_sg, i + 1)
                    dve.tensor_tensor(x1[:, :], sg[:, :], x[:, tile, :].rearrange("p o d -> p (o d)"), ALU.add).then_inc(s.mi_x1, 1)
                    wait(dve, s.mi_x1, i + 1)
                    dve.bn_stats(st1[:, :], x1[:, :]).then_inc(s.mi_stats1, 1)
                    wait(dve, s.mi_stats1, i + 1)
                    dve.tensor_scalar(acc, x1[:, :], 1.0, None, ALU.mult)
                    dve.bn_aggr(mv1[:, :], st1[:, :]).then_inc(s.mi_aggr1, 1)
                if n == 4:
                    wait(dve, s.mi_rstd1, i + 1)
                    dve.tensor_scalar(xn1[:, :], x1[:, :], mv1[:, 0:1], rs1[:, :], ALU.subtract, ALU.mult).then_inc(s.mi_xn1, 1)

            def b(t, n):
                i = num(t)
                tile = slice(i, i + 1) if t[0].__class__ is int else bass.ds(i, 1)
                lg = dn[:, QR + KVR + 2 * ROPE:DOWN]
                if n == 1:
                    r = i * 8
                    wait(dve, s.mi_dn, i + 1)
                    dve.tensor_tensor(gt[:, :, :], lg[:, None, :].to_broadcast([128, E, E]),
                                      lg[:, :, None].to_broadcast([128, E, E]), ALU.is_gt).then_inc(s.mi_route, 1)
                    dve.tensor_tensor(eq[:, :, :], lg[:, None, :].to_broadcast([128, E, E]),
                                      lg[:, :, None].to_broadcast([128, E, E]), ALU.is_equal).then_inc(s.mi_route, 1)
                    wait(dve, s.mi_route, r + 2)
                    dve.tensor_tensor(eq[:, :, :], eq[:, :, :], before[:, :, :], ALU.mult).then_inc(s.mi_route, 1)
                    wait(dve, s.mi_route, r + 3)
                    dve.tensor_tensor(gt[:, :, :], gt[:, :, :], eq[:, :, :], ALU.add).then_inc(s.mi_route, 1)
                    wait(dve, s.mi_route, r + 4)
                    dve.tensor_reduce(rank[:, :], gt[:, :, :], AX, ALU.add).then_inc(s.mi_route, 1)
                    wait(dve, s.mi_route, r + 5)
                    dve.tensor_scalar(sel[:, :], rank[:, :], TOPK - 0.5, None, ALU.is_lt).then_inc(s.mi_route, 1)
                    wait(dve, s.mi_route, r + 6)
                    dve.tensor_tensor(sl[:, :], sel[:, :], lg, ALU.mult).then_inc(s.mi_route, 1)
                    wait(dve, s.mi_route, r + 7)
                    dve.tensor_reduce(hsum[:, 0:1], sl[:, :], AX, ALU.add).then_inc(s.mi_route, 1)
                    wait(dve, s.mi_route, r + 8)
                    dve.scalar_tensor_tensor(garg[:, :], hsum[:, 0:1].to_broadcast([128, E]), -0.5, lg, ALU.mult, ALU.add)\
                        .then_inc(s.mi_route_arg, 1)
                    wait(dve, s.mi_route_tanh, i + 1)
                    dve.tensor_scalar(garg[:, :], garg[:, :], 0.5, 0.5, ALU.mult, ALU.add).then_inc(s.mi_route_arg2, 1)
                    wait(dve, s.mi_route_arg2, i + 1)
                    dve.tensor_tensor(gates[:, :], garg[:, :], sel[:, :], ALU.mult).then_inc(s.mi_gates, 1)
                if n == 2:
                    wait(dve, s.mi_rsd, i + 1)
                    kv = dn[:, QR:QR + KVR]
                    dve.scalar_tensor_tensor(qn[:, :], dn[:, 0:QR], rsd[:, 0:1], norm_w[:, 0:QR], ALU.mult, ALU.mult).then_inc(s.mi_qn, 1)
                    dve.scalar_tensor_tensor(kcat[:, 0:KVR], kv, rsd[:, 1:2], norm_w[:, QR:], ALU.mult, ALU.mult).then_inc(s.mi_kv_done, 1)
                    dve.scalar_tensor_tensor(m.kv[:, tile, :].rearrange("p o d -> p (o d)"), kv, rsd[:, 1:2],
                                             norm_w[:, QR:], ALU.mult, ALU.mult).then_inc(s.mi_kv_done, 1)
                    c = t[1]
                    o = QR + KVR
                    dve.tensor_tensor(kr[:, :], dn[:, o:o + ROPE], kcos[:, c, :], ALU.mult).then_inc(s.mi_rope, 1)
                    dve.tensor_tensor(kcat[:, KVR:], dn[:, o + ROPE:o + 2 * ROPE], ksin[:, c, :], ALU.mult).then_inc(s.mi_rope, 1)
                    wait(dve, s.mi_rope, 2 * i + 2)
                    wait(dve, s.mi_kv_done, 2 * i + 2)
                    dve.tensor_tensor(kcat[:, KVR:], kcat[:, KVR:], kr[:, :], ALU.add).then_inc(s.mi_kcat, 1)
                    wait(dve, s.mi_qk_turned, i + 1)
                    dve.tensor_scalar(m.qkT[:, :, bass.ds(i * 128, 128)], pK[:, 0:256].rearrange("p (a n) -> p a n", a=2),
                                      1.0, None, ALU.mult).then_inc(s.mi_qk_done, 1)
                if n == 3:
                    wait(dve, s.mi_experts_ready, i + 1)
                    for e in range(E):
                        src = pE[e // 2][:, e % 2, :]
                        if e == 0:
                            dve.tensor_scalar(moe[:, :], src, gates[:, 0:1], None, ALU.mult).then_inc(s.mi_expert_added, 1)
                        else:
                            wait(dve, s.mi_expert_added, i * E + e)
                            dve.scalar_tensor_tensor(moe[:, :], src, gates[:, e:e + 1], moe[:, :], ALU.mult, ALU.add)\
                                .then_inc(s.mi_expert_added, 1)
                    wait(dve, s.mi_bias_ready, i + 1)
                    wait(dve, s.mi_expert_added, i * E + E)
                    dve.tensor_tensor(m.moe[:, tile, :].rearrange("p o d -> p (o d)"), moe[:, :], pG[:, 256:512], ALU.add)\
                        .then_inc(s.mi_moe, 1)

            wait(dve, s.mi_loaded, 16 * LOADS)
            run(dve, a, b)

        @block.gpsimd
        def _(pool):
            def a(t, n):
                i = num(t)
                if n == 2:
                    wait(pool, s.mi_aggr, i + 1)
                    pool.tensor_tensor(rs[:, :], mv[:, 1:2], eps[:, 0:1], ALU.add).then_inc(s.mi_eps, 1)
                    wait(pool, s.mi_eps, i + 1)
                    pool.tensor_tensor(rs[:, :], rs[:, :], m.minus_half[:, 0:1], ALU.pow).then_inc(s.mi_rstd, 1)
                if n == 3:
                    wait(pool, s.mi_aggr1, i + 1)
                    pool.tensor_tensor(rs1[:, :], mv1[:, 1:2], eps[:, 1:2], ALU.add).then_inc(s.mi_eps1, 1)
                    wait(pool, s.mi_eps1, i + 1)
                    pool.tensor_tensor(rs1[:, :], rs1[:, :], m.minus_half[:, 0:1], ALU.pow).then_inc(s.mi_rstd1, 1)

            def b(t, n):
                i = num(t)
                if n == 1:
                    wait(pool, s.mi_ssd, 2 * i + 2)
                    pool.tensor_tensor(rsd[:, :], ssd[:, :], inv[:, :], ALU.mult).then_inc(s.mi_rsd_chain, 1)
                    wait(pool, s.mi_rsd_chain, 2 * i + 1)
                    pool.tensor_tensor(rsd[:, :], rsd[:, :], eps[:, 0:1].to_broadcast([128, 2]), ALU.add).then_inc(s.mi_rsd_chain, 1)
                    wait(pool, s.mi_rsd_chain, 2 * i + 2)
                    pool.tensor_tensor(rsd[:, :], rsd[:, :], m.minus_half[:, 0:2], ALU.pow).then_inc(s.mi_rsd, 1)

            pool.memset(inv[:, 0:1], 1.0 / QR).then_inc(s.mi_const, 1)
            pool.memset(inv[:, 1:2], 1.0 / KVR).then_inc(s.mi_const, 1)
            pool.memset(eps[:, 0:1], 1e-6).then_inc(s.mi_const, 1)
            pool.memset(eps[:, 1:2], 1e-5).then_inc(s.mi_const, 1)
            wait(pool, s.mi_const, 4)
            run(pool, a, b)


def attention(nc, m, io):
    SCALE = 1.0 / float(np.sqrt(NOPE + ROPE))
    with ExitStack() as ctx:
        def sb(name, shape, dt=F32):
            return ctx.enter_context(nc.sbuf_tensor(name, shape, dt))

        up_q = sb("at_up_q", [128, AH, QR])
        up_kv = sb("at_up_kv", [128, AH, 2, KVR])
        woT = sb("at_woT", [128, AH, D])
        wq = sb("at_wq", [128, AH, KVR + ROPE])
        wqs = sb("at_wqs", [128, AH, ROPE])
        wvo = sb("at_wvo", [128, APAIRS, D])
        qcos, qsin = sb("at_cos", [128, T]), sb("at_sin", [128, T])
        qin, kin, vin = sb("at_qin", [128, T]), sb("at_kin", [128, T]), sb("at_vin", [128, CH, KVR])
        g1 = sb("at_g1", [128, CH, D])
        qT = [sb(f"at_qT{i}", [128, T]) for i in range(2)]
        qr = sb("at_qr", [128, T])
        PR = sb("at_P", [128, CH, T])
        PT = [sb(f"at_PT{j}", [128, T]) for j in range(2)] + [sb("at_PT2", [128, 256])]
        mx, nm, sm, rc = (sb(f"at_{n}", [128, 2, CH]) for n in ("mx", "nm", "sm", "rc"))
        o = sb("at_o", [128, CH, 2, KVR])
        oT = sb("at_oT", [128, APAIRS, T])
        fin = sb("at_fin", [128, CH, D])
        psS = [ctx.enter_context(nc.psum_tensor(f"at_S{i}", [128, 512], F32)) for i in range(3)]
        psT = [ctx.enter_context(nc.psum_tensor(f"at_T{i}", [128, 512], F32)) for i in range(3)]
        psQ = [ctx.enter_context(nc.psum_tensor(f"at_Q{i}", [128, 512], F32)) for i in range(2)]
        s = sems(nc, ctx, "at_loaded", "at_w_ready0", "at_w_ready1", "at_w_done0", "at_w_done1", "at_in", "at_g1in", "at_g1",
                 "at_q_ready", "at_cos_done", "at_sin_done", "at_qT", "at_s_ready", "at_max", "at_nm", "at_exp",
                 "at_turned", "at_t0", "at_t1", "at_t2", "at_pv_ready", "at_rc", "at_o", "at_oT_ready", "at_oT",
                 "at_out_ready", "at_sg", "at_fin", "at_stored")
        block = ctx.enter_context(nc.Block())
        SCORES = [(0, 0), (1, 0), (0, 128), (2, 0)]
        MADE = [0, 2, 1, 3]
        THERE = [2, 3, 2, 4]

        def place(i, j):
            return {0: (0, i * 128), 1: (1, (i - 1) * 128), 2: (2, (i - 2) * 128), 3: (1, 384)}[j]

        @block.sync
        def _(sp):
            sp.dma_start(up_q[:, :, :], io.wq_up).then_inc(s.at_loaded, 16)
            sp.dma_start(up_kv[:, :, :, :], io.wkv_up).then_inc(s.at_loaded, 16)
            sp.dma_start(woT[:, :, :], io.woT.rearrange("(h v) n -> v h n", v=VDIM)).then_inc(s.at_loaded, 16)
            sp.dma_start(wq[:, :, KVR:], io.wq_ropeT).then_inc(s.at_loaded, 16)
            sp.dma_start(wqs[:, :, :], io.wq_swapT).then_inc(s.at_loaded, 16)
            sp.dma_start(qcos[:, :], io.c_qcos).then_inc(s.at_loaded, 16)
            sp.dma_start(qsin[:, :], io.c_qsin).then_inc(s.at_loaded, 16)
            out_tiles = io.out.rearrange("b (c p) d -> p (b c) d", p=128)
            with sp.Fori(0, B) as b:
                sp.wait_ge(s.at_fin, b + 1)
                sp.wait_ge(s.at_loaded, 16 * 7)
                sp.dma_start(out_tiles[:, bass.ds(b * CH, CH), :], fin[:, :, :]).then_inc(s.at_stored, 16)
            sp.wait_ge(s.at_stored, 16 * B)

        @block.tensor
        def _(pe):
            def queries(b, h):
                n = b * AH + h
                wait(pe, s.at_cos_done, n)
                wait(pe, s.at_sin_done, n)
                pe.matmul(psQ[0][:, :], wq[:, h, :], qin[:, :], start=True, stop=True)
                pe.matmul(psQ[1][KVR:128, :], wqs[:, h, :], qin[:, :], start=True, stop=True).then_inc(s.at_q_ready, 1)

            def scores(b, h, i):
                n = b * AH + h
                bank, at = SCORES[i]
                if i == 0:
                    wait(pe, s.at_qT, n + 1)
                wait(pe, s.at_exp, n * CH)
                w = (i + 1) * 128
                pe.matmul(psS[bank][:, at:at + w], qT[h % 2][:, i * 128:(i + 1) * 128], kin[:, 0:w], start=True, stop=False)
                pe.matmul(psS[bank][:, at + w - 128:at + w], m.identb[:, :], m.maskb[:, 1, :], start=False, stop=True)\
                    .then_inc(s.at_s_ready, 1)

            def turn(b, h, i):
                n = b * AH + h
                wait(pe, s.at_exp, n * CH + i + 1)
                if i == 0:
                    wait(pe, s.at_t0, n)
                    wait(pe, s.at_oT, b * APAIRS + h // 2)
                if i == 1:
                    wait(pe, s.at_t1, n)
                if i == 2:
                    wait(pe, s.at_o, n)
                for j in range(i + 1):
                    bank, at = place(i, j)
                    mm = pe.transpose(psT[bank][:, at:at + 128], PR[:, i, j * 128:(j + 1) * 128], m.ident[:, :])
                if i == CH - 1:
                    mm.then_inc(s.at_turned, 1)

            def values(b, h):
                n = b * AH + h
                wait(pe, s.at_t0, n + 1)
                wait(pe, s.at_t1, n + 1)
                wait(pe, s.at_t2, n + 1)
                for i in range(CH):
                    for j in range(i + 1):
                        bank, at = place(i, j)
                        mm = pe.matmul(psT[2][:, 256 + i * KVR:256 + (i + 1) * KVR], PT[bank][:, at:at + 128], vin[:, j, :],
                                       start=(j == 0), stop=(j == i))
                mm.then_inc(s.at_pv_ready, 1)

            def turn_out(b, h):
                wait(pe, s.at_o, b * AH + h + 1)
                for i in range(CH):
                    mm = pe.transpose(psT[0][:, i * 128:(i + 1) * 128], o[:, i, :, :].rearrange("p h r -> p (h r)"), m.ident[:, :])
                mm.then_inc(s.at_oT_ready, 1)

            wait(pe, s.at_loaded, 16 * 7)
            for h in range(AH):
                half, at = h % 8, h // 8
                pe.matmul(psS[h // 8][:, half * KVR:(half + 1) * KVR], up_q[:, h, :], up_kv[:, h, 0, :], start=True, stop=True)\
                    .then_inc(s.at_w_ready0, 1)
            for pr in range(APAIRS):
                wait(pe, s.at_w_done1, max(pr - 1, 0))
                for hh in range(2):
                    h = 2 * pr + hh
                    mm = pe.matmul(psQ[pr % 2][hh * KVR:(hh + 1) * KVR, 0:D], up_kv[:, h, 1, :], woT[:, h, :], start=True, stop=True)
                mm.then_inc(s.at_w_ready1, 1)
            wait(pe, s.at_w_done0, 2)
            wait(pe, s.at_w_done1, APAIRS)
            def row_of_batch(b):
                wait(pe, s.at_in, b * 3 + 3)
                queries(b, 0)
                for i in MADE:
                    scores(b, 0, i)
                for h in range(AH):
                    if h < AH - 1:
                        queries(b, h + 1)
                    for i in range(CH):
                        turn(b, h, i)
                    if h < AH - 1:
                        for i in MADE:
                            scores(b, h + 1, i)
                    values(b, h)
                    if h % 2:
                        turn_out(b, h)
                wait(pe, s.at_oT, (b + 1) * APAIRS)
                for c in range(CH):
                    for pr in range(APAIRS):
                        mm = pe.matmul(psQ[c // 2][:, c % 2 * D:(c % 2 + 1) * D], oT[:, pr, c * 128:(c + 1) * 128], wvo[:, pr, :],
                                       start=(pr == 0), stop=(pr == APAIRS - 1))
                mm.then_inc(s.at_out_ready, 1)

            row_of_batch(0)
            with pe.Fori(1, B) as b:
                row_of_batch(b)

        @block.scalar
        def _(act):
            for i in range(2):
                wait(act, s.at_w_ready0, 8 * (i + 1))
                act.activation(wq[:, 8 * i:8 * i + 8, 0:KVR], psS[i][:, :].rearrange("p (h r) -> p h r", r=KVR), ACT.Copy)\
                    .then_inc(s.at_w_done0, 1)
            def row_of_batch(b):
                wait(act, s.at_g1in, b + 1)
                act.activation(g1[:, :, :], g1[:, :, :], ACT.Silu).then_inc(s.at_g1, 1)
                for h in range(AH):
                    n = b * AH + h
                    for i in range(CH):
                        bank, at = SCORES[i]
                        w = (i + 1) * 128
                        if i == 0:
                            wait(act, s.at_nm, n + 1)
                            wait(act, s.at_turned, n)
                        act.activation(PR[:, i, 0:w], psS[bank][:, at:at + w], ACT.Exp, bias=nm[:, h % 2, i:i + 1], scale=SCALE,
                                       accum_out=sm[:, h % 2, i:i + 1]).then_inc(s.at_exp, 1)
                    wait(act, s.at_turned, n + 1)
                    wait(act, s.at_pv_ready, n)
                    act.activation(PT[0][:, :], psT[0][:, :], ACT.Copy).then_inc(s.at_t0, 1)
                    act.activation(PT[2][:, :], psT[2][:, 0:256], ACT.Copy).then_inc(s.at_t2, 1)
                    if h % 2:
                        wait(act, s.at_oT_ready, b * APAIRS + h // 2 + 1)
                        act.activation(oT[:, h // 2, :], psT[0][:, :], ACT.Copy).then_inc(s.at_oT, 1)

            row_of_batch(0)
            with act.Fori(1, B) as b:
                row_of_batch(b)

        @block.vector
        def _(dve):
            def rope(b, h):
                n = b * AH + h
                wait(dve, s.at_q_ready, n + 1)
                dve.tensor_tensor(qT[h % 2][:, :], psQ[0][:, :], qcos[:, :], ALU.mult).then_inc(s.at_cos_done, 1)
                wait(dve, s.at_qT, n)
                dve.tensor_tensor(qr[KVR:128, :], psQ[1][KVR:128, :], qsin[KVR:128, :], ALU.mult).then_inc(s.at_sin_done, 1)

            for pr in range(APAIRS):
                wait(dve, s.at_w_ready1, pr + 1)
                dve.tensor_copy(wvo[:, pr, :], psQ[pr % 2][:, 0:D]).then_inc(s.at_w_done1, 1)
            wait(dve, s.at_loaded, 16 * 7)
            def row_of_batch(b):
                row = slice(b * T, b * T + T) if b.__class__ is int else bass.ds(b * T, T)
                tiles = slice(b * CH, b * CH + CH) if b.__class__ is int else bass.ds(b * CH, CH)
                wait(dve, s.at_fin, b)
                dve.tensor_scalar(qin[:, :], m.qkT[:, 0, row], 1.0, None, ALU.mult).then_inc(s.at_in, 1)
                dve.tensor_scalar(kin[:, :], m.qkT[:, 1, row], 1.0, None, ALU.mult).then_inc(s.at_in, 1)
                dve.tensor_scalar(vin[:, :, :], m.kv[:, tiles, :], 1.0, None, ALU.mult).then_inc(s.at_in, 1)
                dve.tensor_scalar(g1[:, :, :], m.moe[:, tiles, :], 1.0, None, ALU.mult).then_inc(s.at_g1in, 1)
                rope(b, 0)
                for h in range(AH):
                    n = b * AH + h
                    for i in range(CH):
                        bank, at = SCORES[i]
                        w = (i + 1) * 128
                        wait(dve, s.at_s_ready, n * CH + THERE[i])
                        dve.tensor_reduce(mx[:, h % 2, i:i + 1], psS[bank][:, at:at + w], AX, ALU.max).then_inc(s.at_max, 1)
                    wait(dve, s.at_max, n * CH + CH)
                    dve.tensor_scalar(nm[:, h % 2, :], mx[:, h % 2, :], -SCALE, None, ALU.mult).then_inc(s.at_nm, 1)
                    if h < AH - 1:
                        rope(b, h + 1)
                    wait(dve, s.at_exp, n * CH + CH)
                    dve.reciprocal(rc[:, h % 2, :], sm[:, h % 2, :]).then_inc(s.at_rc, 1)
                    wait(dve, s.at_turned, n + 1)
                    dve.tensor_copy(PT[1][:, :], psT[1][:, :]).then_inc(s.at_t1, 1)
                    wait(dve, s.at_rc, n + 1)
                    wait(dve, s.at_pv_ready, n + 1)
                    if h % 2 == 0:
                        wait(dve, s.at_oT_ready, b * APAIRS + h // 2)
                    dve.tensor_tensor(o[:, :, h % 2, :], psT[2][:, 256:512].rearrange("p (i r) -> p i r", r=KVR),
                                      rc[:, h % 2, :, None].to_broadcast([128, CH, KVR]), ALU.mult).then_inc(s.at_o, 1)
                wait(dve, s.at_out_ready, b + 1)
                wait(dve, s.at_g1, b + 1)
                wait(dve, s.at_stored, b * 16)
                for half in range(2):
                    dve.tensor_tensor(g1[:, 2 * half:2 * half + 2, :], psQ[half][:, :].rearrange("p (c d) -> p c d", d=D),
                                      g1[:, 2 * half:2 * half + 2, :], ALU.mult).then_inc(s.at_sg, 1)
                wait(dve, s.at_sg, 2 * b + 2)
                dve.tensor_tensor(fin[:, :, :], g1[:, :, :], m.acc[:, tiles, :], ALU.add).then_inc(s.at_fin, 1)

            row_of_batch(0)
            with dve.Fori(1, B) as b:
                row_of_batch(b)

        @block.gpsimd
        def _(pool):
            def row_of_batch(b):
                for h in range(AH):
                    n = b * AH + h
                    wait(pool, s.at_cos_done, n + 1)
                    wait(pool, s.at_sin_done, n + 1)
                    pool.tensor_tensor(qT[h % 2][KVR:128, :], qT[h % 2][KVR:128, :], qr[KVR:128, :], ALU.add).then_inc(s.at_qT, 1)

            row_of_batch(0)
            with pool.Fori(1, B) as b:
                row_of_batch(b)


def constants():
    q = np.arange(128)
    keep_up = q[:, None] <= q[None, :]
    c = {"c_ident": np.eye(128, dtype=np.float32), "c_triu": keep_up.astype(np.float32),
         "c_identb": np.eye(128).astype(mybir.dt.np(BF16)),
         "c_maskb": np.stack([np.where(keep_up, 0.0, MASKED), np.where(keep_up.T, 0.0, MASKED)], 1).astype(mybir.dt.np(BF16)),
         "c_onehot": np.tile(np.eye(H), (3, 1)).astype(mybir.dt.np(BF16))}
    f = (1.0 / 10000.0 ** (np.arange(0, ROPE, 2, dtype=np.float32) / ROPE)).astype(np.float32)
    ang = np.outer(np.arange(T, dtype=np.float32), f)
    cos = np.concatenate([np.cos(ang), np.cos(ang)], 1).astype(np.float32)
    sin = np.concatenate([-np.sin(ang), np.sin(ang)], 1).astype(np.float32)
    c["c_kcos"] = np.ascontiguousarray(cos.reshape(CH, 128, ROPE).transpose(1, 0, 2))
    c["c_ksin"] = np.ascontiguousarray(sin.reshape(CH, 128, ROPE).transpose(1, 0, 2))
    c["c_qcos"] = np.concatenate([np.ones((KVR, T), np.float32), cos.T])
    c["c_qsin"] = np.concatenate([np.zeros((KVR, T), np.float32), sin.T])
    e = np.arange(E)
    c["c_before"] = np.ascontiguousarray(np.broadcast_to((e[None, :] < e[:, None]).astype(np.float32), (128, E, E)))
    return c


def layouts(i):
    win = i["L0_attn_Win"]
    x0, z0, b0, c0 = 0, H * P, 2 * H * P, 2 * H * P + H * N
    a = {"x": i["L0_attn_x"], "A_log": i["L0_attn_A_log"], "dt_bias": i["L0_attn_dt_bias"],
         "w_dt": np.ascontiguousarray(win[c0 + H * N:].T)}
    pack = np.empty((PAIRS, 128, PACK), np.float32)
    for p in range(PAIRS):
        rows = [win[x0 + p * 128:x0 + (p + 1) * 128], win[z0 + p * 128:z0 + (p + 1) * 128]]
        taps = [i["L0_attn_conv_w_x"][2 * p:2 * p + 2].reshape(128, TAPS)]
        for h in (2 * p, 2 * p + 1):
            rows += [win[b0 + h * N:b0 + (h + 1) * N], win[c0 + h * N:c0 + (h + 1) * N]]
            taps += [i["L0_attn_conv_w_b"][h], i["L0_attn_conv_w_c"][h]]
        w = np.concatenate(rows).T
        pack[p, :, 0:PACK_CONV] = w.reshape(KD, 128, CHANNELS).transpose(1, 0, 2).reshape(128, -1)
        pack[p, :, PACK_CONV:] = np.concatenate(taps, 1)
    a["w_pack"] = pack
    a["w_out"] = np.ascontiguousarray(i["L0_attn_Wout"].T.reshape(PAIRS, 128, D))
    for n in ("in_gamma", "in_beta", "agg_w", "agg_b", "pn_gamma", "pn_beta", "d1_w", "d2_w", "d2_b", "bc_w", "bc_b",
              "gate_w", "gate_b", "out_gamma", "out_beta"):
        a[n] = i["L0_ffn_" + n]
    a["d1_b"] = np.ascontiguousarray(i["L0_ffn_d1_b"].reshape(HID // 128, 128).T)
    turned = np.concatenate([np.arange(0, ROPE, 2), np.arange(1, ROPE, 2)])
    swapped = np.roll(turned, ROPE // 2)
    wk = i["L1_attn_wk_rope"]
    a["w_down"] = np.ascontiguousarray(np.concatenate(
        [i["L1_attn_wq_down"], i["L1_attn_wkv_down"], wk[turned], wk[swapped], i["L1_ffn_gate_w"]]).T)
    a["q_norm_w"], a["kv_norm_w"] = i["L1_attn_q_norm_w"], i["L1_attn_kv_norm_w"]
    a["wq_up"] = np.ascontiguousarray(i["L1_attn_wq_up"].reshape(AH, NOPE, QR).transpose(1, 0, 2))
    a["wkv_up"] = np.ascontiguousarray(i["L1_attn_wkv_up"].reshape(AH, 2, NOPE, KVR).transpose(2, 0, 1, 3))
    wr = i["L1_attn_wq_rope"].reshape(AH, ROPE, QR)
    a["wq_ropeT"] = np.ascontiguousarray(wr[:, turned].transpose(2, 0, 1))
    a["wq_swapT"] = np.ascontiguousarray(wr[:, swapped].transpose(2, 0, 1))
    a["woT"] = np.ascontiguousarray(i["L1_attn_wo"].T)
    a["expert_w"], a["expert_b"] = i["L1_ffn_expert_w"], i["L1_ffn_expert_b"]
    return a


def program(nc, io):
    m = Buffers()
    with ExitStack() as whole:
        def sb_in(ctx):
            return lambda name, shape, dt=F32: ctx.enter_context(nc.sbuf_tensor(name, shape, dt))

        shared(m, sb_in(whole))
        with ExitStack() as part:
            mixer_buffers(m, sb_in(part))
            norm_and_decay(nc, m, io)
            thought(nc, m, io)
            mixer(nc, m, io)
        sb = sb_in(whole)
        m.moe = sb("moe", [128, TILES, D])
        m.kv = sb("kv", [128, TILES, KVR])
        m.qkT = sb("qkT", [128, 2, TOK])
        middle(nc, m, io)
        attention(nc, m, io)


def kernel(**inputs):
    import concourse.bacc as bacc
    from concourse.bass_utils import run_bass_kernel_spmd

    nc = bacc.Bacc("TRN2", target_bir_lowering=False, num_devices=1)
    arrays = {**layouts({k: np.asarray(v) for k, v in inputs.items()}), **constants()}
    aps = {k: nc.dram_tensor("in_" + k, a.shape, mybir.dt.from_np(a.dtype), kind="ExternalInput").ap()
           for k, a in arrays.items()}
    aps["out"] = nc.dram_tensor("out_0", (B, T, D), F32, kind="ExternalOutput").ap()
    program(nc, namedtuple("Arrays", aps)(**aps))
    r = run_bass_kernel_spmd(nc, [{"in_" + k: np.ascontiguousarray(a) for k, a in arrays.items()}], core_ids=[0])
    return r.results[0]["out_0"]
```

```python
from collections import namedtuple
from contextlib import ExitStack

import concourse.bass as bass
import numpy as np
from concourse import mybir

F32 = mybir.dt.float32
BF16 = mybir.dt.bfloat16
F32R = mybir.dt.float32r
ACT = mybir.ActivationFunctionType
ALU = mybir.AluOpType
AX = mybir.AxisListType.X

B, T, D = 4, 512, 256
TOK = B * T
TILES = TOK // 128
KD = D // 128
H, P, N, TAPS = 32, 64, 128, 4
PAIRS = H // 2
CH = T // 128
CHANNELS = 2 * P * 2 + 4 * N
CONVS = 5
PACK_CONV = KD * CHANNELS
PACK = PACK_CONV + CONVS * TAPS
HID = 1024
K_STEPS = 4
AH, NOPE, ROPE, VDIM, QR, KVR = 16, 128, 64, 128, 128, 64
APAIRS = AH // 2
E, TOPK = 8, 2
DOWN = QR + KVR + 2 * ROPE + E
MASKED = -1e30


class Buffers:
    pass


def sems(nc, ctx, *names):
    return namedtuple("Sems", names)(*[ctx.enter_context(nc.semaphore(n)) for n in names])


def wait(eng, sem, value):
    if value.__class__ is not int or value > 0:
        eng.wait_ge(sem, value)


def rsqrt_small(pool, out, x, scale, eps, minus_half, chain, base):
    pool.tensor_scalar(out, x, scale, eps, ALU.mult, ALU.add).then_inc(chain, 1)
    pool.wait_ge(chain, base + 1)
    return pool.tensor_tensor(out, out, minus_half, ALU.pow)


def shared(m, sb):
    m.ident = sb("ident", [128, 128])
    m.identb = sb("identb", [128, 128], BF16)
    m.maskb = sb("maskb", [128, 2, 128], BF16)
    m.minus_half = sb("minus_half", [128, TILES])
    m.acc = sb("acc", [128, TILES, D])
    m.mean = sb("mean", [128, TILES])
    m.rstd = sb("rstd", [128, TILES])
    m.bcT = sb("bcT", [128, KD, B])


def mixer_buffers(m, sb):
    m.onehot = sb("onehot", [96, 2, H], BF16)
    m.inv_P = sb("inv_P", [128, 2 * B])
    m.eps6 = sb("eps6", [128, 2 * B])
    m.tab = sb("tab", [128, 4, TILES, H])
    m.cs = sb("cs", [96, TOK], BF16)
    m.xnT2 = [sb(f"xnT_{part}", [128, KD, TOK], F32R) for part in ("hi", "lo")]
    m.w = [sb(f"w{u}", [128, PACK]) for u in range(2)]
    m.wo = sb("wo", [128, 2, D])
    conv = [sb(f"conv{u}", [128, 6, B, T]) for u in range(2)]
    m.conv = [[conv[u][:, ch, :, :] for ch in range(6)] for u in range(2)]
    m.ynT = [sb("ynT0", [128, B, T])[:, :, :], m.conv[1][BZ]]
    m.xnT = conv[0][:, 0:2, :, :].rearrange("p k b t -> p k (b t)")
    flat = conv[1][:, :, :, :].rearrange("p c b t -> p (c b t)")
    m.stage_x = flat[:, 0:TILES * D].rearrange("p (t d) -> p t d", d=D)
    m.work = flat[:, TILES * D:TILES * D + 4096]
    w = flat[:, TILES * D:]
    at = 0
    m.thought_w = {}
    for name, shape in (("agg", (KD, D)), ("d1", (KD, HID)), ("d2", (HID // 128, D)), ("bc", (KD, D)), ("rows", (6, D))):
        size = shape[0] * shape[1]
        m.thought_w[name] = w[:, at:at + size].rearrange("p (a b) -> p a b", a=shape[0])
        at += size
    m.thought_w["d1b"] = w[:, at:at + HID // 128]
    m.stage_rows = flat[:, TILES * D + 4096:TILES * D + 4096 + TOK]


def norm_and_decay(nc, m, io):
    xt = m.stage_x
    with ExitStack() as ctx:
        stats = ctx.enter_context(nc.sbuf_tensor("stats", [128, TILES, 6], F32))
        mv = ctx.enter_context(nc.sbuf_tensor("mv", [128, TILES, 2], F32))
        triu, ones = (ctx.enter_context(nc.sbuf_tensor(f"na_{n}", [128, 128], F32)) for n in ("triu", "ones"))
        w_dt = ctx.enter_context(nc.sbuf_tensor("na_w_dt", [128, KD, H], F32))
        bank = [ctx.enter_context(nc.psum_tensor(f"na{i}", [128, 512], F32)) for i in range(8)]
        s = sems(nc, ctx, "na_const", "na_const2", "na_x0", "na_x1", "na_x2", "na_x3", "na_half", "na_stats", "na_aggr", "na_eps", "na_rstd",
                 "na_xn", "na_turned", "na_even", "na_odd", "na_dtraw", "na_biased", "na_abs", "na_exp", "na_eA",
                 "na_ln", "na_relu", "na_dt", "na_da", "na_da3", "na_cs", "na_tot", "na_tot_copied", "na_csd",
                 "na_tabs", "na_rows", "na_part", "na_zero")
        m.old_sems = list(s)
        x_loaded = [s.na_x0, s.na_x1, s.na_x2, s.na_x3]
        raw, ab, relu, tot = (m.work[:, i * 512:(i + 1) * 512] for i in range(4))
        da3 = m.work[:, 2048:2048 + TILES * 96].rearrange("p (t g h) -> p t g h", g=3, h=H)
        r1 = m.stage_rows[0:96, 0:TOK]
        ex_A = m.work[:, 3600:3600 + H]
        A_row = m.work[:, 3632:3632 + H]
        dtb_row = m.work[:, 3664:3664 + H]
        block = ctx.enter_context(nc.Block())

        def tiles_of(ap, h=H):
            return ap.rearrange("p (t h) -> p t h", h=h)

        @block.sync
        def _(sp):
            for b in range(B):
                sp.dma_start(xt[:, b * CH:(b + 1) * CH, :],
                             io.x[b].rearrange("(c p) d -> p c d", p=128)).then_inc(x_loaded[b], 16)
            sp.dma_start(m.ident[:, :], io.c_ident).then_inc(s.na_const, 16)
            sp.dma_start(triu[:, :], io.c_triu).then_inc(s.na_const, 16)
            sp.dma_start(w_dt[:, :, :], io.w_dt.rearrange("(k p) h -> p k h", p=128)).then_inc(s.na_const, 16)
            sp.dma_start(A_row, io.A_log.partition_broadcast(128)).then_inc(s.na_const2, 16)
            sp.dma_start(dtb_row, io.dt_bias.partition_broadcast(128)).then_inc(s.na_const2, 16)
            sp.dma_start(m.identb[:, :], io.c_identb).then_inc(s.na_const2, 16)
            sp.dma_start(m.maskb[:, :, :], io.c_maskb).then_inc(s.na_const2, 16)
            sp.dma_start(m.onehot[:, :, :], io.c_onehot).then_inc(s.na_const2, 16)
            sp.wait_ge(s.na_const2, 80)

        @block.vector
        def _(dve):
            for t in range(TILES):
                dve.wait_ge(x_loaded[t // CH], 16)
                dve.bn_stats(stats[:, t, :], xt[:, t, :]).then_inc(s.na_stats, 1)
            for t in range(TILES):
                dve.wait_ge(s.na_stats, t + 1)
                dve.bn_aggr(mv[:, t, :], stats[:, t, :]).then_inc(s.na_aggr, 1)
            dve.wait_ge(s.na_rstd, 1)
            for t in range(TILES):
                dve.tensor_scalar(xt[:, t, :], xt[:, t, :], mv[:, t, 0:1], m.rstd[:, t:t + 1],
                                  ALU.subtract, ALU.mult).then_inc(s.na_xn, 1)
            dve.tensor_copy(m.mean[:, :], mv[:, :, 0]).then_inc(s.na_xn, 1)
            for g in range(0, 8, 2):
                dve.wait_ge(s.na_turned, g + 1)
                dve.tensor_copy(m.xnT[:, g % 2, g // 2 * 512:(g // 2 + 1) * 512], bank[g][:, :]).then_inc(s.na_even, 1)
            dve.wait_ge(s.na_dtraw, 1)
            dve.wait_ge(s.na_const2, 80)
            dve.tensor_tensor(tiles_of(raw), tiles_of(bank[0][:, :]),
                              dtb_row[:, None, :].to_broadcast([128, TILES, H]), ALU.add).then_inc(s.na_biased, 1)
            dve.wait_ge(s.na_biased, 1)
            dve.tensor_scalar(relu, raw, 0.0, None, ALU.max).then_inc(s.na_relu, 1)
            dve.wait_ge(s.na_relu, 1)
            dve.wait_ge(s.na_ln, 1)
            dt = m.tab[:, 0, :, :]
            dve.tensor_tensor(dt, tiles_of(relu), tiles_of(ab), ALU.add).then_inc(s.na_dt, 1)
            dve.wait_ge(s.na_dt, 1)
            dve.wait_ge(s.na_eA, 1)
            dve.scalar_tensor_tensor(tiles_of(raw), dt, -1.0,
                                     ex_A[:, None, :].to_broadcast([128, TILES, H]), ALU.mult, ALU.mult).then_inc(s.na_da, 1)
            dve.wait_ge(s.na_da, 1)
            for g in range(3):
                dve.tensor_copy(da3[:, :, g, :], tiles_of(raw)).then_inc(s.na_da3, 1)
            dve.wait_ge(s.na_tot, 1)
            dve.tensor_copy(tot, bank[2][:, :]).then_inc(s.na_tot_copied, 1)
            dve.wait_ge(s.na_tot_copied, 1)
            dve.wait_ge(s.na_tabs, 1)
            dve.tensor_tensor(relu, tot, bank[1][:, :], ALU.subtract).then_inc(s.na_csd, 1)
            n = 0
            for q in range(4):
                dve.wait_ge(s.na_rows, q + 1)
                at = slice(q * 512, (q + 1) * 512)
                rows = bank[3 + q][0:96, :]
                dve.tensor_copy(m.cs[:, at], rows).then_inc(s.na_part, 1)
                dve.wait_ge(s.na_part, n + 1)
                dve.tensor_tensor(r1[:, at], rows, m.cs[:, at], ALU.subtract).then_inc(s.na_part, 1)
                dve.wait_ge(s.na_part, n + 2)
                dve.tensor_copy(m.cs[0:64, at], r1[0:64, at]).then_inc(s.na_part, 1)
                dve.wait_ge(s.na_part, n + 3)
                dve.tensor_tensor(r1[0:32, at], r1[0:32, at], m.cs[0:32, at], ALU.subtract).then_inc(s.na_part, 1)
                dve.wait_ge(s.na_part, n + 4)
                dve.tensor_copy(m.cs[0:32, at], r1[0:32, at]).then_inc(s.na_part, 1)
                n += 5

        @block.gpsimd
        def _(pool):
            pool.memset(m.minus_half[:, :], -0.5).then_inc(s.na_half, 1)
            pool.memset(ones[:, :], 1.0).then_inc(s.na_half, 1)
            pool.memset(m.inv_P[:, :], 1.0 / P).then_inc(s.na_zero, 1)
            pool.memset(m.eps6[:, :], 1e-6).then_inc(s.na_zero, 1)
            pool.memset(m.acc[:, :, :], 0.0).then_inc(s.na_zero, 1)
            pool.wait_ge(s.na_half, 1)
            pool.wait_ge(s.na_aggr, TILES)
            rsqrt_small(pool, m.rstd[:, :], mv[:, :, 1], 1.0, 1e-5, m.minus_half[:, 0:TILES], s.na_eps, 0)\
                .then_inc(s.na_rstd, 1)

        @block.tensor
        def _(pe):
            pe.wait_ge(s.na_const, 48)
            for g in range(8):
                b, k = g // 2, g % 2
                pe.wait_ge(s.na_xn, CH * (b + 1))
                for c in range(CH):
                    mm = pe.transpose(bank[g][:, c * 128:(c + 1) * 128], xt[:, b * CH + c, k * 128:(k + 1) * 128],
                                      m.ident[:, :])
                mm.then_inc(s.na_turned, 1)
            pe.wait_ge(s.na_even, 4)
            pe.wait_ge(s.na_odd, 4)
            for t in range(TILES):
                for k in range(KD):
                    mm = pe.matmul(bank[0][:, t * H:(t + 1) * H], m.xnT[:, k, t * 128:(t + 1) * 128],
                                   w_dt[:, k, :], start=(k == 0), stop=(k == KD - 1))
            mm.then_inc(s.na_dtraw, 1)
            pe.wait_ge(s.na_da, 1)
            pe.wait_ge(s.na_half, 2)
            pe.matmul(bank[1][:, :], triu[:, :], raw, start=True, stop=True).then_inc(s.na_cs, 1)
            pe.matmul(bank[2][:, :], ones[:, :], raw, start=True, stop=True).then_inc(s.na_tot, 1)
            pe.wait_ge(s.na_da3, 3)
            for q in range(4):
                for c in range(4):
                    t = 4 * q + c
                    mm = pe.matmul(bank[3 + q][0:96, c * 128:(c + 1) * 128],
                                   da3[:, t, :, :].rearrange("p g h -> p (g h)"), triu[:, :], start=True, stop=True)
                mm.then_inc(s.na_rows, 1)

        @block.scalar
        def _(act):
            for g in range(1, 8, 2):
                act.wait_ge(s.na_turned, g + 1)
                act.activation(m.xnT[:, g % 2, g // 2 * 512:(g // 2 + 1) * 512], bank[g][:, :], ACT.Copy)\
                    .then_inc(s.na_odd, 1)
            act.wait_ge(s.na_const2, 80)
            act.activation(ex_A, A_row, ACT.Exp).then_inc(s.na_eA, 1)
            act.wait_ge(s.na_biased, 1)
            act.activation(ab, raw, ACT.Abs).then_inc(s.na_abs, 1)
            act.wait_ge(s.na_abs, 1)
            act.activation(ab, ab, ACT.Exp, scale=-1.0).then_inc(s.na_exp, 1)
            act.wait_ge(s.na_exp, 1)
            act.activation(ab, ab, ACT.Ln, bias=1.0).then_inc(s.na_ln, 1)
            act.wait_ge(s.na_cs, 1)
            act.activation(m.tab[:, 1, :, :], tiles_of(bank[1][:, :]), ACT.Exp).then_inc(s.na_tabs, 1)
            act.wait_ge(s.na_csd, 1)
            act.activation(m.tab[:, 2, :, :], tiles_of(relu), ACT.Exp).then_inc(s.na_tabs, 1)
            act.activation(m.tab[:, 3, :, :], tiles_of(tot), ACT.Exp).then_inc(s.na_tabs, 1)


BX, BZ, BB0, BC0, BB1, BC1 = range(6)
PIECES = [(ch, half) for ch in (BB0, BC0, BB1, BC1, BX, BZ) for half in range(2)]
NP = len(PIECES)
NC = 2 * CONVS
CONV_OF = {BX: 0, BB0: 1, BC0: 2, BB1: 3, BC1: 4}
PER_STEP = NP // CH
OUTS = CH
PER_TRIP = 2 * NP + OUTS


def mixer(nc, m, io):
    with ExitStack() as ctx:
        def sb(name, shape, dt=F32):
            return ctx.enter_context(nc.sbuf_tensor(name, shape, dt))

        L = [sb(f"L{h}", [128, B, 128]) for h in range(2)]
        BT = [sb(f"BT{h}", [128, B, 128]) for h in range(2)]
        dtx, dtx2, y, tmp, S, Sdl = (sb(n, [128, B, 2, P]) for n in ("dtx", "dtx2", "y", "tmp", "S", "Sdl"))
        sq = tmp
        wsp = [[sb(f"w_{part}{i}", [128, KD, 128], F32R) for part in ("hi", "lo")] for i in range(2)]
        ss = sb("ss", [128, B, 2])
        rs = sb("rs", [128, B, 2])
        tabp = [sb(f"tabp{u}", [128, 4, TILES, 2]) for u in range(2)]
        hot = [sb(f"hot{u}", [96, 2, 2, 128], BF16) for u in range(2)]
        piece = [ctx.enter_context(nc.psum_tensor(f"piece{i}", [128, 2, 512], F32)) for i in range(2)]
        bank = [ctx.enter_context(nc.psum_tensor(f"scan{i}", [128, 512], F32)) for i in range(4)]
        s = sems(nc, ctx, "w_loaded0", "w_loaded1", "wo_loaded", "piece_ready", "piece_read0", "piece_read1", "tap_done", "conv_chain",
                 "piece_final", "pair_tabs", "diff_ready", "exp_done", "scores_ready", "masked_done", "xT_ready",
                 "dtx_done", "dtx2_done", "BT_ready", "BT_done", "intra_ready", "inter_ready", "inter_read",
                 "y_done", "sadd_ready", "sdl_done", "S_done", "sq_done", "ss_done", "eps_done", "rs_done",
                 "ysc_done", "yT_ready", "yn_done", "w_hi_done", "w_lo_done")
        w_loaded = [s.w_loaded0, s.w_loaded1]
        piece_read = [s.piece_read0, s.piece_read1]
        block = ctx.enter_context(nc.Block())
        LAST = PAIRS // 2 - 1

        def w_of(u, ch):
            return m.w[u][:, 0:PACK_CONV].rearrange("p (k n) -> p k n", k=KD)[:, :, ch * 128:(ch + 1) * 128]

        def weights_split_after(i, it, u, last=False):
            if i % 2:
                return None
            if i < NP - 2:
                return i // 2 + 1, it, u
            return None if last and u else (0, it + u, 1 - u)

        def weights_of(place, u):
            return w_of(u, PIECES[2 * place][0])

        def tap_w(u, ch, k):
            at = PACK_CONV + CONV_OF[ch] * TAPS + k
            return m.w[u][:, at:at + 1]

        def row4(ap):
            return ap.rearrange("p b h d -> p (b h) d")

        def tab_of(u, kind, c):
            return tabp[u][:, kind, c::CH, :]

        def spread(ap):
            return ap[:, :, :, None].to_broadcast([128, B, 2, P])

        def first_piece(it):
            return NP + it * PER_TRIP

        def pieces_of_step(u, c, more):
            per = PER_STEP if more else 0
            outs = max(c - 1, 0) if u else 0
            at = (NP if u else 0) + per * c + outs
            return [(at + i, c * PER_STEP + i) for i in range(per)], (at + per if u and c > 0 else None)

        def tail_piece(more):
            return NP + (NP + OUTS - 1 if more else OUTS - 1)

        @block.tensor
        def _(pe):
            def proj(splits, n, i, slot, first=False):
                ch, half = PIECES[i]
                if not first:
                    wait(pe, piece_read[slot], n)
                if half == 0:
                    wait(pe, s.w_lo_done, splits + i // 2 + 1)
                w = wsp[i // 2 % 2]
                for b in range(2):
                    at = (2 * half + b) * T
                    for k in range(KD):
                        mm = split_matmul(pe, piece[slot][:, b, :], [v[:, k, :] for v in w], [v[:, k, at:at + T] for v in m.xnT2],
                                          first=(k == 0), last=(k == KD - 1))
                mm.then_inc(s.piece_ready, 1)

            def out_piece(it, n, c, slot):
                wait(pe, piece_read[slot], n)
                wait(pe, s.yn_done, (2 * it + 1) * CH + c + 1)
                wait(pe, s.wo_loaded, 16 * (it + 1))
                for b in range(B):
                    for u in range(2):
                        mm = pe.matmul(piece[slot][:, b // 2, b % 2 * D:(b % 2 + 1) * D], m.ynT[u][:, b, c * 128:(c + 1) * 128],
                                       m.wo[:, u, :], start=(u == 0), stop=(u == 1))
                mm.then_inc(s.piece_ready, 1)

            def uses(it, n):
                return (NP + n) // 2 + it * (PER_TRIP // 2)

            def turn_y(p, u, c):
                wait(pe, s.ysc_done, p * CH + c + 1)
                for b in range(B):
                    mm = pe.transpose(bank[3][:, b * 128:(b + 1) * 128],
                                      y[:, b, :, :].rearrange("p h d -> p (h d)"), m.ident[:, :])
                mm.then_inc(s.yT_ready, 1)

            def step(it, p, u, c, more):
                buf = m.conv[u]
                todo, out = pieces_of_step(u, c, more)
                if c == 0:
                    wait(pe, s.pair_tabs, 2 * (p + 1))
                for h in range(2):
                    if h == 0:
                        wait(pe, s.y_done, p * CH + c)
                    elif c == 1:
                        wait(pe, s.BT_done, p * 2 * (CH - 1) + 1)
                    else:
                        wait(pe, s.inter_read, p * (CH - 1) + max(c - 1, 0))
                    for b in range(B):
                        q = slice(b * T + c * 128, b * T + (c + 1) * 128)
                        o = bank[h][:, b * 128:(b + 1) * 128]
                        pe.matmul(o, m.cs[:, q], hot[u][:, 1, h, :], start=True, stop=False)
                        pe.matmul(o, hot[u][:, 0, h, :], m.cs[:, q], start=False, stop=False)
                        mm = pe.matmul(o, m.identb[:, :], m.maskb[:, 0, :], start=False, stop=True)
                    mm.then_inc(s.diff_ready, 1)
                for h in range(2):
                    if c == 0:
                        wait(pe, s.piece_final, p * NC + 4 * (h + 1))
                    if h == 0:
                        wait(pe, s.S_done, p * (CH - 1) + c)
                    else:
                        wait(pe, s.yn_done, p * CH + max(c - 1, 0))
                        if c == 1:
                            wait(pe, s.masked_done, (p * CH + c) * 2)
                    for b in range(B):
                        q = slice(c * 128, (c + 1) * 128)
                        mm = pe.matmul(bank[2 + h][:, b * 128:(b + 1) * 128], buf[BB0 + 2 * h][:, b, q],
                                       buf[BC0 + 2 * h][:, b, q], start=True, stop=True)
                    mm.then_inc(s.scores_ready, 1)
                for n, i in todo[0:1]:
                    proj(NP // 2 * (p + 1), uses(it, n), i, n % 2)
                if c == 0:
                    wait(pe, s.piece_final, p * NC + 10)
                wait(pe, s.exp_done, (p * CH + c) * 2 + 1)
                for b in range(B):
                    mm = pe.transpose(bank[0][:, b * 128:(b + 1) * 128], buf[BX][:, b, c * 128:(c + 1) * 128], m.ident[:, :])
                mm.then_inc(s.xT_ready, 1)
                if c < CH - 1:
                    for h in range(2):
                        if h == 0:
                            wait(pe, s.exp_done, (p * CH + c) * 2 + 2)
                        else:
                            wait(pe, s.masked_done, (p * CH + c) * 2 + 1)
                        for b in range(B):
                            mm = pe.transpose(bank[1 + h][:, b * 128:(b + 1) * 128],
                                              buf[BB0 + 2 * h][:, b, c * 128:(c + 1) * 128], m.ident[:, :])
                        mm.then_inc(s.BT_ready, 1)
                if c > 0:
                    wait(pe, s.masked_done, (p * CH + c) * 2 + 2)
                    turn_y(p, u, c - 1)
                for n, i in todo[1:2]:
                    proj(NP // 2 * (p + 1), uses(it, n), i, n % 2)
                wait(pe, s.masked_done, (p * CH + c) * 2 + 2)
                wait(pe, s.dtx_done, p * CH + c + 1)
                for b in range(B):
                    for h in range(2):
                        at = (b * 2 + h) * P
                        mm = pe.matmul(bank[0][:, at:at + P], L[h][:, b, :], dtx[:, b, h, :], start=True, stop=True)
                mm.then_inc(s.intra_ready, 1)
                if c > 0:
                    wait(pe, s.S_done, p * (CH - 1) + c)
                    if c < CH - 1:
                        wait(pe, s.BT_done, (p * (CH - 1) + c) * 2 + 1)
                    else:
                        wait(pe, s.exp_done, (p * CH + c) * 2 + 2)
                    for b in range(B):
                        for h in range(2):
                            at = (b * 2 + h) * P
                            mm = pe.matmul(bank[1][:, at:at + P], buf[BC0 + 2 * h][:, b, c * 128:(c + 1) * 128],
                                           S[:, b, h, :], start=True, stop=True)
                    mm.then_inc(s.inter_ready, 1)
                if c < CH - 1:
                    wait(pe, s.BT_done, (p * (CH - 1) + c) * 2 + 2)
                    wait(pe, s.dtx2_done, p * (CH - 1) + c + 1)
                    for b in range(B):
                        for h in range(2):
                            at = (b * 2 + h) * P
                            mm = pe.matmul(bank[2][:, at:at + P], BT[h][:, b, :], dtx2[:, b, h, :], start=True, stop=True)
                    mm.then_inc(s.sadd_ready, 1)
                for n, i in todo[2:]:
                    proj(NP // 2 * (p + 1), uses(it, n), i, n % 2)
                if out is not None:
                    out_piece(it, uses(it, out), c - 1, out % 2)

            def trip(it, last=False):
                for u in range(2):
                    p = 2 * it + u
                    more = not (last and u)
                    for c in range(CH):
                        step(it, p, u, c, more)
                    turn_y(p, u, CH - 1)
                    if u:
                        n = tail_piece(more)
                        out_piece(it, uses(it, n), CH - 1, n % 2)

            for i in range(NP):
                proj(0, i // 2, i, i % 2, first=i < 2)
            trip(0)
            with pe.Fori(1, LAST) as it:
                trip(it)
            trip(LAST, last=True)

        @block.scalar
        def _(act):
            def high(todo, ready=0):
                if todo is not None:
                    place, it, u = todo
                    wait(act, s.piece_ready, ready)
                    wait(act, w_loaded[u], 16 * (it + 1))
                    act.activation(wsp[place % 2][0][:, :, :], weights_of(place, u), ACT.Copy).then_inc(s.w_hi_done, 1)

            def tap(u, n, i, slot):
                ch, half = PIECES[i]
                if ch == BZ:
                    return
                wait(act, s.piece_ready, n + 1)
                act.activation(m.conv[u][ch][:, 2 * half:2 * half + 2, :], piece[slot][:, :, :], ACT.Copy,
                               scale=tap_w(u, ch, TAPS - 1)).then_inc(s.tap_done, 1)

            def fin(u, n, i, slot, uses):
                ch, half = PIECES[i]
                dst = m.conv[u][ch][:, 2 * half:2 * half + 2, :]
                if ch == BZ:
                    wait(act, s.piece_ready, n + 1)
                    act.activation(dst, piece[slot][:, :, :], ACT.Silu).then_inc(piece_read[slot], 1)
                else:
                    wait(act, piece_read[slot], uses + 1)
                    act.activation(dst, dst, ACT.Silu).then_inc(s.piece_final, 1)

            def step(it, p, u, c, more, last):
                todo, _ = pieces_of_step(u, c, more)
                for h in range(2):
                    wait(act, s.diff_ready, (p * CH + c) * 2 + h + 1)
                    act.activation(L[h][:, :, :].rearrange("p b q -> p (b q)"), bank[h][:, :], ACT.Exp).then_inc(s.exp_done, 1)

                def args(k):
                    n, i = todo[k]
                    return first_piece(it) + n, i, n % 2, (NP + n) // 2 + it * (PER_TRIP // 2)

                if more:
                    n, i, slot, uses = args(0)
                    tap(1 - u, n, i, slot)
                    high(weights_split_after(i, it + u, 1 - u, last), n + 1)
                if c < CH - 1:
                    for h in range(2):
                        wait(act, s.BT_ready, (p * (CH - 1) + c) * 2 + h + 1)
                        act.activation(BT[h][:, :, :].rearrange("p b q -> p (b q)"), bank[1 + h][:, :], ACT.Copy)\
                            .then_inc(s.BT_done, 1)
                for k in (1, 2):
                    if more:
                        n, i, slot, uses = args(k)
                        tap(1 - u, n, i, slot)
                        high(weights_split_after(i, it + u, 1 - u, last), n + 1)
                        n, i, slot, uses = args(k - 1)
                        fin(1 - u, n, i, slot, uses)
                wait(act, s.y_done, p * CH + c + 1)
                act.activation(sq[:, :, :, :], y[:, :, :, :], ACT.Square).then_inc(s.sq_done, 1)
                if more:
                    n, i, slot, uses = args(2)
                    fin(1 - u, n, i, slot, uses)

            def trip(it, last=False):
                for u in range(2):
                    for c in range(CH):
                        step(it, 2 * it + u, u, c, not (last and u), last)

            high((0, 0, 0))
            for i in range(NP + 1):
                if i < NP:
                    tap(0, i, i, i % 2)
                    high(weights_split_after(i, 0, 0), i + 1)
                if i > 0:
                    fin(0, i - 1, i - 1, (i - 1) % 2, (i - 1) // 2)
            trip(0)
            with act.Fori(1, LAST) as it:
                trip(it)
            trip(LAST, last=True)

        @block.vector
        def _(dve):
            def conv(u, i, slot, j):
                ch, half = PIECES[i]
                if ch == BZ:
                    return
                wait(dve, s.tap_done, j + 1)
                for k in range(1, TAPS):
                    dst = m.conv[u][ch][:, 2 * half:2 * half + 2, k:T]
                    if k > 1:
                        wait(dve, s.conv_chain, 2 * j + k - 1)
                    dve.scalar_tensor_tensor(dst, piece[slot][:, :, 0:T - k], tap_w(u, ch, TAPS - 1 - k), dst,
                                             ALU.mult, ALU.add)\
                        .then_inc(s.conv_chain if k < TAPS - 1 else piece_read[slot], 1)

            def low(todo):
                if todo is not None:
                    place, it, u = todo
                    high, low = wsp[place % 2]
                    wait(dve, s.w_hi_done, NP // 2 * (2 * it + u) + place + 1)
                    dve.tensor_tensor(low[:, :, :], weights_of(place, u), high[:, :, :].bitcast(F32), ALU.subtract)\
                        .then_inc(s.w_lo_done, 1)

            def add_out(n, c, slot):
                wait(dve, s.piece_ready, n + 1)
                for b2 in range(2):
                    a = m.acc[:, (2 * b2) * CH + c:(2 * b2 + 1) * CH + c + 1:CH, :]
                    i = dve.tensor_tensor(a, a, piece[slot][:, b2, :].rearrange("p (b d) -> p b d", b=2), ALU.add)
                i.then_inc(piece_read[slot], 1)

            def norm_y(p, u, c):
                wait(dve, s.yT_ready, p * CH + c + 1)
                dve.tensor_tensor(m.ynT[u][:, :, c * 128:(c + 1) * 128], bank[3][:, :].rearrange("p (b q) -> p b q", b=B),
                                  m.conv[u][BZ][:, :, c * 128:(c + 1) * 128], ALU.mult).then_inc(s.yn_done, 1)

            def step(it, p, u, c, more, last):
                todo, out = pieces_of_step(u, c, more)
                bk = [b[:, :].rearrange("p (b h d) -> p b h d", h=2, d=P) for b in bank]
                for h in range(2):
                    wait(dve, s.exp_done, (p * CH + c) * 2 + h + 1)
                    wait(dve, s.scores_ready, (p * CH + c) * 2 + h + 1)
                    flat = L[h][:, :, :].rearrange("p b q -> p (b q)")
                    dve.tensor_tensor(flat, bank[2 + h][:, :], flat, ALU.mult).then_inc(s.masked_done, 1)
                wait(dve, s.xT_ready, p * CH + c + 1)
                if c == 0:
                    wait(dve, s.pair_tabs, 2 * (p + 1))
                wait(dve, s.dtx2_done, p * (CH - 1) + c)
                dve.tensor_tensor(dtx[:, :, :, :], bk[0], spread(tab_of(u, 0, c)), ALU.mult).then_inc(s.dtx_done, 1)
                for n, i in todo[0:1]:
                    conv(1 - u, i, n % 2, (p + 1) * NC + i)
                    low(weights_split_after(i, it + u, 1 - u, last))
                if c > 0:
                    norm_y(p, u, c - 1)
                for n, i in todo[1:2]:
                    conv(1 - u, i, n % 2, (p + 1) * NC + i)
                    low(weights_split_after(i, it + u, 1 - u, last))
                if c > 0:
                    wait(dve, s.inter_ready, p * (CH - 1) + c)
                    wait(dve, s.ss_done, p * CH + c)
                    dve.tensor_tensor(tmp[:, :, :, :], bk[1], spread(tab_of(u, 1, c)), ALU.mult).then_inc(s.inter_read, 1)
                    wait(dve, s.intra_ready, p * CH + c + 1)
                    wait(dve, s.inter_read, p * (CH - 1) + c)
                    dve.tensor_tensor(row4(y[:, :, :, :]), row4(bk[0]), row4(tmp[:, :, :, :]), ALU.add).then_inc(s.y_done, 1)
                else:
                    wait(dve, s.intra_ready, p * CH + c + 1)
                    dve.tensor_copy(row4(y[:, :, :, :]), row4(bk[0])).then_inc(s.y_done, 1)
                if c < CH - 1:
                    wait(dve, s.sadd_ready, p * (CH - 1) + c + 1)
                    if c > 0:
                        wait(dve, s.sdl_done, p * (CH - 2) + c)
                        dve.tensor_tensor(row4(S[:, :, :, :]), row4(bk[2]), row4(Sdl[:, :, :, :]), ALU.add).then_inc(s.S_done, 1)
                    else:
                        dve.tensor_copy(row4(S[:, :, :, :]), row4(bk[2])).then_inc(s.S_done, 1)
                for n, i in todo[2:3]:
                    conv(1 - u, i, n % 2, (p + 1) * NC + i)
                    low(weights_split_after(i, it + u, 1 - u, last))
                wait(dve, s.sq_done, p * CH + c + 1)
                dve.tensor_reduce(ss[:, :, :], sq[:, :, :, :], AX, ALU.add).then_inc(s.ss_done, 1)
                if out is not None:
                    add_out(first_piece(it) + out, c - 1, out % 2)

            def trip(it, last=False):
                for u in range(2):
                    p = 2 * it + u
                    more = not (last and u)
                    for c in range(CH):
                        step(it, p, u, c, more, last)
                    norm_y(p, u, CH - 1)
                    if u:
                        n = tail_piece(more)
                        add_out(first_piece(it) + n, CH - 1, n % 2)

            low((0, 0, 0))
            for i in range(NP):
                conv(0, i, i % 2, i)
                low(weights_split_after(i, 0, 0))
            trip(0)
            with dve.Fori(1, LAST) as it:
                trip(it)
            trip(LAST, last=True)

        @block.gpsimd
        def _(pool):
            def tabs(p, u, head):
                pool.tensor_copy(tabp[u][:, :, :, :].rearrange("p k t h -> p (k t) h"),
                                 m.tab[:, :, :, bass.ds(head, 2)].rearrange("p k t h -> p (k t) h")).then_inc(s.pair_tabs, 1)
                pool.tensor_copy(hot[u][:, :, :, :], m.onehot[:, :, bass.ds(head, 2)][:, :, :, None].to_broadcast([96, 2, 2, 128]))\
                    .then_inc(s.pair_tabs, 1)

            def step(p, u, c):
                if c < CH - 1:
                    wait(pool, s.dtx_done, p * CH + c + 1)
                    pool.tensor_tensor(dtx2[:, :, :, :], dtx[:, :, :, :], spread(tab_of(u, 2, c)), ALU.mult)\
                        .then_inc(s.dtx2_done, 1)
                if 0 < c < CH - 1:
                    wait(pool, s.S_done, p * (CH - 1) + c)
                    pool.tensor_tensor(Sdl[:, :, :, :], S[:, :, :, :], spread(tab_of(u, 3, c)), ALU.mult)\
                        .then_inc(s.sdl_done, 1)
                e = (p * CH + c) * 2
                wait(pool, s.ss_done, p * CH + c + 1)
                pool.tensor_tensor(rs[:, :, :], ss[:, :, :], m.inv_P[:, :].rearrange("p (b h) -> p b h", b=B), ALU.mult).then_inc(s.eps_done, 1)
                wait(pool, s.eps_done, e + 1)
                pool.tensor_tensor(rs[:, :, :], rs[:, :, :], m.eps6[:, :].rearrange("p (b h) -> p b h", b=B), ALU.add).then_inc(s.eps_done, 1)
                wait(pool, s.eps_done, e + 2)
                pool.tensor_tensor(rs[:, :, :], rs[:, :, :], m.minus_half[:, 0:8].rearrange("p (b h) -> p b h", b=B), ALU.pow).then_inc(s.rs_done, 1)
                wait(pool, s.rs_done, p * CH + c + 1)
                pool.tensor_tensor(y[:, :, :, :], y[:, :, :, :], spread(rs[:, :, :]), ALU.mult).then_inc(s.ysc_done, 1)

            def trip(it, last=False):
                for u in range(2):
                    p = 2 * it + u
                    for c in range(CH):
                        step(p, u, c)
                        if c == 1 and not (last and u):
                            tabs(p + 1, 1 - u, 4 * it + 2 * (u + 1))

            for old in m.old_sems:
                pool.sem_clear(old)
            tabs(0, 0, 0)
            trip(0)
            with pool.Fori(1, LAST) as it:
                trip(it)
            trip(LAST, last=True)

        @block.sync
        def _(sp):
            def load_out(p):
                sp.dma_start(m.wo[:, :, :], io.w_out[p:p + 2].rearrange("u p n -> p u n")).then_inc(s.wo_loaded, 16)

            for u in range(2):
                sp.dma_start(m.w[u][:, :], io.w_pack[u]).then_inc(w_loaded[u], 16)
            load_out(0)
            for it in range(LAST):
                for u in range(2):
                    sp.wait_ge(s.piece_ready, it * PER_TRIP + NP * (u + 1))
                    sp.wait_ge(s.piece_final, (2 * it + u + 1) * NC)
                    sp.dma_start(m.w[u][:, :], io.w_pack[2 * it + 2 + u]).then_inc(w_loaded[u], 16)
                sp.wait_ge(s.piece_ready, first_piece(it + 1))
                load_out(2 * it + 2)
            for u in range(2):
                sp.wait_ge(w_loaded[u], 16 * (LAST + 1))


def thought(nc, m, io):
    w = m.thought_w
    agg, d1, d2, bcw = w["agg"], w["d1"], w["d2"], w["bc"]
    rows, d1b = w["rows"], w["d1b"]
    HT = HID // 128
    with ExitStack() as ctx:
        def sb(name, shape):
            return ctx.enter_context(nc.sbuf_tensor(name, shape, F32))

        x4, normed, state = (sb(f"th_{n}", [4, D]) for n in ("x4", "normed", "state"))
        stats, mv, rstd = sb("th_st", [4, 6]), sb("th_mv", [4, 2]), sb("th_rs", [4, 1])
        xT, hT = sb("th_xT", [128, KD, B]), sb("th_hT", [128, HT, B])
        bcb = sb("th_bcb", [128, KD])
        ps_row, ps_T, ps_h = (ctx.enter_context(nc.psum_tensor(f"th_{n}", [128, 512], F32)) for n in ("row", "T", "h"))
        s = sems(nc, ctx, "th_loaded", "th_row_ready", "th_state", "th_stats", "th_aggr", "th_eps", "th_rstd", "th_hat",
                 "th_scaled", "th_normed", "th_turned", "th_T", "th_h_ready", "th_h_biased", "th_gelu", "th_added",
                 "th_bc_ready", "th_bc_done", "th_xn_hi", "th_xn_lo")
        block = ctx.enter_context(nc.Block())
        LNS = K_STEPS + 1
        LOADS = 12

        @block.sync
        def _(sp):
            for i, v in enumerate((io.in_gamma, io.in_beta, io.agg_b, io.pn_gamma, io.pn_beta, io.d2_b)):
                sp.dma_start(rows[0:B, i, :], v.partition_broadcast(B)).then_inc(s.th_loaded, 16)
            sp.dma_start(agg, io.agg_w.rearrange("(k p) n -> p k n", p=128)).then_inc(s.th_loaded, 16)
            sp.dma_start(d1, io.d1_w.rearrange("(k p) n -> p k n", p=128)).then_inc(s.th_loaded, 16)
            sp.dma_start(d2, io.d2_w.rearrange("(k p) n -> p k n", p=128)).then_inc(s.th_loaded, 16)
            sp.dma_start(bcw, io.bc_w.rearrange("(k p) n -> p k n", p=128)).then_inc(s.th_loaded, 16)
            sp.dma_start(d1b, io.d1_b).then_inc(s.th_loaded, 16)
            sp.dma_start(bcb[:, :], io.bc_b).then_inc(s.th_loaded, 16)

        @block.tensor
        def _(pe):
            def turn(n, src):
                for k in range(KD):
                    mm = pe.transpose(ps_T[:, k * B:(k + 1) * B], src[:, k * 128:(k + 1) * 128], m.ident[0:B, 0:B])
                mm.then_inc(s.th_turned, 1)

            for k in range(KD):
                mm = pe.matmul(ps_row[0:B, k * 128:(k + 1) * 128], m.xnT[:, k, T - 1::T], m.ident[:, :], start=True, stop=True)
            mm.then_inc(s.th_row_ready, 1)
            pe.wait_ge(s.th_loaded, 16 * LOADS)
            for n in range(LNS):
                pe.wait_ge(s.th_normed, n + 1)
                turn(n, normed)
                pe.wait_ge(s.th_T, n + 1)
                if n == 0:
                    for k in range(KD):
                        mm = pe.matmul(ps_row[0:B, 0:D], xT[:, k, :], agg[:, k, :], start=(k == 0), stop=(k == KD - 1))
                    mm.then_inc(s.th_row_ready, 1)
                    continue
                for j in range(HT):
                    for k in range(KD):
                        mm = pe.matmul(ps_h[:, j * B:(j + 1) * B], d1[:, k, j * 128:(j + 1) * 128], xT[:, k, :],
                                       start=(k == 0), stop=(k == KD - 1))
                mm.then_inc(s.th_h_ready, 1)
                pe.wait_ge(s.th_gelu, n)
                for j in range(HT):
                    mm = pe.matmul(ps_row[0:B, 0:D], hT[:, j, :], d2[:, j, :], start=(j == 0), stop=(j == HT - 1))
                mm.then_inc(s.th_row_ready, 1)
            pe.wait_ge(s.th_state, LNS)
            turn(LNS, state)
            pe.wait_ge(s.th_T, LNS + 1)
            for j in range(KD):
                for k in range(KD):
                    mm = pe.matmul(ps_h[:, j * B:(j + 1) * B], bcw[:, k, j * 128:(j + 1) * 128], xT[:, k, :],
                                   start=(k == 0), stop=(k == KD - 1))
            mm.then_inc(s.th_bc_ready, 1)

        @block.vector
        def _(dve):
            def layer_norm(n, src, gamma, beta):
                dve.bn_stats(stats[:, :], src[:, :]).then_inc(s.th_stats, 1)
                dve.wait_ge(s.th_stats, n + 1)
                dve.bn_aggr(mv[:, :], stats[:, :]).then_inc(s.th_aggr, 1)
                dve.wait_ge(s.th_rstd, n + 1)
                dve.tensor_scalar(normed[:, :], src[:, :], mv[:, 0:1], rstd[:, 0:1], ALU.subtract, ALU.mult).then_inc(s.th_hat, 1)
                dve.wait_ge(s.th_hat, n + 1)
                dve.tensor_tensor(normed[:, :], normed[:, :], rows[0:B, gamma, :], ALU.mult).then_inc(s.th_scaled, 1)
                dve.wait_ge(s.th_scaled, n + 1)
                dve.tensor_tensor(normed[:, :], normed[:, :], rows[0:B, beta, :], ALU.add).then_inc(s.th_normed, 1)

            dve.wait_ge(s.th_loaded, 16 * LOADS)
            dve.wait_ge(s.th_row_ready, 1)
            dve.tensor_copy(x4[:, :], ps_row[0:B, 0:D]).then_inc(s.th_added, 1)
            dve.wait_ge(s.th_added, 1)
            for n in range(LNS):
                layer_norm(n, x4 if n == 0 else state, 0 if n == 0 else 3, 1 if n == 0 else 4)
                dve.wait_ge(s.th_turned, n + 1)
                dve.tensor_copy(xT[:, :, :].rearrange("p k b -> p (k b)"), ps_T[:, 0:KD * B]).then_inc(s.th_T, 1)
                if n == 0:
                    dve.wait_ge(s.th_row_ready, 2)
                    dve.tensor_tensor(state[:, :], ps_row[0:B, 0:D], rows[0:B, 2, :], ALU.add).then_inc(s.th_state, 1)
                    dve.wait_ge(s.th_state, 1)
                    continue
                dve.wait_ge(s.th_h_ready, n)
                dve.tensor_tensor(hT[:, :, :], ps_h[:, 0:HT * B].rearrange("p (j b) -> p j b", b=B),
                                  d1b[:, :, None].to_broadcast([128, HT, B]), ALU.add).then_inc(s.th_h_biased, 1)
                dve.wait_ge(s.th_row_ready, n + 2)
                dve.tensor_tensor(state[:, :], ps_row[0:B, 0:D], state[:, :], ALU.add).then_inc(s.th_added, 1)
                dve.wait_ge(s.th_added, n + 1)
                dve.tensor_tensor(state[:, :], state[:, :], rows[0:B, 5, :], ALU.add).then_inc(s.th_state, 1)
                dve.wait_ge(s.th_state, n + 1)
            dve.wait_ge(s.th_turned, LNS + 1)
            dve.tensor_copy(xT[:, :, :].rearrange("p k b -> p (k b)"), ps_T[:, 0:KD * B]).then_inc(s.th_T, 1)
            dve.wait_ge(s.th_bc_ready, 1)
            dve.tensor_tensor(m.bcT[:, :, :], ps_h[:, 0:KD * B].rearrange("p (k b) -> p k b", b=B),
                              bcb[:, :, None].to_broadcast([128, KD, B]), ALU.add).then_inc(s.th_bc_done, 1)

        @block.gpsimd
        def _(pool):
            def low(q):
                at = slice(q * T, (q + 1) * T)
                pool.wait_ge(s.th_xn_hi, q + 1)
                pool.tensor_tensor(m.xnT2[1][:, :, at], m.xnT[:, :, at], m.xnT2[0][:, :, at].bitcast(F32), ALU.subtract)\
                    .then_inc(s.th_xn_lo, 1)

            for n in range(LNS):
                if n:
                    low(n - 1)
                pool.wait_ge(s.th_aggr, n + 1)
                rsqrt_small(pool, rstd[:, :], mv[:, 1:2], 1.0, 1e-6, m.minus_half[0:B, 0:1], s.th_eps, n).then_inc(s.th_rstd, 1)

        @block.scalar
        def _(act):
            for q in range(B):
                at = slice(q * T, (q + 1) * T)
                act.activation(m.xnT2[0][:, :, at], m.xnT[:, :, at], ACT.Copy).then_inc(s.th_xn_hi, 1)
            for n in range(1, LNS):
                act.wait_ge(s.th_h_biased, n)
                act.activation(hT[:, :, :], hT[:, :, :], ACT.Gelu).then_inc(s.th_gelu, 1)


def middle(nc, m, io):
    with ExitStack() as ctx:
        def sb(name, shape, dt=F32):
            return ctx.enter_context(nc.sbuf_tensor(name, shape, dt))

        x = sb("mi_x", [128, TILES, D])
        spread = sb("mi_spread", [128, B, KD, 128])
        half_bc = sb("mi_half_bc", [128, B, D])
        gate_w, gate_b = sb("mi_gw", [128, KD, D]), sb("mi_gb", [128, D])
        out_g, out_b = sb("mi_og", [128, D]), sb("mi_ob", [128, D])
        down_w = sb("mi_dw", [128, KD, DOWN])
        ew = sb("mi_ew", [128, E, KD, D])
        eb = sb("mi_eb", [E, D])
        norm_w = sb("mi_nw", [128, QR + KVR])
        kcos, ksin = sb("mi_cos", [128, CH, ROPE]), sb("mi_sin", [128, CH, ROPE])
        before = sb("mi_before", [128, E, E])
        inv = sb("mi_inv", [128, 2])
        eps = sb("mi_eps", [128, 2])
        xn0, out, hat, xn1 = (sb(f"mi_{n}", [128, D]) for n in ("xn0", "out", "hat", "xn1"))
        th, sg = sb("mi_th", [128, D]), sb("mi_sg", [128, D])
        x1, idle = sb("mi_x1", [128, D]), sb("mi_idle", [128, 1])
        T0, T1 = sb("mi_T0", [128, KD, 128]), sb("mi_T1", [128, KD, 128])
        st, mv, rs = sb("mi_st", [128, 6]), sb("mi_mv", [128, 2]), sb("mi_rs", [128, 1])
        st1, mv1, rs1 = sb("mi_st1", [128, 6]), sb("mi_mv1", [128, 2]), sb("mi_rs1", [128, 1])
        dn, sqd, ssd, rsd = sb("mi_dn", [128, DOWN]), sb("mi_sqd", [128, QR]), sb("mi_ssd", [128, 2]), sb("mi_rsd", [128, 2])
        gt, eq = sb("mi_gt", [128, E, E]), sb("mi_eq", [128, E, E])
        rank, sel, sl, hsum, garg, gates = (sb(f"mi_{n}", [128, E]) for n in ("rank", "sel", "sl", "hsum", "garg", "gates"))
        qn, kcat = sb("mi_qn", [128, QR]), sb("mi_kcat", [128, KVR + ROPE + KVR])
        kr = sb("mi_kr", [128, ROPE])
        gT = sb("mi_gT", [E, 128])
        moe = sb("mi_moe", [128, D])
        pT, pG, pD, pK = (ctx.enter_context(nc.psum_tensor(f"mi_p{n}", [128, 512], F32)) for n in "TGDK")
        pE = [ctx.enter_context(nc.psum_tensor(f"mi_e{i}", [128, 2, D], F32)) for i in range(4)]
        s = sems(nc, ctx, "mi_loaded", "mi_consts", "mi_xn0", "mi_turned0", "mi_T0", "mi_gate_ready", "mi_gate_biased",
                 "mi_tanh", "mi_gated", "mi_out", "mi_stats", "mi_aggr", "mi_eps", "mi_rstd", "mi_hat", "mi_hat2",
                 "mi_hat3", "mi_silu", "mi_sg", "mi_x1", "mi_stats1", "mi_aggr1", "mi_eps1", "mi_rstd1", "mi_xn1",
                 "mi_turned1", "mi_T1", "mi_down_ready", "mi_dn", "mi_ssd", "mi_rsd_chain", "mi_rsd", "mi_route",
                 "mi_route_arg", "mi_route_tanh", "mi_gates", "mi_kv_done", "mi_qn", "mi_rope", "mi_kcat",
                 "mi_qk_turned", "mi_qk_done", "mi_gates_turned", "mi_gT", "mi_bias_ready", "mi_experts_ready",
                 "mi_expert_added", "mi_moe", "mi_route_arg2", "mi_const", "mi_spread",
                 "mi_bc_ready", "mi_half_bc")
        block = ctx.enter_context(nc.Block())
        NCONST = 3
        LOADS = 14

        def order(stage_a, stage_b, t, has_next, nxt):
            if has_next:
                stage_a(nxt, 1)
            stage_b(t, 1)
            if has_next:
                stage_a(nxt, 2)
            stage_b(t, 2)
            if has_next:
                stage_a(nxt, 3)
            stage_b(t, 3)
            if has_next:
                stage_a(nxt, 4)

        def run(eng, stage_a, stage_b):
            for n in range(1, 5):
                stage_a((0, 0), n)
            for c in range(CH):
                order(stage_a, stage_b, (0, c), True, (0, c + 1))
            with eng.Fori(1, B - 1) as b:
                for c in range(CH):
                    order(stage_a, stage_b, (b, c), True, (b, c + 1))
            for c in range(CH):
                order(stage_a, stage_b, (B - 1, c), c < CH - 1, (B - 1, c + 1))

        def num(t):
            return t[0] * CH + t[1]

        @block.sync
        def _(sp):
            for b in range(B):
                sp.dma_start(x[:, b * CH:(b + 1) * CH, :], io.x[b].rearrange("(c p) d -> p c d", p=128)).then_inc(s.mi_loaded, 16)
            sp.dma_start(gate_w[:, :, :], io.gate_w.rearrange("(k p) n -> p k n", p=128)).then_inc(s.mi_loaded, 16)
            sp.dma_start(gate_b[:, :], io.gate_b.partition_broadcast(128)).then_inc(s.mi_loaded, 16)
            sp.dma_start(out_g[:, :], io.out_gamma.partition_broadcast(128)).then_inc(s.mi_loaded, 16)
            sp.dma_start(out_b[:, :], io.out_beta.partition_broadcast(128)).then_inc(s.mi_loaded, 16)
            sp.dma_start(down_w[:, :, :], io.w_down.rearrange("(k p) n -> p k n", p=128)).then_inc(s.mi_loaded, 16)
            sp.dma_start(norm_w[:, 0:QR], io.q_norm_w.partition_broadcast(128)).then_inc(s.mi_loaded, 16)
            sp.dma_start(norm_w[:, QR:], io.kv_norm_w.partition_broadcast(128)).then_inc(s.mi_loaded, 16)
            sp.dma_start(kcos[:, :, :], io.c_kcos).then_inc(s.mi_loaded, 16)
            sp.dma_start(ksin[:, :, :], io.c_ksin).then_inc(s.mi_loaded, 16)
            sp.dma_start(before[:, :, :], io.c_before).then_inc(s.mi_loaded, 16)
            sp.dma_start(ew[:, :, :, :], io.expert_w.rearrange("e (k p) n -> p e k n", p=128)).then_inc(s.mi_consts, 16)
            sp.dma_start(eb[:, :], io.expert_b).then_inc(s.mi_consts, 16)

        @block.tensor
        def _(pe):
            def a(t, n):
                i = num(t)
                if n == 2:
                    wait(pe, s.mi_xn0, i + 1)
                    for k in range(KD):
                        mm = pe.transpose(pT[:, k * 128:(k + 1) * 128], xn0[:, k * 128:(k + 1) * 128], m.ident[:, :])
                    mm.then_inc(s.mi_turned0, 1)
                    wait(pe, s.mi_T0, i + 1)
                    for k in range(KD):
                        mm = pe.matmul(pG[:, 0:D], T0[:, k, :], gate_w[:, k, :], start=(k == 0), stop=(k == KD - 1))
                    mm.then_inc(s.mi_gate_ready, 1)

            def b(t, n):
                i = num(t)
                if n == 1:
                    wait(pe, s.mi_xn1, i + 1)
                    for k in range(KD):
                        mm = pe.transpose(pT[:, 256 + k * 128:256 + (k + 1) * 128], xn1[:, k * 128:(k + 1) * 128], m.ident[:, :])
                    mm.then_inc(s.mi_turned1, 1)
                    wait(pe, s.mi_T1, i + 1)
                    for k in range(KD):
                        mm = pe.matmul(pD[:, 0:DOWN], T1[:, k, :], down_w[:, k, :], start=(k == 0), stop=(k == KD - 1))
                    mm.then_inc(s.mi_down_ready, 1)
                    wait(pe, s.mi_expert_added, i * E)
                    for e in range(E):
                        for k in range(KD):
                            mm = pe.matmul(pE[e // 2][:, e % 2, :], T1[:, k, :], ew[:, e, k, :], start=(k == 0), stop=(k == KD - 1))
                    mm.then_inc(s.mi_experts_ready, 1)
                if n == 2:
                    wait(pe, s.mi_gates, i + 1)
                    wait(pe, s.mi_moe, i)
                    pe.transpose(pK[0:E, 384:512], gates[:, :], m.ident[:, :]).then_inc(s.mi_gates_turned, 1)
                    wait(pe, s.mi_qn, i + 1)
                    wait(pe, s.mi_kcat, i + 1)
                    wait(pe, s.mi_gT, i + 1)
                    pe.transpose(pK[:, 0:128], qn[:, :], m.ident[:, :])
                    pe.transpose(pK[:, 128:256], kcat[:, 0:128], m.ident[:, :])
                    pe.transpose(pK[:, 256:384], kcat[:, ROPE:ROPE + 128], m.ident[:, :]).then_inc(s.mi_qk_turned, 1)
                    pe.matmul(pG[:, 256:512], gT[:, :], eb[:, :], start=True, stop=True).then_inc(s.mi_bias_ready, 1)

            wait(pe, s.mi_loaded, 16 * LOADS)
            wait(pe, s.mi_consts, 32)
            wait(pe, s.mi_spread, KD)
            for row in range(B):
                for k in range(KD):
                    mm = pe.transpose(pE[row // 2][:, row % 2, k * 128:(k + 1) * 128], spread[:, row, k, :], m.ident[:, :])
            mm.then_inc(s.mi_bc_ready, 1)
            wait(pe, s.mi_half_bc, 2)
            run(pe, a, b)

        @block.scalar
        def _(act):
            def a(t, n):
                i = num(t)
                if n == 2:
                    wait(act, s.mi_turned0, i + 1)
                    act.activation(T0[:, :, :].rearrange("p k n -> p (k n)"), pT[:, 0:256], ACT.Copy).then_inc(s.mi_T0, 1)
                    wait(act, s.mi_gate_biased, i + 1)
                    act.activation(th[:, :], th[:, :], ACT.Tanh, scale=0.5).then_inc(s.mi_tanh, 1)
                if n == 3:
                    wait(act, s.mi_hat3, i + 1)
                    act.activation(hat[:, :], hat[:, :], ACT.Silu).then_inc(s.mi_silu, 1)

            def b(t, n):
                i = num(t)
                if n == 1:
                    wait(act, s.mi_turned1, i + 1)
                    act.activation(T1[:, :, :].rearrange("p k n -> p (k n)"), pT[:, 256:512], ACT.Copy).then_inc(s.mi_T1, 1)
                    wait(act, s.mi_down_ready, i + 1)
                    act.activation(dn[:, :], pD[:, 0:DOWN], ACT.Copy).then_inc(s.mi_dn, 1)
                    wait(act, s.mi_dn, i + 1)
                    act.activation(sqd[:, 0:QR], dn[:, 0:QR], ACT.Square, accum_out=ssd[:, 0:1]).then_inc(s.mi_ssd, 1)
                    wait(act, s.mi_ssd, 2 * i + 1)
                    act.activation(sqd[:, 0:KVR], dn[:, QR:QR + KVR], ACT.Square, accum_out=ssd[:, 1:2]).then_inc(s.mi_ssd, 1)
                    wait(act, s.mi_route_arg, i + 1)
                    act.activation(garg[:, :], garg[:, :], ACT.Tanh).then_inc(s.mi_route_tanh, 1)
                if n == 2:
                    wait(act, s.mi_gates_turned, i + 1)
                    act.activation(gT[:, :], pK[0:E, 384:512], ACT.Copy).then_inc(s.mi_gT, 1)

            run(act, a, b)

        @block.vector
        def _(dve):
            def a(t, n):
                i = num(t)
                tile = slice(i, i + 1) if t[0].__class__ is int else bass.ds(i, 1)
                if n == 1:
                    dve.tensor_scalar(xn0[:, :], x[:, tile, :].rearrange("p o d -> p (o d)"), m.mean[:, tile], m.rstd[:, tile],
                                      ALU.subtract, ALU.mult).then_inc(s.mi_xn0, 1)
                if n == 2:
                    row = slice(t[0], t[0] + 1) if t[0].__class__ is int else bass.ds(t[0], 1)
                    wait(dve, s.mi_gate_ready, i + 1)
                    dve.tensor_tensor(th[:, :], pG[:, 0:D], gate_b[:, :], ALU.add).then_inc(s.mi_gate_biased, 1)
                    wait(dve, s.mi_tanh, i + 1)
                    if t[1] == CH:
                        row = slice(t[0] + 1, t[0] + 2) if t[0].__class__ is int else bass.ds(t[0] + 1, 1)
                    dve.scalar_tensor_tensor(th[:, :], th[:, :], 1.0, half_bc[:, row, :].rearrange("p o d -> p (o d)"),
                                             ALU.add, ALU.mult).then_inc(s.mi_gated, 1)
                    wait(dve, s.mi_gated, i + 1)
                    dve.tensor_tensor(out[:, :], xn0[:, :], th[:, :], ALU.add).then_inc(s.mi_out, 1)
                    wait(dve, s.mi_out, i + 1)
                    dve.bn_stats(st[:, :], out[:, :]).then_inc(s.mi_stats, 1)
                    wait(dve, s.mi_stats, i + 1)
                    dve.tensor_copy(idle[:, :], m.minus_half[:, 0:1])
                    dve.bn_aggr(mv[:, :], st[:, :]).then_inc(s.mi_aggr, 1)
                if n == 3:
                    wait(dve, s.mi_rstd, i + 1)
                    dve.tensor_scalar(hat[:, :], out[:, :], mv[:, 0:1], rs[:, :], ALU.subtract, ALU.mult).then_inc(s.mi_hat, 1)
                    wait(dve, s.mi_hat, i + 1)
                    dve.tensor_tensor(hat[:, :], hat[:, :], out_g[:, :], ALU.mult).then_inc(s.mi_hat2, 1)
                    wait(dve, s.mi_hat2, i + 1)
                    dve.tensor_tensor(hat[:, :], hat[:, :], out_b[:, :], ALU.add).then_inc(s.mi_hat3, 1)
                    wait(dve, s.mi_silu, i + 1)
                    acc = m.acc[:, tile, :].rearrange("p o d -> p (o d)")
                    dve.tensor_tensor(sg[:, :], acc, hat[:, :], ALU.mult).then_inc(s.mi_sg, 1)
                    wait(dve, s.mi_sg, i + 1)
                    dve.tensor_tensor(x1[:, :], sg[:, :], x[:, tile, :].rearrange("p o d -> p (o d)"), ALU.add).then_inc(s.mi_x1, 1)
                    wait(dve, s.mi_x1, i + 1)
                    dve.bn_stats(st1[:, :], x1[:, :]).then_inc(s.mi_stats1, 1)
                    wait(dve, s.mi_stats1, i + 1)
                    dve.tensor_scalar(acc, x1[:, :], 1.0, None, ALU.mult)
                    dve.bn_aggr(mv1[:, :], st1[:, :]).then_inc(s.mi_aggr1, 1)
                if n == 4:
                    wait(dve, s.mi_rstd1, i + 1)
                    dve.tensor_scalar(xn1[:, :], x1[:, :], mv1[:, 0:1], rs1[:, :], ALU.subtract, ALU.mult).then_inc(s.mi_xn1, 1)

            def b(t, n):
                i = num(t)
                tile = slice(i, i + 1) if t[0].__class__ is int else bass.ds(i, 1)
                lg = dn[:, QR + KVR + 2 * ROPE:DOWN]
                if n == 1:
                    r = i * 8
                    wait(dve, s.mi_dn, i + 1)
                    dve.tensor_tensor(gt[:, :, :], lg[:, None, :].to_broadcast([128, E, E]),
                                      lg[:, :, None].to_broadcast([128, E, E]), ALU.is_gt).then_inc(s.mi_route, 1)
                    dve.tensor_tensor(eq[:, :, :], lg[:, None, :].to_broadcast([128, E, E]),
                                      lg[:, :, None].to_broadcast([128, E, E]), ALU.is_equal).then_inc(s.mi_route, 1)
                    wait(dve, s.mi_route, r + 2)
                    dve.tensor_tensor(eq[:, :, :], eq[:, :, :], before[:, :, :], ALU.mult).then_inc(s.mi_route, 1)
                    wait(dve, s.mi_route, r + 3)
                    dve.tensor_tensor(gt[:, :, :], gt[:, :, :], eq[:, :, :], ALU.add).then_inc(s.mi_route, 1)
                    wait(dve, s.mi_route, r + 4)
                    dve.tensor_reduce(rank[:, :], gt[:, :, :], AX, ALU.add).then_inc(s.mi_route, 1)
                    wait(dve, s.mi_route, r + 5)
                    dve.tensor_scalar(sel[:, :], rank[:, :], TOPK - 0.5, None, ALU.is_lt).then_inc(s.mi_route, 1)
                    wait(dve, s.mi_route, r + 6)
                    dve.tensor_tensor(sl[:, :], sel[:, :], lg, ALU.mult).then_inc(s.mi_route, 1)
                    wait(dve, s.mi_route, r + 7)
                    dve.tensor_reduce(hsum[:, 0:1], sl[:, :], AX, ALU.add).then_inc(s.mi_route, 1)
                    wait(dve, s.mi_route, r + 8)
                    dve.scalar_tensor_tensor(garg[:, :], hsum[:, 0:1].to_broadcast([128, E]), -0.5, lg, ALU.mult, ALU.add)\
                        .then_inc(s.mi_route_arg, 1)
                    wait(dve, s.mi_route_tanh, i + 1)
                    dve.tensor_scalar(garg[:, :], garg[:, :], 0.5, 0.5, ALU.mult, ALU.add).then_inc(s.mi_route_arg2, 1)
                    wait(dve, s.mi_route_arg2, i + 1)
                    dve.tensor_tensor(gates[:, :], garg[:, :], sel[:, :], ALU.mult).then_inc(s.mi_gates, 1)
                if n == 2:
                    wait(dve, s.mi_rsd, i + 1)
                    kv = dn[:, QR:QR + KVR]
                    dve.scalar_tensor_tensor(qn[:, :], dn[:, 0:QR], rsd[:, 0:1], norm_w[:, 0:QR], ALU.mult, ALU.mult).then_inc(s.mi_qn, 1)
                    dve.scalar_tensor_tensor(kcat[:, 0:KVR], kv, rsd[:, 1:2], norm_w[:, QR:], ALU.mult, ALU.mult).then_inc(s.mi_kv_done, 1)
                    dve.scalar_tensor_tensor(kcat[:, KVR + ROPE:], kv, rsd[:, 1:2], norm_w[:, QR:], ALU.mult, ALU.mult).then_inc(s.mi_kv_done, 1)
                    dve.scalar_tensor_tensor(m.kv[:, tile, :].rearrange("p o d -> p (o d)"), kv, rsd[:, 1:2],
                                             norm_w[:, QR:], ALU.mult, ALU.mult).then_inc(s.mi_kv_done, 1)
                    c = t[1]
                    o = QR + KVR
                    dve.tensor_tensor(kr[:, :], dn[:, o:o + ROPE], kcos[:, c, :], ALU.mult).then_inc(s.mi_rope, 1)
                    dve.tensor_tensor(kcat[:, KVR:KVR + ROPE], dn[:, o + ROPE:o + 2 * ROPE], ksin[:, c, :], ALU.mult).then_inc(s.mi_rope, 1)
                    wait(dve, s.mi_rope, 2 * i + 2)
                    wait(dve, s.mi_kv_done, 3 * i + 3)
                    dve.tensor_tensor(kcat[:, KVR:KVR + ROPE], kcat[:, KVR:KVR + ROPE], kr[:, :], ALU.add).then_inc(s.mi_kcat, 1)
                    wait(dve, s.mi_qk_turned, i + 1)
                    dve.tensor_scalar(m.qkT[:, :, bass.ds(i * 128, 128)], pK[:, 0:384].rearrange("p (a n) -> p a n", a=3),
                                      1.0, None, ALU.mult).then_inc(s.mi_qk_done, 1)
                if n == 3:
                    wait(dve, s.mi_experts_ready, i + 1)
                    for e in range(E):
                        src = pE[e // 2][:, e % 2, :]
                        if e == 0:
                            dve.tensor_scalar(moe[:, :], src, gates[:, 0:1], None, ALU.mult).then_inc(s.mi_expert_added, 1)
                        else:
                            wait(dve, s.mi_expert_added, i * E + e)
                            dve.scalar_tensor_tensor(moe[:, :], src, gates[:, e:e + 1], moe[:, :], ALU.mult, ALU.add)\
                                .then_inc(s.mi_expert_added, 1)
                    wait(dve, s.mi_bias_ready, i + 1)
                    wait(dve, s.mi_expert_added, i * E + E)
                    dve.tensor_tensor(m.moe[:, tile, :].rearrange("p o d -> p (o d)"), moe[:, :], pG[:, 256:512], ALU.add)\
                        .then_inc(s.mi_moe, 1)

            for k in range(KD):
                dve.tensor_copy(spread[:, :, k, :], m.bcT[:, k, :, None].to_broadcast([128, B, 128])).then_inc(s.mi_spread, 1)
            wait(dve, s.mi_bc_ready, 1)
            for i in range(2):
                dve.tensor_scalar(half_bc[:, 2 * i:2 * i + 2, :], pE[i][:, :, :], 0.5, None, ALU.mult).then_inc(s.mi_half_bc, 1)
            wait(dve, s.mi_half_bc, 2)
            wait(dve, s.mi_loaded, 16 * LOADS)
            run(dve, a, b)

        @block.gpsimd
        def _(pool):
            def a(t, n):
                i = num(t)
                if n == 2:
                    wait(pool, s.mi_aggr, i + 1)
                    pool.tensor_tensor(rs[:, :], mv[:, 1:2], eps[:, 0:1], ALU.add).then_inc(s.mi_eps, 1)
                    wait(pool, s.mi_eps, i + 1)
                    pool.tensor_tensor(rs[:, :], rs[:, :], m.minus_half[:, 0:1], ALU.pow).then_inc(s.mi_rstd, 1)
                if n == 3:
                    wait(pool, s.mi_aggr1, i + 1)
                    pool.tensor_tensor(rs1[:, :], mv1[:, 1:2], eps[:, 1:2], ALU.add).then_inc(s.mi_eps1, 1)
                    wait(pool, s.mi_eps1, i + 1)
                    pool.tensor_tensor(rs1[:, :], rs1[:, :], m.minus_half[:, 0:1], ALU.pow).then_inc(s.mi_rstd1, 1)

            def b(t, n):
                i = num(t)
                if n == 1:
                    wait(pool, s.mi_ssd, 2 * i + 2)
                    pool.tensor_tensor(rsd[:, :], ssd[:, :], inv[:, :], ALU.mult).then_inc(s.mi_rsd_chain, 1)
                    wait(pool, s.mi_rsd_chain, 2 * i + 1)
                    pool.tensor_tensor(rsd[:, :], rsd[:, :], eps[:, 0:1].to_broadcast([128, 2]), ALU.add).then_inc(s.mi_rsd_chain, 1)
                    wait(pool, s.mi_rsd_chain, 2 * i + 2)
                    pool.tensor_tensor(rsd[:, :], rsd[:, :], m.minus_half[:, 0:2], ALU.pow).then_inc(s.mi_rsd, 1)

            pool.memset(inv[:, 0:1], 1.0 / QR).then_inc(s.mi_const, 1)
            pool.memset(inv[:, 1:2], 1.0 / KVR).then_inc(s.mi_const, 1)
            pool.memset(eps[:, 0:1], 1e-6).then_inc(s.mi_const, 1)
            pool.memset(eps[:, 1:2], 1e-5).then_inc(s.mi_const, 1)
            wait(pool, s.mi_const, 4)
            run(pool, a, b)


def split_matmul(pe, out, w, x, first=True, last=True):
    pe.matmul(out, w[0], x[0], start=first, stop=False)
    pe.matmul(out, w[0], x[1], start=False, stop=False)
    return pe.matmul(out, w[1], x[0], start=False, stop=last)


def attention(nc, m, io):
    SCALE = 1.0 / float(np.sqrt(NOPE + ROPE))
    UNITS = AH * CH
    with ExitStack() as ctx:
        def sb(name, shape, dt=F32):
            return ctx.enter_context(nc.sbuf_tensor(name, shape, dt))

        def split(name, shape):
            return [sb(f"{name}_hi", shape, F32R), sb(f"{name}_lo", shape, F32R)]

        up_q = sb("at_up_q", [128, AH, QR])
        up_kv = sb("at_up_kv", [128, AH, 2, KVR])
        wide = sb("at_wide", [128, AH * D])
        woT = wide[:, :].rearrange("p (h n) -> p h n", h=AH)
        oT = wide[:, :].rearrange("p (a t) -> p a t", a=APAIRS)
        wq, wqs = sb("at_wq", [128, AH, KVR + ROPE]), sb("at_wqs", [128, APAIRS, 2 * ROPE])
        wq2, wqs2 = split("at_wq2", [128, AH, KVR + ROPE]), split("at_wqs2", [128, APAIRS, 2 * ROPE])
        wvo = sb("at_wvo", [128, APAIRS, D])
        qcos = [sb(f"at_cos{i}", [128, T]) for i in range(2)]
        qsin = sb("at_sin", [128, T])
        qin, kin = split("at_qin", [128, T]), [split(f"at_kin{i}", [128, T]) for i in range(2)]
        vin = sb("at_vin", [128, CH, KVR])
        g1 = sb("at_g1", [128, CH, D])
        q, qsw = sb("at_q", [128, T]), sb("at_qsw", [128, T])
        qT = [split(f"at_qT{i}", [128, T]) for i in range(2)]
        PR = [sb(f"at_P{i}", [128, T]) for i in range(3)]
        PT = [sb(f"at_PT{i}", [128, T]) for i in range(3)]
        nm, sm, rc = (sb(f"at_{n}", [128, 2, 2, CH]) for n in ("nm", "sm", "rc"))
        o = sb("at_o", [128, CH, 2, KVR])
        psS = [ctx.enter_context(nc.psum_tensor(f"at_S{i}", [128, 512], F32)) for i in range(3)]
        psT = [ctx.enter_context(nc.psum_tensor(f"at_T{i}", [128, 512], F32)) for i in range(2)]
        psQ = [ctx.enter_context(nc.psum_tensor(f"at_Q{i}", [128, 512], F32)) for i in range(2)]
        psO = ctx.enter_context(nc.psum_tensor("at_O", [128, 512], F32))
        s = sems(nc, ctx, "at_loaded", "at_w_ready0", "at_w_ready1", "at_w_done0", "at_w_done1", "at_w_split", "at_in",
                 "at_g1", "at_q_ready", "at_cos", "at_sin", "at_qsum", "at_q_hi", "at_qT", "at_s_ready",
                 "at_nm", "at_exp", "at_turned", "at_evA", "at_evD", "at_pv", "at_rc", "at_o",
                 "at_oT_ready", "at_oT", "at_out_ready", "at_sg", "at_fin", "at_stored")
        block = ctx.enter_context(nc.Block())
        LOADS = 10

        def steps():
            def unit(n):
                return n if 0 <= n < UNITS else None

            divide = {8 * pr + 7 + CH: pr for pr in range(APAIRS)}
            turn_out = {min(8 * pr + 10 + CH, UNITS + CH): pr for pr in range(APAIRS)}
            for n in range(UNITS + CH + 1):
                yield n, unit(n), unit(n - 2), unit(n - 3), unit(n - 4), divide.get(n), turn_out.get(n)

        def of_pair(t, n):
            return t[:, n // 8 % 2, n // 4 % 2, n % 4:n % 4 + 1]

        @block.sync
        def _(sp):
            sp.dma_start(up_q[:, :, :], io.wq_up).then_inc(s.at_loaded, 16)
            sp.dma_start(up_kv[:, :, :, :], io.wkv_up).then_inc(s.at_loaded, 16)
            sp.dma_start(woT, io.woT.rearrange("(h v) n -> v h n", v=VDIM)).then_inc(s.at_loaded, 16)
            for par in range(2):
                at = ROPE * (1 - par)
                sp.dma_start(wq[:, par::2, at:at + ROPE], io.wq_ropeT[:, par::2, :]).then_inc(s.at_loaded, 16)
                sp.dma_start(qcos[par][:, :], io.c_qcos[par]).then_inc(s.at_loaded, 16)
            sp.dma_start(wqs[:, :, :], io.wq_swapT).then_inc(s.at_loaded, 16)
            sp.dma_start(qsin[:, :], io.c_qsin).then_inc(s.at_loaded, 16)
            sp.wait_ge(s.at_loaded, 16 * (LOADS - 1))
            out = io.out.rearrange("b (c p) d -> b p c d", p=128)
            for b in range(B):
                sp.wait_ge(s.at_fin, b + 1)
                sp.dma_start(out[b], m.acc[:, b * CH:(b + 1) * CH, :]).then_inc(s.at_stored, 16)
            sp.wait_ge(s.at_stored, 16 * B)

        @block.tensor
        def _(pe):
            def queries(b, h):
                wait(pe, s.at_cos, b * AH + h)
                mm = split_matmul(pe, psQ[0][:, :], [w[:, h, :] for w in wq2], [x[:, :] for x in qin])
                mm.then_inc(s.at_q_ready, 1)
                if h % 2 == 0:
                    pr = h // 2
                    wait(pe, s.at_sin, b * APAIRS + pr)
                    if pr >= 3:
                        pe.wait_ge(s.at_oT, b * APAIRS + pr - 2)
                    mm = split_matmul(pe, psQ[1][:, :], [w[:, pr, :] for w in wqs2], [x[:, :] for x in qin])
                    mm.then_inc(s.at_q_ready, 1)

            def scores(b, n):
                h, i = n // CH, n % CH
                if i == 0:
                    pe.wait_ge(s.at_qT, b * AH + h + 1)
                if n >= 3:
                    pe.wait_ge(s.at_exp, b * UNITS + n - 2)
                w = (i + 1) * 128
                split_matmul(pe, psS[n % 3][:, 0:w], [x[:, i * 128:(i + 1) * 128] for x in qT[h % 2]],
                             [x[:, 0:w] for x in kin[h % 2]], last=False)
                pe.matmul(psS[n % 3][:, w - 128:w], m.identb[:, :], m.maskb[:, 1, :], start=False, stop=True)\
                    .then_inc(s.at_s_ready, 1)

            def evacuated(b, n):
                if n % CH == CH - 1:
                    pe.wait_ge(s.at_evD, b * AH + n // CH + 1)
                else:
                    pe.wait_ge(s.at_evA, b * AH * (CH - 1) + n // CH * (CH - 1) + n % CH + 1)

            def turn(b, n):
                pe.wait_ge(s.at_exp, b * UNITS + n + 1)
                if n >= 2:
                    evacuated(b, n - 2)
                for j in range(n % CH + 1):
                    mm = pe.transpose(psT[n % 2][:, j * 128:(j + 1) * 128], PR[n % 3][:, j * 128:(j + 1) * 128], m.ident[:, :])
                mm.then_inc(s.at_turned, 1)

            def values(b, n):
                evacuated(b, n)
                if n % 8 == 0 and n:
                    pe.wait_ge(s.at_o, b * APAIRS + n // 8)
                i = n % CH
                at = n % 8 * KVR
                for j in range(i + 1):
                    mm = pe.matmul(psO[:, at:at + KVR], PT[n % 3][:, j * 128:(j + 1) * 128], vin[:, j, :],
                                   start=(j == 0), stop=(j == i))
                mm.then_inc(s.at_pv, 1)

            def turn_out(b, pr):
                pe.wait_ge(s.at_o, b * APAIRS + pr + 1)
                pe.wait_ge(s.at_sin, b * APAIRS + min(pr + 3, APAIRS))
                for i in range(CH):
                    mm = pe.transpose(psQ[1][:, i * 128:(i + 1) * 128], o[:, i, :, :].rearrange("p h r -> p (h r)"), m.ident[:, :])
                mm.then_inc(s.at_oT_ready, 1)

            pe.wait_ge(s.at_loaded, 16 * (LOADS - 1))
            for h in range(AH):
                at = h // 2 * KVR
                pe.matmul(psS[h % 2][:, at:at + KVR], up_q[:, h, :], up_kv[:, h, 0, :], start=True, stop=True)\
                    .then_inc(s.at_w_ready0, 1)
            for pr in range(APAIRS):
                if pr >= 2:
                    pe.wait_ge(s.at_w_done1, pr - 1)
                for hh in range(2):
                    h = 2 * pr + hh
                    mm = pe.matmul(psQ[pr % 2][hh * KVR:(hh + 1) * KVR, 0:D], up_kv[:, h, 1, :], woT[:, h, :], start=True, stop=True)
                mm.then_inc(s.at_w_ready1, 1)
            pe.wait_ge(s.at_w_done1, APAIRS)
            pe.wait_ge(s.at_w_split, 4)
            def first_queries(b):
                pe.wait_ge(s.at_in, b * 7 + 7)
                queries(b, 0)
                queries(b, 1)

            def row(b, last=False):
                for n, made, turned, _, applied, _, turned_out in steps():
                    if n % CH == CH - 1 and n // CH + 2 < AH:
                        queries(b, n // CH + 2)
                    if made is not None:
                        scores(b, made)
                    if turned is not None:
                        turn(b, turned)
                    if turned_out is not None:
                        turn_out(b, turned_out)
                    if applied is not None:
                        values(b, applied)
                pe.wait_ge(s.at_oT, (b + 1) * APAIRS)
                if not last:
                    first_queries(b + 1)
                for c in range(CH):
                    for pr in range(APAIRS):
                        mm = pe.matmul(psT[c // 2][:, c % 2 * D:(c % 2 + 1) * D], oT[:, pr, c * 128:(c + 1) * 128], wvo[:, pr, :],
                                       start=(pr == 0), stop=(pr == APAIRS - 1))
                mm.then_inc(s.at_out_ready, 1)
                if not last:
                    pe.wait_ge(s.at_sg, 2 * b + 2)

            first_queries(0)
            with pe.Fori(0, B - 1) as b:
                row(b)
            row(B - 1, last=True)

        @block.scalar
        def _(act):
            def high(b, h):
                act.wait_ge(s.at_qsum, b * AH + h + 1)
                act.activation(qT[h % 2][0][:, :], q[:, :], ACT.Copy).then_inc(s.at_q_hi, 1)

            act.activation(m.moe[:, :, :], m.moe[:, :, :], ACT.Silu).then_inc(s.at_g1, 1)
            act.wait_ge(s.at_loaded, 16 * (LOADS - 1))
            for par in range(2):
                act.wait_ge(s.at_w_ready0, AH - 1 + par)
                at = ROPE * par
                act.activation(wq[:, par::2, at:at + KVR], psS[par][:, :].rearrange("p (h r) -> p h r", r=KVR), ACT.Copy, scale=SCALE)\
                    .then_inc(s.at_w_done0, 1)
                at = ROPE - at
                act.activation(wq[:, par::2, at:at + ROPE], wq[:, par::2, at:at + ROPE], ACT.Copy, scale=SCALE).then_inc(s.at_w_done0, 1)
            act.activation(wqs[:, :, :], wqs[:, :, :], ACT.Copy, scale=SCALE).then_inc(s.at_w_done0, 1)
            act.wait_ge(s.at_w_done0, 5)
            act.activation(wq2[0][:, :, :], wq[:, :, :], ACT.Copy).then_inc(s.at_w_split, 1)
            act.activation(wqs2[0][:, :, :], wqs[:, :, :], ACT.Copy).then_inc(s.at_w_split, 1)

            def row(b, last=False):
                for n, made, _, left, _, _, turned_out in steps():
                    if left is not None and left % CH < CH - 1:
                        w = (left % CH + 1) * 128
                        act.wait_ge(s.at_turned, b * UNITS + left + 1)
                        act.activation(PT[left % 3][:, 0:w], psT[left % 2][:, 0:w], ACT.Copy).then_inc(s.at_evA, 1)
                    if made is not None:
                        w = (n % CH + 1) * 128
                        act.wait_ge(s.at_nm, b * UNITS + n + 1)
                        act.activation(PR[n % 3][:, 0:w], psS[n % 3][:, 0:w], ACT.Exp, bias=of_pair(nm, n),
                                       accum_out=of_pair(sm, n)).then_inc(s.at_exp, 1)
                        if n % CH == 1 and n // CH < AH - 1:
                            high(b, n // CH + 1)
                    if turned_out is not None:
                        act.wait_ge(s.at_oT_ready, b * APAIRS + turned_out + 1)
                        act.activation(oT[:, turned_out, :], psQ[1][:, :], ACT.Copy).then_inc(s.at_oT, 1)
                if not last:
                    high(b + 1, 0)

            high(0, 0)
            with act.Fori(0, B - 1) as b:
                row(b)
            row(B - 1, last=True)

        @block.vector
        def _(dve):
            def places(b):
                return bass.ds(b * T, T), bass.ds(b * CH, CH)

            def pair_of_tiles(b, half):
                return bass.ds(b * CH + 2 * half, 2)

            def rope(b, h):
                k = b * (AH + APAIRS) + h + (h + 1) // 2
                dve.wait_ge(s.at_q_ready, k + 1)
                wait(dve, s.at_qT, b * AH + h)
                dve.tensor_tensor(q[:, :], psQ[0][:, :], qcos[h % 2][:, :], ALU.mult).then_inc(s.at_cos, 1)
                if h % 2 == 0:
                    dve.wait_ge(s.at_q_ready, k + 2)
                    dve.tensor_tensor(qsw[:, :], psQ[1][:, :], qsin[:, :], ALU.mult).then_inc(s.at_sin, 1)

            dve.wait_ge(s.at_loaded, 16 * (LOADS - 1))
            for pr in range(APAIRS):
                dve.wait_ge(s.at_w_ready1, pr + 1)
                dve.tensor_copy(wvo[:, pr, :], psQ[pr % 2][:, 0:D]).then_inc(s.at_w_done1, 1)
            dve.wait_ge(s.at_w_split, 2)
            dve.tensor_tensor(wq2[1][:, :, :], wq[:, :, :], wq2[0][:, :, :].bitcast(F32), ALU.subtract).then_inc(s.at_w_split, 1)
            dve.tensor_tensor(wqs2[1][:, :, :], wqs[:, :, :], wqs2[0][:, :, :].bitcast(F32), ALU.subtract).then_inc(s.at_w_split, 1)

            def split_row(b):
                row, tiles = places(b)
                parts = [qin] + kin
                for i in range(3):
                    dve.tensor_scalar(parts[i][0][:, :], m.qkT[:, i, row], 1.0, None, ALU.mult).then_inc(s.at_in, 1)
                for i in range(3):
                    dve.wait_ge(s.at_in, b * 7 + 1 + i)
                    dve.tensor_tensor(parts[i][1][:, :], m.qkT[:, i, row], parts[i][0][:, :].bitcast(F32), ALU.subtract).then_inc(s.at_in, 1)
                dve.tensor_scalar(vin[:, :, :], m.kv[:, tiles, :], 1.0, None, ALU.mult).then_inc(s.at_in, 1)
                rope(b, 0)

            def row(b, last=False):
                _, tiles = places(b)
                for n, made, _, left, _, divided, _ in steps():
                    if left is not None and left % CH == CH - 1:
                        dve.wait_ge(s.at_turned, b * UNITS + left + 1)
                        dve.tensor_copy(PT[left % 3][:, :], psT[left % 2][:, :]).then_inc(s.at_evD, 1)
                    if made is not None:
                        w = (n % CH + 1) * 128
                        dve.wait_ge(s.at_s_ready, b * UNITS + n + 1)
                        dve.tensor_reduce(of_pair(nm, n), psS[n % 3][:, 0:w], AX, ALU.max, negate=True).then_inc(s.at_nm, 1)
                        if n % CH == 0 and n // CH < AH - 1:
                            rope(b, n // CH + 1)
                    if divided is not None:
                        par = divided % 2
                        dve.wait_ge(s.at_exp, b * UNITS + divided * 8 + 8)
                        dve.reciprocal(rc[:, par, :, :], sm[:, par, :, :]).then_inc(s.at_rc, 1)
                        dve.wait_ge(s.at_rc, b * APAIRS + divided + 1)
                        dve.wait_ge(s.at_pv, b * UNITS + divided * 8 + 8)
                        if divided:
                            dve.wait_ge(s.at_oT_ready, b * APAIRS + divided)
                        dve.tensor_tensor(o[:, :, :, :].rearrange("p i h r -> p h i r"),
                                          psO[:, :].rearrange("p (h i r) -> p h i r", h=2, i=CH),
                                          rc[:, par, :, :, None].to_broadcast([128, 2, CH, KVR]), ALU.mult).then_inc(s.at_o, 1)
                if not last:
                    dve.wait_ge(s.at_oT_ready, (b + 1) * APAIRS)
                    split_row(b + 1)
                dve.wait_ge(s.at_out_ready, b + 1)
                dve.wait_ge(s.at_g1, 1)
                for half in range(2):
                    dve.tensor_tensor(g1[:, 2 * half:2 * half + 2, :], psT[half][:, :].rearrange("p (c d) -> p c d", d=D),
                                      m.moe[:, pair_of_tiles(b, half), :], ALU.mult).then_inc(s.at_sg, 1)
                dve.wait_ge(s.at_sg, 2 * b + 2)
                dve.tensor_tensor(m.acc[:, tiles, :], g1[:, :, :], m.acc[:, tiles, :], ALU.add).then_inc(s.at_fin, 1)
                if not last:
                    dve.wait_ge(s.at_fin, b + 1)

            split_row(0)
            with dve.Fori(0, B - 1) as b:
                row(b)
            row(B - 1, last=True)

        @block.gpsimd
        def _(pool):
            with pool.Fori(0, B) as b:
                for h in range(AH):
                    n = b * AH + h
                    half = slice(KVR * (1 - h % 2), KVR * (2 - h % 2))
                    pool.wait_ge(s.at_cos, n + 1)
                    pool.wait_ge(s.at_sin, b * APAIRS + h // 2 + 1)
                    pool.tensor_tensor(q[half, :], q[half, :], qsw[half, :], ALU.add).then_inc(s.at_qsum, 1)
                    pool.wait_ge(s.at_q_hi, n + 1)
                    pool.tensor_tensor(qT[h % 2][1][:, :], q[:, :], qT[h % 2][0][:, :].bitcast(F32), ALU.subtract).then_inc(s.at_qT, 1)


def constants():
    q = np.arange(128)
    keep_up = q[:, None] <= q[None, :]
    c = {"c_ident": np.eye(128, dtype=np.float32), "c_triu": keep_up.astype(np.float32),
         "c_identb": np.eye(128).astype(mybir.dt.np(BF16)),
         "c_maskb": np.stack([np.where(keep_up, 0.0, MASKED), np.where(keep_up.T, 0.0, MASKED)], 1).astype(mybir.dt.np(BF16)),
         "c_onehot": np.stack([np.tile(np.eye(H), (3, 1)), -np.tile(np.eye(H), (3, 1))], 1).astype(mybir.dt.np(BF16))}
    f = (1.0 / 10000.0 ** (np.arange(0, ROPE, 2, dtype=np.float32) / ROPE)).astype(np.float32)
    ang = np.outer(np.arange(T, dtype=np.float32), f)
    cos = np.concatenate([np.cos(ang), np.cos(ang)], 1).astype(np.float32)
    sin = np.concatenate([-np.sin(ang), np.sin(ang)], 1).astype(np.float32)
    c["c_kcos"] = np.ascontiguousarray(cos.reshape(CH, 128, ROPE).transpose(1, 0, 2))
    c["c_ksin"] = np.ascontiguousarray(sin.reshape(CH, 128, ROPE).transpose(1, 0, 2))
    one = np.ones((KVR, T), np.float32)
    c["c_qcos"] = np.stack([np.concatenate([one, cos.T]), np.concatenate([cos.T, one])])
    c["c_qsin"] = np.concatenate([sin.T, sin.T])
    e = np.arange(E)
    c["c_before"] = np.ascontiguousarray(np.broadcast_to((e[None, :] < e[:, None]).astype(np.float32), (128, E, E)))
    return c


def layouts(i):
    win = i["L0_attn_Win"]
    x0, z0, b0, c0 = 0, H * P, 2 * H * P, 2 * H * P + H * N
    a = {"x": i["L0_attn_x"], "A_log": i["L0_attn_A_log"], "dt_bias": i["L0_attn_dt_bias"],
         "w_dt": np.ascontiguousarray(win[c0 + H * N:].T)}
    pack = np.empty((PAIRS, 128, PACK), np.float32)
    for p in range(PAIRS):
        rows = [win[x0 + p * 128:x0 + (p + 1) * 128], win[z0 + p * 128:z0 + (p + 1) * 128]]
        taps = [i["L0_attn_conv_w_x"][2 * p:2 * p + 2].reshape(128, TAPS)]
        for h in (2 * p, 2 * p + 1):
            rows += [win[b0 + h * N:b0 + (h + 1) * N], win[c0 + h * N:c0 + (h + 1) * N]]
            taps += [i["L0_attn_conv_w_b"][h], i["L0_attn_conv_w_c"][h]]
        w = np.concatenate(rows).T
        pack[p, :, 0:PACK_CONV] = w.reshape(KD, 128, CHANNELS).transpose(1, 0, 2).reshape(128, -1)
        pack[p, :, PACK_CONV:] = np.concatenate(taps, 1)
    a["w_pack"] = pack
    a["w_out"] = np.ascontiguousarray(i["L0_attn_Wout"].T.reshape(PAIRS, 128, D))
    for n in ("in_gamma", "in_beta", "agg_w", "agg_b", "pn_gamma", "pn_beta", "d1_w", "d2_w", "d2_b", "bc_w",
              "gate_w", "gate_b", "out_gamma", "out_beta"):
        a[n] = i["L0_ffn_" + n]
    a["bc_b"] = np.ascontiguousarray(i["L0_ffn_bc_b"].reshape(KD, 128).T)
    a["d1_b"] = np.ascontiguousarray(i["L0_ffn_d1_b"].reshape(HID // 128, 128).T)
    turned = np.concatenate([np.arange(0, ROPE, 2), np.arange(1, ROPE, 2)])
    swapped = np.roll(turned, ROPE // 2)
    wk = i["L1_attn_wk_rope"]
    a["w_down"] = np.ascontiguousarray(np.concatenate(
        [i["L1_attn_wq_down"], i["L1_attn_wkv_down"], wk[turned], wk[swapped], i["L1_ffn_gate_w"]]).T)
    a["q_norm_w"], a["kv_norm_w"] = i["L1_attn_q_norm_w"], i["L1_attn_kv_norm_w"]
    a["wq_up"] = np.ascontiguousarray(i["L1_attn_wq_up"].reshape(AH, NOPE, QR).transpose(1, 0, 2))
    a["wkv_up"] = np.ascontiguousarray(i["L1_attn_wkv_up"].reshape(AH, 2, NOPE, KVR).transpose(2, 0, 1, 3))
    wr = i["L1_attn_wq_rope"].reshape(AH, ROPE, QR)
    a["wq_ropeT"] = np.ascontiguousarray(wr[:, turned].transpose(2, 0, 1))
    swap = wr[:, swapped].reshape(APAIRS, 2, ROPE, QR)[:, ::-1]
    a["wq_swapT"] = np.ascontiguousarray(swap.transpose(3, 0, 1, 2).reshape(QR, APAIRS, 2 * ROPE))
    a["woT"] = np.ascontiguousarray(i["L1_attn_wo"].T)
    a["expert_w"], a["expert_b"] = i["L1_ffn_expert_w"], i["L1_ffn_expert_b"]
    return a


def program(nc, io):
    m = Buffers()
    with ExitStack() as whole:
        def sb_in(ctx):
            return lambda name, shape, dt=F32: ctx.enter_context(nc.sbuf_tensor(name, shape, dt))

        shared(m, sb_in(whole))
        with ExitStack() as part:
            mixer_buffers(m, sb_in(part))
            norm_and_decay(nc, m, io)
            thought(nc, m, io)
            mixer(nc, m, io)
        sb = sb_in(whole)
        m.moe = sb("moe", [128, TILES, D])
        m.kv = sb("kv", [128, TILES, KVR])
        m.qkT = sb("qkT", [128, 3, TOK])
        middle(nc, m, io)
        attention(nc, m, io)


def kernel(**inputs):
    import concourse.bacc as bacc
    from concourse.bass_utils import run_bass_kernel_spmd

    nc = bacc.Bacc("TRN2", target_bir_lowering=False, num_devices=1)
    arrays = {**layouts({k: np.asarray(v) for k, v in inputs.items()}), **constants()}
    aps = {k: nc.dram_tensor("in_" + k, a.shape, mybir.dt.from_np(a.dtype), kind="ExternalInput").ap()
           for k, a in arrays.items()}
    aps["out"] = nc.dram_tensor("out_0", (B, T, D), F32, kind="ExternalOutput").ap()
    program(nc, namedtuple("Arrays", aps)(**aps))
    r = run_bass_kernel_spmd(nc, [{"in_" + k: np.ascontiguousarray(a) for k, a in arrays.items()}], core_ids=[0])
    return r.results[0]["out_0"]
```

```python
from collections import namedtuple
from contextlib import ExitStack

import concourse.bass as bass
import numpy as np
from concourse import mybir

F32 = mybir.dt.float32
BF16 = mybir.dt.bfloat16
F32R = mybir.dt.float32r
ACT = mybir.ActivationFunctionType
ALU = mybir.AluOpType
AX = mybir.AxisListType.X

B, T, D = 4, 512, 256
TOK = B * T
TILES = TOK // 128
KD = D // 128
H, P, N, TAPS = 32, 64, 128, 4
PAIRS = H // 2
CH = T // 128
CHANNELS = 2 * P * 2 + 4 * N
CONVS = 5
PACK_CONV = KD * CHANNELS
PACK = PACK_CONV + CONVS * TAPS
HID = 1024
K_STEPS = 4
AH, NOPE, ROPE, VDIM, QR, KVR = 16, 128, 64, 128, 128, 64
APAIRS = AH // 2
E, TOPK = 8, 2
DOWN = QR + KVR + 2 * ROPE + E
MASKED = -1e30


class Buffers:
    pass


def sems(nc, ctx, *names):
    return namedtuple("Sems", names)(*[ctx.enter_context(nc.semaphore(n)) for n in names])


def wait(eng, sem, value):
    if value.__class__ is not int or value > 0:
        eng.wait_ge(sem, value)


def rsqrt_small(pool, out, x, scale, eps, minus_half, chain, base):
    pool.tensor_scalar(out, x, scale, eps, ALU.mult, ALU.add).then_inc(chain, 1)
    pool.wait_ge(chain, base + 1)
    return pool.tensor_tensor(out, out, minus_half, ALU.pow)


def split_matmul(pe, out, w, x, first=True, last=True):
    pe.matmul(out, w[0], x[0], start=first, stop=False)
    pe.matmul(out, w[0], x[1], start=False, stop=False)
    return pe.matmul(out, w[1], x[0], start=False, stop=last)


def shared(m, sb):
    m.ident = sb("ident", [128, 128])
    m.identb = sb("identb", [128, 128], BF16)
    m.maskb = sb("maskb", [128, 2, 128], BF16)
    m.minus_half = sb("minus_half", [128, TILES])
    m.acc = sb("acc", [128, TILES, D])
    m.mean = sb("mean", [128, TILES])
    m.rstd = sb("rstd", [128, TILES])
    m.bcT = sb("bcT", [128, KD, B])
    m.conv0 = sb("conv0", [128, 6, B, T])
    m.w = [sb("w0", [128, PACK])]
    place = m.conv0[:, :, :, :].rearrange("p c b t -> p (c b t)")
    m.x = place[:, 2 * TOK:4 * TOK].rearrange("p (t d) -> p t d", d=D)
    m.wide = place[:, 4 * TOK:6 * TOK]
    m.up_q = place[:, 0:TOK].rearrange("p (h r) -> p h r", h=AH)
    m.up_kv = place[:, TOK:2 * TOK].rearrange("p (h a r) -> p h a r", h=AH, a=2)
    m.gate_w = m.w[0][:, 0:KD * D].rearrange("p (k n) -> p k n", k=KD)
    m.gate_b, m.out_g, m.out_b = (m.w[0][:, i * D:(i + 1) * D] for i in range(KD, KD + 3))


def mixer_buffers(m, sb):
    m.onehot = sb("onehot", [96, 2, H], BF16)
    m.tab = sb("tab", [128, 4, TILES, H])
    m.cs = sb("cs", [96, TOK], BF16)
    m.xnT2 = [sb(f"xnT_{part}", [128, KD, TOK], F32R) for part in ("hi", "lo")]
    m.w.append(sb("w1", [128, PACK]))
    m.wo = sb("wo", [128, 2, D])
    conv = [m.conv0, sb("conv1", [128, 6, B, T])]
    m.conv = [[conv[u][:, ch, :, :] for ch in range(6)] for u in range(2)]
    m.ynT = [sb("ynT0", [128, B, T])[:, :, :], m.conv[1][BZ]]
    first, second = (c[:, :, :, :].rearrange("p c b t -> p (c b t)") for c in conv)
    m.xnT = first[:, 0:2 * TOK].rearrange("p (k t) -> p k t", k=KD)
    m.work = first[:, 2 * TOK:4 * TOK]
    m.stage_rows = first[:, 4 * TOK:5 * TOK]
    m.stage_x = second[:, 0:TILES * D].rearrange("p (t d) -> p t d", d=D)
    at = TILES * D
    m.thought = {}
    for name, shape in (("agg", (KD, D)), ("d1", (KD, HID)), ("d2", (HID // 128, D)), ("bc", (KD, D)), ("rows", (6, D)),
                        ("x4", (1, D)), ("normed", (1, D)), ("state", (1, D)), ("xT", (KD, B)), ("hT", (HID // 128, B)),
                        ("d1b", (1, HID // 128)), ("bcb", (1, KD)), ("stats", (1, 6)), ("mv", (1, 2)), ("rstd", (1, 1))):
        size = shape[0] * shape[1]
        place = second[:, at:at + size]
        m.thought[name] = place.rearrange("p (a b) -> p a b", a=shape[0]) if shape[0] > 1 else place
        at += size


def norm_and_decay(nc, m, io):
    xt = m.stage_x
    with ExitStack() as ctx:
        stats = ctx.enter_context(nc.sbuf_tensor("stats", [128, TILES, 6], F32))
        mv = ctx.enter_context(nc.sbuf_tensor("mv", [128, TILES, 2], F32))
        triu, ones = (ctx.enter_context(nc.sbuf_tensor(f"na_{n}", [128, 128], F32)) for n in ("triu", "ones"))
        w_dt = ctx.enter_context(nc.sbuf_tensor("na_w_dt", [128, KD, H], F32))
        bank = [ctx.enter_context(nc.psum_tensor(f"na{i}", [128, 512], F32)) for i in range(8)]
        s = sems(nc, ctx, "na_const", "na_const2", "na_x0", "na_x1", "na_x2", "na_x3", "na_half", "na_stats", "na_aggr", "na_eps", "na_rstd",
                 "na_xn", "na_turned", "na_even", "na_odd", "na_dtraw", "na_biased", "na_abs", "na_exp", "na_eA",
                 "na_ln", "na_relu", "na_dt", "na_da", "na_da3", "na_cs", "na_tot", "na_tot_copied", "na_csd",
                 "na_tabs", "na_rows", "na_part", "na_zero", "na_next", "na_xn_hi", "na_xn_lo")
        m.old_sems = list(s)
        x_loaded = [s.na_x0, s.na_x1, s.na_x2, s.na_x3]
        raw, ab, relu, tot = (m.work[:, i * 512:(i + 1) * 512] for i in range(4))
        da3 = m.work[:, 2048:2048 + TILES * 96].rearrange("p (t g h) -> p t g h", g=3, h=H)
        r1 = m.stage_rows[0:96, 0:TOK]
        ex_A = m.work[:, 3600:3600 + H]
        A_row = m.work[:, 3632:3632 + H]
        dtb_row = m.work[:, 3664:3664 + H]
        block = ctx.enter_context(nc.Block())

        def tiles_of(ap, h=H):
            return ap.rearrange("p (t h) -> p t h", h=h)

        @block.sync
        def _(sp):
            for b in range(B):
                sp.dma_start(xt[:, b * CH:(b + 1) * CH, :],
                             io.x[b].rearrange("(c p) d -> p c d", p=128)).then_inc(x_loaded[b], 16)
            sp.dma_start(m.ident[:, :], io.c_ident).then_inc(s.na_const, 16)
            sp.dma_start(triu[:, :], io.c_triu).then_inc(s.na_const, 16)
            sp.dma_start(w_dt[:, :, :], io.w_dt.rearrange("(k p) h -> p k h", p=128)).then_inc(s.na_const, 16)
            sp.dma_start(A_row, io.A_log.partition_broadcast(128)).then_inc(s.na_const2, 16)
            sp.dma_start(dtb_row, io.dt_bias.partition_broadcast(128)).then_inc(s.na_const2, 16)
            sp.dma_start(m.identb[:, :], io.c_identb).then_inc(s.na_const2, 16)
            sp.dma_start(m.maskb[:, :, :], io.c_maskb).then_inc(s.na_const2, 16)
            sp.dma_start(m.onehot[:, :, :], io.c_onehot).then_inc(s.na_const2, 16)
            sp.wait_ge(s.na_const2, 80)
            sp.dma_start(m.w[0][:, :], io.w_pack[0]).then_inc(s.na_next, 16)
            w = m.thought
            for i, v in enumerate((io.in_gamma, io.in_beta, io.agg_b, io.pn_gamma, io.pn_beta, io.d2_b)):
                sp.dma_start(w["rows"][0:B, i, :], v.partition_broadcast(B)).then_inc(s.na_next, 16)
            for name, v in (("agg", io.agg_w), ("d1", io.d1_w), ("d2", io.d2_w), ("bc", io.bc_w)):
                sp.dma_start(w[name], v.rearrange("(k p) n -> p k n", p=128)).then_inc(s.na_next, 16)
            sp.dma_start(w["d1b"], io.d1_b).then_inc(s.na_next, 16)
            sp.dma_start(w["bcb"], io.bc_b).then_inc(s.na_next, 16)
            sp.wait_ge(s.na_next, 16 * 13)

        @block.vector
        def _(dve):
            for b in range(B + 2):
                if b < B:
                    dve.wait_ge(x_loaded[b], 16)
                    for t in range(b * CH, (b + 1) * CH):
                        dve.bn_stats(stats[:, t, :], xt[:, t, :]).then_inc(s.na_stats, 1)
                    for t in range(b * CH, (b + 1) * CH):
                        dve.wait_ge(s.na_stats, t + 1)
                        dve.bn_aggr(mv[:, t, :], stats[:, t, :]).then_inc(s.na_aggr, 1)
                if 0 < b <= B:
                    dve.wait_ge(s.na_rstd, b)
                    for t in range((b - 1) * CH, b * CH):
                        dve.tensor_scalar(xt[:, t, :], xt[:, t, :], mv[:, t, 0:1], m.rstd[:, t:t + 1],
                                          ALU.subtract, ALU.mult).then_inc(s.na_xn, 1)
                if b > 1:
                    g = 2 * (b - 2)
                    dve.wait_ge(s.na_turned, g + 1)
                    dve.tensor_copy(m.xnT[:, g % 2, g // 2 * 512:(g // 2 + 1) * 512], bank[g][:, :]).then_inc(s.na_even, 1)
            dve.tensor_copy(m.mean[:, :], mv[:, :, 0]).then_inc(s.na_xn, 1)
            dve.wait_ge(s.na_dtraw, 1)
            dve.wait_ge(s.na_const2, 80)
            dve.tensor_tensor(tiles_of(raw), tiles_of(bank[0][:, :]),
                              dtb_row[:, None, :].to_broadcast([128, TILES, H]), ALU.add).then_inc(s.na_biased, 1)
            dve.wait_ge(s.na_biased, 1)
            dve.tensor_scalar(relu, raw, 0.0, None, ALU.max).then_inc(s.na_relu, 1)
            dve.wait_ge(s.na_relu, 1)
            dve.wait_ge(s.na_ln, 1)
            dt = m.tab[:, 0, :, :]
            dve.tensor_tensor(dt, tiles_of(relu), tiles_of(ab), ALU.add).then_inc(s.na_dt, 1)
            dve.wait_ge(s.na_dt, 1)
            dve.wait_ge(s.na_eA, 1)
            dve.scalar_tensor_tensor(tiles_of(raw), dt, -1.0,
                                     ex_A[:, None, :].to_broadcast([128, TILES, H]), ALU.mult, ALU.mult).then_inc(s.na_da, 1)
            dve.wait_ge(s.na_da, 1)
            for g in range(3):
                dve.tensor_copy(da3[:, :, g, :], tiles_of(raw)).then_inc(s.na_da3, 1)
            dve.wait_ge(s.na_tot, 1)
            dve.tensor_copy(tot, bank[2][:, :]).then_inc(s.na_tot_copied, 1)
            dve.wait_ge(s.na_tot_copied, 1)
            dve.wait_ge(s.na_tabs, 1)
            dve.tensor_tensor(relu, tot, bank[1][:, :], ALU.subtract).then_inc(s.na_csd, 1)
            n = 0
            for q in range(4):
                dve.wait_ge(s.na_rows, q + 1)
                at = slice(q * 512, (q + 1) * 512)
                rows = bank[3 + q][0:96, :]
                dve.tensor_copy(m.cs[:, at], rows).then_inc(s.na_part, 1)
                dve.wait_ge(s.na_part, n + 1)
                dve.tensor_tensor(r1[:, at], rows, m.cs[:, at], ALU.subtract).then_inc(s.na_part, 1)
                dve.wait_ge(s.na_part, n + 2)
                dve.tensor_copy(m.cs[0:64, at], r1[0:64, at]).then_inc(s.na_part, 1)
                dve.wait_ge(s.na_part, n + 3)
                dve.tensor_tensor(r1[0:32, at], r1[0:32, at], m.cs[0:32, at], ALU.subtract).then_inc(s.na_part, 1)
                dve.wait_ge(s.na_part, n + 4)
                dve.tensor_copy(m.cs[0:32, at], r1[0:32, at]).then_inc(s.na_part, 1)
                n += 5

        @block.gpsimd
        def _(pool):
            pool.memset(m.minus_half[:, :], -0.5).then_inc(s.na_half, 1)
            pool.memset(ones[:, :], 1.0).then_inc(s.na_half, 1)
            pool.memset(m.acc[:, :, :], 0.0).then_inc(s.na_zero, 1)
            pool.wait_ge(s.na_half, 1)
            for b in range(B):
                row = slice(b * CH, (b + 1) * CH)
                pool.wait_ge(s.na_aggr, CH * (b + 1))
                rsqrt_small(pool, m.rstd[:, row], mv[:, row, 1], 1.0, 1e-5, m.minus_half[:, 0:CH], s.na_eps, b)\
                    .then_inc(s.na_rstd, 1)
            for b in range(B):
                at = slice(b * T, (b + 1) * T)
                pool.wait_ge(s.na_xn_hi, b + 1)
                pool.tensor_tensor(m.xnT2[1][:, :, at], m.xnT[:, :, at], m.xnT2[0][:, :, at].bitcast(F32), ALU.subtract)\
                    .then_inc(s.na_xn_lo, 1)

        @block.tensor
        def _(pe):
            pe.wait_ge(s.na_const, 48)
            def raw_dt(b):
                pe.wait_ge(s.na_even, b + 1)
                pe.wait_ge(s.na_odd, b + 1)
                for t in range(b * CH, (b + 1) * CH):
                    for k in range(KD):
                        mm = pe.matmul(bank[0][:, t * H:(t + 1) * H], m.xnT[:, k, t * 128:(t + 1) * 128],
                                       w_dt[:, k, :], start=(k == 0), stop=(k == KD - 1))
                return mm

            for g in range(8):
                b, k = g // 2, g % 2
                pe.wait_ge(s.na_xn, CH * (b + 1))
                for c in range(CH):
                    mm = pe.transpose(bank[g][:, c * 128:(c + 1) * 128], xt[:, b * CH + c, k * 128:(k + 1) * 128],
                                      m.ident[:, :])
                mm.then_inc(s.na_turned, 1)
                if k == KD - 1 and b > 0:
                    raw_dt(b - 1)
            raw_dt(B - 1).then_inc(s.na_dtraw, 1)
            pe.wait_ge(s.na_da, 1)
            pe.wait_ge(s.na_half, 2)
            pe.matmul(bank[1][:, :], triu[:, :], raw, start=True, stop=True).then_inc(s.na_cs, 1)
            pe.matmul(bank[2][:, :], ones[:, :], raw, start=True, stop=True).then_inc(s.na_tot, 1)
            pe.wait_ge(s.na_da3, 3)
            for q in range(4):
                for c in range(4):
                    t = 4 * q + c
                    mm = pe.matmul(bank[3 + q][0:96, c * 128:(c + 1) * 128],
                                   da3[:, t, :, :].rearrange("p g h -> p (g h)"), triu[:, :], start=True, stop=True)
                mm.then_inc(s.na_rows, 1)

        @block.scalar
        def _(act):
            for g in range(1, 8, 2):
                act.wait_ge(s.na_turned, g + 1)
                act.activation(m.xnT[:, g % 2, g // 2 * 512:(g // 2 + 1) * 512], bank[g][:, :], ACT.Copy)\
                    .then_inc(s.na_odd, 1)
            act.wait_ge(s.na_even, 4)
            act.wait_ge(s.na_odd, 4)
            for b in range(B):
                at = slice(b * T, (b + 1) * T)
                act.activation(m.xnT2[0][:, :, at], m.xnT[:, :, at], ACT.Copy).then_inc(s.na_xn_hi, 1)
            act.wait_ge(s.na_const2, 80)
            act.activation(ex_A, A_row, ACT.Exp).then_inc(s.na_eA, 1)
            act.wait_ge(s.na_biased, 1)
            act.activation(ab, raw, ACT.Abs).then_inc(s.na_abs, 1)
            act.wait_ge(s.na_abs, 1)
            act.activation(ab, ab, ACT.Exp, scale=-1.0).then_inc(s.na_exp, 1)
            act.wait_ge(s.na_exp, 1)
            act.activation(ab, ab, ACT.Ln, bias=1.0).then_inc(s.na_ln, 1)
            act.wait_ge(s.na_cs, 1)
            act.activation(m.tab[:, 1, :, :], tiles_of(bank[1][:, :]), ACT.Exp).then_inc(s.na_tabs, 1)
            act.wait_ge(s.na_csd, 1)
            act.activation(m.tab[:, 2, :, :], tiles_of(relu), ACT.Exp).then_inc(s.na_tabs, 1)
            act.activation(m.tab[:, 3, :, :], tiles_of(tot), ACT.Exp).then_inc(s.na_tabs, 1)


LNS = K_STEPS + 1
HT = HID // 128
THOUGHT_SEMS = ("th_row_ready", "th_state", "th_stats", "th_aggr", "th_eps", "th_rstd", "th_hat",
                "th_scaled", "th_normed", "th_turned", "th_T", "th_h_ready", "th_h_biased", "th_gelu", "th_added",
                "th_bc_ready", "th_bc_done")


class ThoughtTensor:
    def __init__(self, pe, m, s, banks):
        self.pe, self.m, self.s, self.w = pe, m, s, m.thought
        self.row, self.T, self.h = banks[0:3]

    def rows(self):
        for k in range(KD):
            mm = self.pe.matmul(self.row[0:B, k * 128:(k + 1) * 128], self.m.xnT[:, k, T - 1::T], self.m.ident[:, :], start=True, stop=True)
        mm.then_inc(self.s.th_row_ready, 1)

    def turn(self, src):
        for k in range(KD):
            mm = self.pe.transpose(self.T[:, k * B:(k + 1) * B], src[0:B, k * 128:(k + 1) * 128], self.m.ident[0:B, 0:B])
        mm.then_inc(self.s.th_turned, 1)

    def up(self, n):
        pe, s, w = self.pe, self.s, self.w
        pe.wait_ge(s.th_normed, n + 1)
        self.turn(w["normed"])
        pe.wait_ge(s.th_T, n + 1)
        if n == 0:
            for k in range(KD):
                mm = pe.matmul(self.row[0:B, 0:D], w["xT"][:, k, :], w["agg"][:, k, :], start=(k == 0), stop=(k == KD - 1))
            mm.then_inc(s.th_row_ready, 1)
        else:
            for j in range(HT):
                for k in range(KD):
                    mm = pe.matmul(self.h[:, j * B:(j + 1) * B], w["d1"][:, k, j * 128:(j + 1) * 128], w["xT"][:, k, :],
                                   start=(k == 0), stop=(k == KD - 1))
            mm.then_inc(s.th_h_ready, 1)

    def down(self, n):
        pe, s, w = self.pe, self.s, self.w
        pe.wait_ge(s.th_gelu, n)
        for j in range(HT):
            mm = pe.matmul(self.row[0:B, 0:D], w["hT"][:, j, :], w["d2"][:, j, :], start=(j == 0), stop=(j == HT - 1))
        mm.then_inc(s.th_row_ready, 1)

    def broadcast(self):
        pe, s, w = self.pe, self.s, self.w
        pe.wait_ge(s.th_state, LNS)
        self.turn(w["state"])
        pe.wait_ge(s.th_T, LNS + 1)
        for j in range(KD):
            for k in range(KD):
                mm = pe.matmul(self.h[:, j * B:(j + 1) * B], w["bc"][:, k, j * 128:(j + 1) * 128], w["xT"][:, k, :],
                               start=(k == 0), stop=(k == KD - 1))
        mm.then_inc(s.th_bc_ready, 1)
        pe.wait_ge(s.th_bc_done, 1)


class ThoughtVector:
    def __init__(self, dve, m, s, banks):
        self.dve, self.m, self.s, self.w = dve, m, s, m.thought
        self.row, self.T, self.h = banks[0:3]

    def rows(self):
        self.dve.wait_ge(self.s.th_row_ready, 1)
        self.dve.tensor_copy(self.w["x4"][0:B, :], self.row[0:B, 0:D]).then_inc(self.s.th_added, 1)
        self.dve.wait_ge(self.s.th_added, 1)

    def keep_turn(self, n):
        self.dve.wait_ge(self.s.th_turned, n + 1)
        self.dve.tensor_copy(self.w["xT"].rearrange("p k b -> p (k b)"), self.T[:, 0:KD * B]).then_inc(self.s.th_T, 1)

    def norm(self, n):
        dve, s, w = self.dve, self.s, self.w
        src = (w["x4"] if n == 0 else w["state"])[0:B, :]
        normed, rows = w["normed"][0:B, :], w["rows"]
        stats, mv, rstd = w["stats"][0:B, :], w["mv"][0:B, :], w["rstd"][0:B, :]
        gamma, beta = (0, 1) if n == 0 else (3, 4)
        dve.bn_stats(stats, src).then_inc(s.th_stats, 1)
        dve.wait_ge(s.th_stats, n + 1)
        dve.bn_aggr(mv, stats).then_inc(s.th_aggr, 1)
        dve.wait_ge(s.th_rstd, n + 1)
        dve.tensor_scalar(normed, src, mv[:, 0:1], rstd, ALU.subtract, ALU.mult).then_inc(s.th_hat, 1)
        dve.wait_ge(s.th_hat, n + 1)
        dve.tensor_tensor(normed, normed, rows[0:B, gamma, :], ALU.mult).then_inc(s.th_scaled, 1)
        dve.wait_ge(s.th_scaled, n + 1)
        dve.tensor_tensor(normed, normed, rows[0:B, beta, :], ALU.add).then_inc(s.th_normed, 1)
        self.keep_turn(n)

    def hidden_bias(self, n):
        w, s = self.w, self.s
        self.dve.wait_ge(s.th_h_ready, n)
        self.dve.tensor_tensor(w["hT"], self.h[:, 0:HT * B].rearrange("p (j b) -> p j b", b=B),
                               w["d1b"][:, :, None].to_broadcast([128, HT, B]), ALU.add).then_inc(s.th_h_biased, 1)

    def new_state(self, n):
        dve, s, w = self.dve, self.s, self.w
        state, rows = w["state"][0:B, :], w["rows"]
        dve.wait_ge(s.th_row_ready, n + 2)
        if n == 0:
            dve.tensor_tensor(state, self.row[0:B, 0:D], rows[0:B, 2, :], ALU.add).then_inc(s.th_state, 1)
        else:
            dve.tensor_tensor(state, self.row[0:B, 0:D], state, ALU.add).then_inc(s.th_added, 1)
            dve.wait_ge(s.th_added, n + 1)
            dve.tensor_tensor(state, state, rows[0:B, 5, :], ALU.add).then_inc(s.th_state, 1)
        dve.wait_ge(s.th_state, n + 1)

    def broadcast(self):
        self.keep_turn(LNS)
        self.dve.wait_ge(self.s.th_bc_ready, 1)
        self.dve.tensor_tensor(self.m.bcT[:, :, :], self.h[:, 0:KD * B].rearrange("p (k b) -> p k b", b=B),
                               self.w["bcb"][:, :, None].to_broadcast([128, KD, B]), ALU.add).then_inc(self.s.th_bc_done, 1)


BX, BZ, BB0, BC0, BB1, BC1 = range(6)
PIECES = [(ch, half) for ch in (BB0, BC0, BB1, BC1, BX, BZ) for half in range(2)]
NP = len(PIECES)
NC = 2 * CONVS
CONV_OF = {BX: 0, BB0: 1, BC0: 2, BB1: 3, BC1: 4}
PER_STEP = NP // CH
OUTS = CH
PER_TRIP = 2 * NP + OUTS


BETWEEN = ((2, 3, 4), (5, 6, 7), (8, 9), (10, 11))


def mixer(nc, m, io):
    with ExitStack() as ctx:
        def sb(name, shape, dt=F32):
            return ctx.enter_context(nc.sbuf_tensor(name, shape, dt))

        L = [sb(f"L{h}", [128, B, 128]) for h in range(2)]
        BT = [sb(f"BT{h}", [128, B, 128]) for h in range(2)]
        dtx, dtx2, y, tmp, S, Sdl = (sb(n, [128, B, 2, P]) for n in ("dtx", "dtx2", "y", "tmp", "S", "Sdl"))
        sq = tmp
        wsp = [[sb(f"w_{part}{i}", [128, KD, 128], F32R) for part in ("hi", "lo")] for i in range(2)]
        ss = sb("ss", [128, B, 2])
        rs = sb("rs", [128, B, 2])
        tabp = [sb(f"tabp{u}", [128, 4, TILES, 2]) for u in range(2)]
        hot = [sb(f"hot{u}", [96, 2, 2, 128], BF16) for u in range(2)]
        piece = [ctx.enter_context(nc.psum_tensor(f"piece{i}", [128, 2, 512], F32)) for i in range(2)]
        bank = [ctx.enter_context(nc.psum_tensor(f"scan{i}", [128, 512], F32)) for i in range(4)]
        s = sems(nc, ctx, "w_loaded0", "w_loaded1", "wo_loaded", "piece_ready", "piece_read0", "piece_read1", "tap_done", "conv_chain",
                 "piece_final", "pair_tabs", "diff_ready", "exp_done", "scores_ready", "masked_done", "xT_ready",
                 "dtx_done", "dtx2_done", "BT_ready", "BT_done", "intra_ready", "inter_ready", "inter_read",
                 "y_done", "sadd_ready", "sdl_done", "S_done", "sq_done", "ss_done", "eps_done", "rs_done",
                 "ysc_done", "yT_ready", "yn_done", "w_hi_done", "w_lo_done", "next_loaded", *THOUGHT_SEMS)
        w_loaded = [s.w_loaded0, s.w_loaded1]
        piece_read = [s.piece_read0, s.piece_read1]
        block = ctx.enter_context(nc.Block())
        LAST = PAIRS // 2 - 1

        def w_of(u, ch):
            return m.w[u][:, 0:PACK_CONV].rearrange("p (k n) -> p k n", k=KD)[:, :, ch * 128:(ch + 1) * 128]

        def weights_split_after(i, it, u, last=False):
            if i % 2:
                return None
            if i < NP - 2:
                return i // 2 + 1, it, u
            return None if last and u else (0, it + u, 1 - u)

        def weight_loads(it, u):
            return 16 * (it + u)

        def weights_of(place, u):
            return w_of(u, PIECES[2 * place][0])

        def tap_w(u, ch, k):
            at = PACK_CONV + CONV_OF[ch] * TAPS + k
            return m.w[u][:, at:at + 1]

        def row4(ap):
            return ap.rearrange("p b h d -> p (b h) d")

        def tab_of(u, kind, c):
            return tabp[u][:, kind, c::CH, :]

        def spread(ap):
            return ap[:, :, :, None].to_broadcast([128, B, 2, P])

        def first_piece(it):
            return NP + it * PER_TRIP

        def pieces_of_step(u, c, more):
            per = PER_STEP if more else 0
            outs = max(c - 1, 0) if u else 0
            at = (NP if u else 0) + per * c + outs
            return [(at + i, c * PER_STEP + i) for i in range(per)], (at + per if u and c > 0 else None)

        def follows(it, u, c):
            return c == 0 and not (it.__class__ is int and it == 0 and u == 0)

        def tail_piece(more):
            return NP + (NP + OUTS - 1 if more else OUTS - 1)

        @block.tensor
        def _(pe):
            def proj(splits, n, i, slot, first=False):
                half = PIECES[i][1]
                if not first:
                    wait(pe, piece_read[slot], n)
                if half == 0:
                    wait(pe, s.w_lo_done, splits + i // 2 + 1)
                w = wsp[i // 2 % 2]
                for b in range(2):
                    at = (2 * half + b) * T
                    for k in range(KD):
                        mm = split_matmul(pe, piece[slot][:, b, :], [v[:, k, :] for v in w], [v[:, k, at:at + T] for v in m.xnT2],
                                          first=(k == 0), last=(k == KD - 1))
                mm.then_inc(s.piece_ready, 1)

            def out_piece(it, n, c, slot):
                wait(pe, piece_read[slot], n)
                wait(pe, s.yn_done, (2 * it + 1) * CH + c + 1)
                wait(pe, s.wo_loaded, 16 * (it + 1))
                for b in range(B):
                    for u in range(2):
                        mm = pe.matmul(piece[slot][:, b // 2, b % 2 * D:(b % 2 + 1) * D], m.ynT[u][:, b, c * 128:(c + 1) * 128],
                                       m.wo[:, u, :], start=(u == 0), stop=(u == 1))
                mm.then_inc(s.piece_ready, 1)

            def uses(it, n):
                return (NP + n) // 2 + it * (PER_TRIP // 2)

            def turn_y(p, u, c):
                wait(pe, s.ysc_done, p * CH + c + 1)
                for b in range(B):
                    mm = pe.transpose(bank[3][:, b * 128:(b + 1) * 128],
                                      y[:, b, :, :].rearrange("p h d -> p (h d)"), m.ident[:, :])
                mm.then_inc(s.yT_ready, 1)

            def out_last(it, more):
                n = tail_piece(more)
                out_piece(it, uses(it, n), CH - 1, n % 2)

            def step(it, p, u, c, more):
                buf = m.conv[u]
                todo, out = pieces_of_step(u, c, more)
                prev = follows(it, u, c)
                if c == 0:
                    wait(pe, s.pair_tabs, 2 * (p + 1))
                for h in range(2):
                    if h == 0:
                        wait(pe, s.y_done, p * CH + c)
                    elif c == 1:
                        wait(pe, s.BT_done, p * 2 * (CH - 1) + 1)
                    else:
                        wait(pe, s.inter_read, p * (CH - 1) + max(c - 1, 0))
                    for b in range(B):
                        q = slice(b * T + c * 128, b * T + (c + 1) * 128)
                        o = bank[h][:, b * 128:(b + 1) * 128]
                        pe.matmul(o, m.cs[:, q], hot[u][:, 1, h, :], start=True, stop=False)
                        pe.matmul(o, hot[u][:, 0, h, :], m.cs[:, q], start=False, stop=False)
                        mm = pe.matmul(o, m.identb[:, :], m.maskb[:, 0, :], start=False, stop=True)
                    mm.then_inc(s.diff_ready, 1)
                for h in range(2):
                    if h and prev:
                        if u and todo:
                            n, i = todo.pop(0)
                            proj(NP // 2 * (p + 1), uses(it, n), i, n % 2)
                        turn_y(p - 1, 1 - u, CH - 1)
                        if u == 0:
                            out_last(it - 1, True)
                    if c == 0:
                        wait(pe, s.piece_final, p * NC + 4 * (h + 1))
                    if h == 0:
                        wait(pe, s.S_done, p * (CH - 1) + c)
                    else:
                        wait(pe, s.yn_done, p * CH + max(c - 1, 0))
                        if c == 1:
                            wait(pe, s.masked_done, (p * CH + c) * 2)
                    for b in range(B):
                        q = slice(c * 128, (c + 1) * 128)
                        mm = pe.matmul(bank[2 + h][:, b * 128:(b + 1) * 128], buf[BB0 + 2 * h][:, b, q],
                                       buf[BC0 + 2 * h][:, b, q], start=True, stop=True)
                    mm.then_inc(s.scores_ready, 1)
                for n, i in todo[:-2]:
                    proj(NP // 2 * (p + 1), uses(it, n), i, n % 2)
                if c == 0:
                    wait(pe, s.piece_final, p * NC + 10)
                wait(pe, s.exp_done, (p * CH + c) * 2 + 1)
                for b in range(B):
                    mm = pe.transpose(bank[0][:, b * 128:(b + 1) * 128], buf[BX][:, b, c * 128:(c + 1) * 128], m.ident[:, :])
                mm.then_inc(s.xT_ready, 1)
                if c < CH - 1:
                    for h in range(2):
                        if h == 0:
                            wait(pe, s.exp_done, (p * CH + c) * 2 + 2)
                        else:
                            wait(pe, s.masked_done, (p * CH + c) * 2 + 1)
                        for b in range(B):
                            mm = pe.transpose(bank[1 + h][:, b * 128:(b + 1) * 128],
                                              buf[BB0 + 2 * h][:, b, c * 128:(c + 1) * 128], m.ident[:, :])
                        mm.then_inc(s.BT_ready, 1)
                if c > 0:
                    wait(pe, s.masked_done, (p * CH + c) * 2 + 2)
                    turn_y(p, u, c - 1)
                for n, i in todo[-2:-1]:
                    proj(NP // 2 * (p + 1), uses(it, n), i, n % 2)
                wait(pe, s.masked_done, (p * CH + c) * 2 + 2)
                wait(pe, s.dtx_done, p * CH + c + 1)
                for b in range(B):
                    for h in range(2):
                        at = (b * 2 + h) * P
                        mm = pe.matmul(bank[0][:, at:at + P], L[h][:, b, :], dtx[:, b, h, :], start=True, stop=True)
                mm.then_inc(s.intra_ready, 1)
                if c > 0:
                    wait(pe, s.S_done, p * (CH - 1) + c)
                    if c < CH - 1:
                        wait(pe, s.BT_done, (p * (CH - 1) + c) * 2 + 1)
                    else:
                        wait(pe, s.exp_done, (p * CH + c) * 2 + 2)
                    for b in range(B):
                        for h in range(2):
                            at = (b * 2 + h) * P
                            mm = pe.matmul(bank[1][:, at:at + P], buf[BC0 + 2 * h][:, b, c * 128:(c + 1) * 128],
                                           S[:, b, h, :], start=True, stop=True)
                    mm.then_inc(s.inter_ready, 1)
                if c < CH - 1:
                    wait(pe, s.BT_done, (p * (CH - 1) + c) * 2 + 2)
                    wait(pe, s.dtx2_done, p * (CH - 1) + c + 1)
                    for b in range(B):
                        for h in range(2):
                            at = (b * 2 + h) * P
                            mm = pe.matmul(bank[2][:, at:at + P], BT[h][:, b, :], dtx2[:, b, h, :], start=True, stop=True)
                    mm.then_inc(s.sadd_ready, 1)
                for n, i in todo[-1:]:
                    proj(NP // 2 * (p + 1), uses(it, n), i, n % 2)
                if out is not None:
                    out_piece(it, uses(it, out), c - 1, out % 2)

            def trip(it, last=False):
                for u in range(2):
                    p = 2 * it + u
                    more = not (last and u)
                    for c in range(CH):
                        step(it, p, u, c, more)
                if last:
                    turn_y(2 * it + 1, 1, CH - 1)
                    out_last(it, False)

            def pieces(*numbers):
                for i in numbers:
                    proj(0, i // 2, i, i % 2, first=i < 2)

            th = ThoughtTensor(pe, m, s, bank)
            th.rows()
            pieces(0)
            th.up(0)
            pieces(1)
            for n in range(1, LNS):
                between = BETWEEN[n - 1]
                th.up(n)
                pieces(between[0])
                th.down(n)
                pieces(*between[1:])
            th.broadcast()
            trip(0)
            with pe.Fori(1, LAST) as it:
                trip(it)
            trip(LAST, last=True)

        @block.scalar
        def _(act):
            def high(todo, ready=0):
                if todo is not None:
                    place, it, u = todo
                    wait(act, s.piece_ready, ready)
                    wait(act, w_loaded[u], weight_loads(it, u))
                    act.activation(wsp[place % 2][0][:, :, :], weights_of(place, u), ACT.Copy).then_inc(s.w_hi_done, 1)

            def tap(u, n, i, slot):
                ch, half = PIECES[i]
                if ch == BZ:
                    return
                wait(act, s.piece_ready, n + 1)
                act.activation(m.conv[u][ch][:, 2 * half:2 * half + 2, :], piece[slot][:, :, :], ACT.Copy,
                               scale=tap_w(u, ch, TAPS - 1)).then_inc(s.tap_done, 1)

            def fin(u, n, i, slot, uses):
                ch, half = PIECES[i]
                dst = m.conv[u][ch][:, 2 * half:2 * half + 2, :]
                if ch == BZ:
                    wait(act, s.piece_ready, n + 1)
                    act.activation(dst, piece[slot][:, :, :], ACT.Silu).then_inc(piece_read[slot], 1)
                else:
                    wait(act, piece_read[slot], uses + 1)
                    act.activation(dst, dst, ACT.Silu).then_inc(s.piece_final, 1)

            def step(it, p, u, c, more, last):
                todo, _ = pieces_of_step(u, c, more)
                for h in range(2):
                    wait(act, s.diff_ready, (p * CH + c) * 2 + h + 1)
                    act.activation(L[h][:, :, :].rearrange("p b q -> p (b q)"), bank[h][:, :], ACT.Exp).then_inc(s.exp_done, 1)

                def args(k, todo=todo):
                    n, i = todo[k]
                    return first_piece(it) + n, i, n % 2, (NP + n) // 2 + it * (PER_TRIP // 2)

                if more and c > 0:
                    n, i, slot, uses = args(2, pieces_of_step(u, c - 1, more)[0])
                    fin(1 - u, n, i, slot, uses)
                if more:
                    n, i, slot, uses = args(0)
                    tap(1 - u, n, i, slot)
                    high(weights_split_after(i, it + u, 1 - u, last), n + 1)
                if c < CH - 1:
                    for h in range(2):
                        wait(act, s.BT_ready, (p * (CH - 1) + c) * 2 + h + 1)
                        act.activation(BT[h][:, :, :].rearrange("p b q -> p (b q)"), bank[1 + h][:, :], ACT.Copy)\
                            .then_inc(s.BT_done, 1)
                for k in (1, 2):
                    if k == 2:
                        wait(act, s.y_done, p * CH + c + 1)
                        act.activation(sq[:, :, :, :], y[:, :, :, :], ACT.Square).then_inc(s.sq_done, 1)
                    if more:
                        n, i, slot, uses = args(k)
                        tap(1 - u, n, i, slot)
                        high(weights_split_after(i, it + u, 1 - u, last), n + 1)
                        n, i, slot, uses = args(k - 1)
                        fin(1 - u, n, i, slot, uses)
                if more and c == CH - 1:
                    n, i, slot, uses = args(2)
                    fin(1 - u, n, i, slot, uses)

            def trip(it, last=False):
                for u in range(2):
                    for c in range(CH):
                        step(it, 2 * it + u, u, c, not (last and u), last)

            high((0, 0, 0))
            hidden = [between[0] for between in BETWEEN]
            for i in range(NP + 1):
                if i < NP:
                    if i in hidden:
                        n = hidden.index(i) + 1
                        act.wait_ge(s.th_h_biased, n)
                        act.activation(m.thought["hT"], m.thought["hT"], ACT.Gelu).then_inc(s.th_gelu, 1)
                    tap(0, i, i, i % 2)
                    high(weights_split_after(i, 0, 0), i + 1)
                if i > 0:
                    fin(0, i - 1, i - 1, (i - 1) % 2, (i - 1) // 2)
            trip(0)
            with act.Fori(1, LAST) as it:
                trip(it)
            trip(LAST, last=True)

        @block.vector
        def _(dve):
            def conv(u, i, slot, j):
                ch, half = PIECES[i]
                if ch == BZ:
                    return
                wait(dve, s.tap_done, j + 1)
                for k in range(1, TAPS):
                    dst = m.conv[u][ch][:, 2 * half:2 * half + 2, k:T]
                    if k > 1:
                        wait(dve, s.conv_chain, 2 * j + k - 1)
                    dve.scalar_tensor_tensor(dst, piece[slot][:, :, 0:T - k], tap_w(u, ch, TAPS - 1 - k), dst,
                                             ALU.mult, ALU.add)\
                        .then_inc(s.conv_chain if k < TAPS - 1 else piece_read[slot], 1)

            def low(todo):
                if todo is not None:
                    place, it, u = todo
                    high, low = wsp[place % 2]
                    wait(dve, s.w_hi_done, NP // 2 * (2 * it + u) + place + 1)
                    dve.tensor_tensor(low[:, :, :], weights_of(place, u), high[:, :, :].bitcast(F32), ALU.subtract)\
                        .then_inc(s.w_lo_done, 1)

            def add_out(n, c, slot):
                wait(dve, s.piece_ready, n + 1)
                for b2 in range(2):
                    a = m.acc[:, (2 * b2) * CH + c:(2 * b2 + 1) * CH + c + 1:CH, :]
                    i = dve.tensor_tensor(a, a, piece[slot][:, b2, :].rearrange("p (b d) -> p b d", b=2), ALU.add)
                i.then_inc(piece_read[slot], 1)

            def norm_y(p, u, c):
                wait(dve, s.yT_ready, p * CH + c + 1)
                dve.tensor_tensor(m.ynT[u][:, :, c * 128:(c + 1) * 128], bank[3][:, :].rearrange("p (b q) -> p b q", b=B),
                                  m.conv[u][BZ][:, :, c * 128:(c + 1) * 128], ALU.mult).then_inc(s.yn_done, 1)

            def step(it, p, u, c, more, last):
                todo, out = pieces_of_step(u, c, more)
                bk = [b[:, :].rearrange("p (b h d) -> p b h d", h=2, d=P) for b in bank]
                for h in range(2):
                    if h and follows(it, u, c):
                        norm_y(p - 1, 1 - u, CH - 1)
                        if u == 0:
                            n = tail_piece(True)
                            add_out(first_piece(it - 1) + n, CH - 1, n % 2)
                    wait(dve, s.exp_done, (p * CH + c) * 2 + h + 1)
                    wait(dve, s.scores_ready, (p * CH + c) * 2 + h + 1)
                    flat = L[h][:, :, :].rearrange("p b q -> p (b q)")
                    dve.tensor_tensor(flat, bank[2 + h][:, :], flat, ALU.mult).then_inc(s.masked_done, 1)
                wait(dve, s.xT_ready, p * CH + c + 1)
                if c == 0:
                    wait(dve, s.pair_tabs, 2 * (p + 1))
                wait(dve, s.dtx2_done, p * (CH - 1) + c)
                dve.tensor_tensor(dtx[:, :, :, :], bk[0], spread(tab_of(u, 0, c)), ALU.mult).then_inc(s.dtx_done, 1)
                for n, i in todo[0:1]:
                    conv(1 - u, i, n % 2, (p + 1) * NC + i)
                    low(weights_split_after(i, it + u, 1 - u, last))
                if c > 0:
                    norm_y(p, u, c - 1)
                for n, i in todo[1:2]:
                    conv(1 - u, i, n % 2, (p + 1) * NC + i)
                    low(weights_split_after(i, it + u, 1 - u, last))
                if c > 0:
                    wait(dve, s.inter_ready, p * (CH - 1) + c)
                    wait(dve, s.ss_done, p * CH + c)
                    dve.tensor_tensor(tmp[:, :, :, :], bk[1], spread(tab_of(u, 1, c)), ALU.mult).then_inc(s.inter_read, 1)
                    wait(dve, s.intra_ready, p * CH + c + 1)
                    wait(dve, s.inter_read, p * (CH - 1) + c)
                    dve.tensor_tensor(row4(y[:, :, :, :]), row4(bk[0]), row4(tmp[:, :, :, :]), ALU.add).then_inc(s.y_done, 1)
                else:
                    wait(dve, s.intra_ready, p * CH + c + 1)
                    dve.tensor_copy(row4(y[:, :, :, :]), row4(bk[0])).then_inc(s.y_done, 1)
                if c < CH - 1:
                    wait(dve, s.sadd_ready, p * (CH - 1) + c + 1)
                    if c > 0:
                        wait(dve, s.sdl_done, p * (CH - 2) + c)
                        dve.tensor_tensor(row4(S[:, :, :, :]), row4(bk[2]), row4(Sdl[:, :, :, :]), ALU.add).then_inc(s.S_done, 1)
                    else:
                        dve.tensor_copy(row4(S[:, :, :, :]), row4(bk[2])).then_inc(s.S_done, 1)
                wait(dve, s.sq_done, p * CH + c + 1)
                dve.tensor_reduce(ss[:, :, :], sq[:, :, :, :], AX, ALU.add).then_inc(s.ss_done, 1)
                wait(dve, s.ss_done, p * CH + c + 1)
                wait(dve, s.ysc_done, p * CH + c)
                dve.tensor_scalar(rs[:, :, :], ss[:, :, :], 1.0 / P, 1e-6, ALU.mult, ALU.add).then_inc(s.eps_done, 1)
                for n, i in todo[2:3]:
                    conv(1 - u, i, n % 2, (p + 1) * NC + i)
                    low(weights_split_after(i, it + u, 1 - u, last))
                if out is not None:
                    add_out(first_piece(it) + out, c - 1, out % 2)

            def trip(it, last=False):
                for u in range(2):
                    p = 2 * it + u
                    more = not (last and u)
                    for c in range(CH):
                        step(it, p, u, c, more, last)
                if last:
                    norm_y(2 * it + 1, 1, CH - 1)
                    n = tail_piece(False)
                    add_out(first_piece(it) + n, CH - 1, n % 2)

            low((0, 0, 0))
            def convs(*numbers):
                for i in numbers:
                    conv(0, i, i % 2, i)
                    low(weights_split_after(i, 0, 0))

            th = ThoughtVector(dve, m, s, bank)
            th.rows()
            th.norm(0)
            convs(0)
            th.new_state(0)
            for n in range(1, LNS):
                between = BETWEEN[n - 1]
                th.norm(n)
                convs(*(BETWEEN[n - 2][1:] if n > 1 else (1,)))
                th.hidden_bias(n)
                convs(between[0])
                th.new_state(n)
            th.broadcast()
            trip(0)
            with dve.Fori(1, LAST) as it:
                trip(it)
            trip(LAST, last=True)

        @block.gpsimd
        def _(pool):
            def tabs(p, u, head):
                pool.tensor_copy(tabp[u][:, :, :, :].rearrange("p k t h -> p (k t) h"),
                                 m.tab[:, :, :, bass.ds(head, 2)].rearrange("p k t h -> p (k t) h")).then_inc(s.pair_tabs, 1)
                pool.tensor_copy(hot[u][:, :, :, :], m.onehot[:, :, bass.ds(head, 2)][:, :, :, None].to_broadcast([96, 2, 2, 128]))\
                    .then_inc(s.pair_tabs, 1)

            def step(p, u, c):
                if c < CH - 1:
                    wait(pool, s.dtx_done, p * CH + c + 1)
                    pool.tensor_tensor(dtx2[:, :, :, :], dtx[:, :, :, :], spread(tab_of(u, 2, c)), ALU.mult)\
                        .then_inc(s.dtx2_done, 1)
                if 0 < c < CH - 1:
                    wait(pool, s.S_done, p * (CH - 1) + c)
                    pool.tensor_tensor(Sdl[:, :, :, :], S[:, :, :, :], spread(tab_of(u, 3, c)), ALU.mult)\
                        .then_inc(s.sdl_done, 1)
                wait(pool, s.eps_done, p * CH + c + 1)
                pool.tensor_tensor(rs[:, :, :], rs[:, :, :], m.minus_half[:, 0:8].rearrange("p (b h) -> p b h", b=B), ALU.pow).then_inc(s.rs_done, 1)
                wait(pool, s.rs_done, p * CH + c + 1)
                pool.tensor_tensor(y[:, :, :, :], y[:, :, :, :], spread(rs[:, :, :]), ALU.mult).then_inc(s.ysc_done, 1)

            def trip(it, last=False):
                for u in range(2):
                    p = 2 * it + u
                    for c in range(CH):
                        step(p, u, c)
                        if c == 1 and not (last and u):
                            tabs(p + 1, 1 - u, 4 * it + 2 * (u + 1))

            for old in m.old_sems:
                pool.sem_clear(old)
            mv, rstd = m.thought["mv"][0:B, :], m.thought["rstd"][0:B, :]
            for n in range(LNS):
                pool.wait_ge(s.th_aggr, n + 1)
                rsqrt_small(pool, rstd, mv[:, 1:2], 1.0, 1e-6, m.minus_half[0:B, 0:1], s.th_eps, n).then_inc(s.th_rstd, 1)
            tabs(0, 0, 0)
            trip(0)
            with pool.Fori(1, LAST) as it:
                trip(it)
            trip(LAST, last=True)

        @block.sync
        def _(sp):
            def load_out(p):
                sp.dma_start(m.wo[:, :, :], io.w_out[p:p + 2].rearrange("u p n -> p u n")).then_inc(s.wo_loaded, 16)

            sp.dma_start(m.w[1][:, :], io.w_pack[1]).then_inc(w_loaded[1], 16)
            load_out(0)
            for it in range(LAST):
                for u in range(2):
                    sp.wait_ge(s.piece_ready, it * PER_TRIP + NP * (u + 1))
                    sp.wait_ge(s.piece_final, (2 * it + u + 1) * NC)
                    sp.dma_start(m.w[u][:, :], io.w_pack[2 * it + 2 + u]).then_inc(w_loaded[u], 16)
                sp.wait_ge(s.piece_ready, first_piece(it + 1))
                load_out(2 * it + 2)
            for u in range(2):
                sp.wait_ge(w_loaded[u], weight_loads(LAST, u))
            sp.wait_ge(s.piece_final, PAIRS * NC)
            sp.wait_ge(s.inter_ready, (PAIRS - 1) * (CH - 1))
            for b in range(B):
                sp.dma_start(m.x[:, b * CH:(b + 1) * CH, :], io.x[b].rearrange("(c p) d -> p c d", p=128)).then_inc(s.next_loaded, 16)
            sp.dma_start(m.gate_w, io.gate_w.rearrange("(k p) n -> p k n", p=128)).then_inc(s.next_loaded, 16)
            for place, row in ((m.gate_b, io.gate_b), (m.out_g, io.out_gamma), (m.out_b, io.out_beta)):
                sp.dma_start(place, row.partition_broadcast(128)).then_inc(s.next_loaded, 16)
            sp.wait_ge(s.next_loaded, 16 * 8)


def middle(nc, m, io):
    R = CH
    with ExitStack() as ctx:
        def sb(name, shape, dt=F32):
            return ctx.enter_context(nc.sbuf_tensor(name, shape, dt))

        x, gate_w, gate_b, out_g, out_b = m.x, m.gate_w, m.gate_b, m.out_g, m.out_b
        spread = sb("mi_spread", [128, B, KD, 128])
        half_bc = sb("mi_half_bc", [128, B, D])
        down_w = sb("mi_dw", [128, KD, DOWN])
        ew = sb("mi_ew", [128, E, KD, D])
        eb = sb("mi_eb", [E, D])
        norm_w = sb("mi_nw", [128, QR + KVR])
        kcos, ksin = sb("mi_cos", [128, CH, ROPE]), sb("mi_sin", [128, CH, ROPE])
        before = sb("mi_before", [128, E, E])
        inv = sb("mi_inv", [128, R, 2])
        eps = sb("mi_eps", [128, 2])
        out, th, hat, x1, xn1 = (sb(f"mi_{n}", [128, R, D]) for n in ("out", "th", "hat", "x1", "xn1"))
        T0, T1 = sb("mi_T0", [128, KD, T]), sb("mi_T1", [128, KD, T])
        idle = sb("mi_idle", [128, 1])
        st, mv, rs = (sb(f"mi_{n}", [128, 2, R, w]) for n, w in (("st", 6), ("mv", 2), ("rs", 1)))
        dn, sqd = sb("mi_dn", [128, R, DOWN]), sb("mi_sqd", [128, R, QR + KVR])
        ssd, rsd = sb("mi_ssd", [128, R, 2]), sb("mi_rsd", [128, R, 2])
        gt, eq = sb("mi_gt", [128, R, E, E]), sb("mi_eq", [128, R, E, E])
        rank, sel, sl, garg, gates = (sb(f"mi_{n}", [128, R, E]) for n in ("rank", "sel", "sl", "garg", "gates"))
        hsum = sb("mi_hsum", [128, R])
        qn, kvn = sb("mi_qn", [128, R, QR]), sb("mi_kvn", [128, R, KVR])
        kcat = sb("mi_kcat", [128, R, KVR + ROPE + KVR])
        kr = sb("mi_kr", [128, R, ROPE])
        gT = sb("mi_gT", [E, T])
        moe = sb("mi_moe", [128, R, D])
        pA = ctx.enter_context(nc.psum_tensor("mi_pA", [128, 2, 512], F32))
        pB = ctx.enter_context(nc.psum_tensor("mi_pB", [128, 2, 512], F32))
        pE = ctx.enter_context(nc.psum_tensor("mi_pE", [128, 4, 512], F32))
        s = sems(nc, ctx, "mi_weights", "mi_next_loaded", "mi_const", "mi_spread", "mi_bc_ready", "mi_half_bc",
                 "mi_xn0", "mi_turned0", "mi_T0", "mi_gate_ready", "mi_gate_biased", "mi_tanh", "mi_gated", "mi_out",
                 "mi_stats", "mi_aggr", "mi_eps", "mi_rstd", "mi_hat", "mi_hat2", "mi_hat3", "mi_silu", "mi_sg",
                 "mi_x1", "mi_acc", "mi_xn1", "mi_turned1", "mi_T1", "mi_down_ready", "mi_dn", "mi_sq", "mi_ssd",
                 "mi_rsd_chain", "mi_rsd", "mi_route", "mi_route_arg", "mi_route_tanh", "mi_route_arg2", "mi_gates",
                 "mi_scaled", "mi_qn", "mi_kvn", "mi_rope", "mi_kcat", "mi_qk_turned", "mi_qk_done",
                 "mi_gates_turned", "mi_gT", "mi_bias_ready", "mi_experts_ready", "mi_expert_added", "mi_moe")
        block = ctx.enter_context(nc.Block())
        LOADS = 8

        def flat(ap):
            return ap.rearrange("p a b -> p (a b)")

        def tiles(r):
            return slice(r * R, (r + 1) * R) if r.__class__ is int else bass.ds(r * R, R)

        def tokens(r):
            return slice(r * T, (r + 1) * T) if r.__class__ is int else bass.ds(r * T, T)

        def run(eng, start, body, end):
            start(0)
            body(0)
            with eng.Fori(1, B - 1) as r:
                body(r)
            end(B - 1)

        @block.sync
        def _(sp):
            sp.dma_start(down_w[:, :, :], io.w_down.rearrange("(k p) n -> p k n", p=128)).then_inc(s.mi_weights, 16)
            sp.dma_start(norm_w[:, 0:QR], io.q_norm_w.partition_broadcast(128)).then_inc(s.mi_weights, 16)
            sp.dma_start(norm_w[:, QR:], io.kv_norm_w.partition_broadcast(128)).then_inc(s.mi_weights, 16)
            sp.dma_start(kcos[:, :, :], io.c_kcos).then_inc(s.mi_weights, 16)
            sp.dma_start(ksin[:, :, :], io.c_ksin).then_inc(s.mi_weights, 16)
            sp.dma_start(before[:, :, :], io.c_before).then_inc(s.mi_weights, 16)
            sp.dma_start(eb[:, :], io.expert_b).then_inc(s.mi_weights, 16)
            sp.dma_start(ew[:, :, :, :], io.expert_w.rearrange("e (k p) n -> p e k n", p=128)).then_inc(s.mi_weights, 16)
            sp.dma_start(m.up_q[:, :, :], io.wq_up).then_inc(s.mi_next_loaded, 16)
            sp.dma_start(m.up_kv[:, :, :, :], io.wkv_up).then_inc(s.mi_next_loaded, 16)
            sp.dma_start(m.wide.rearrange("p (h n) -> p h n", h=AH), io.woT.rearrange("(h v) n -> v h n", v=VDIM)).then_inc(s.mi_next_loaded, 16)
            sp.wait_ge(s.mi_next_loaded, 48)

        @block.tensor
        def _(pe):
            def turn0(r):
                wait(pe, s.mi_xn0, R * (r + 1))
                wait(pe, s.mi_moe, r - 1)
                for k in range(KD):
                    for t in range(R):
                        mm = pe.transpose(pA[:, k, t * 128:(t + 1) * 128], out[:, t, k * 128:(k + 1) * 128], m.ident[:, :])
                mm.then_inc(s.mi_turned0, 1)

            def gate(r):
                wait(pe, s.mi_T0, r + 1)
                for t in range(R):
                    for k in range(KD):
                        mm = pe.matmul(pA[:, t // 2, t % 2 * D:(t % 2 + 1) * D], T0[:, k, t * 128:(t + 1) * 128], gate_w[:, k, :],
                                       start=(k == 0), stop=(k == KD - 1))
                mm.then_inc(s.mi_gate_ready, 1)

            def turn1(r):
                wait(pe, s.mi_xn1, R * (r + 1))
                wait(pe, s.mi_gT, r)
                for k in range(KD):
                    for t in range(R):
                        mm = pe.transpose(pB[:, k, t * 128:(t + 1) * 128], xn1[:, t, k * 128:(k + 1) * 128], m.ident[:, :])
                mm.then_inc(s.mi_turned1, 1)

            def down(r):
                wait(pe, s.mi_T1, r + 1)
                wait(pe, s.mi_expert_added, r * R * E)
                for t in range(R):
                    for k in range(KD):
                        mm = pe.matmul(pE[:, t, 0:DOWN], T1[:, k, t * 128:(t + 1) * 128], down_w[:, k, :], start=(k == 0), stop=(k == KD - 1))
                mm.then_inc(s.mi_down_ready, 1)

            def experts(r, t):
                i = r * R + t
                if t == 0:
                    wait(pe, s.mi_dn, r + 1)
                for e in range(E):
                    if t and e % 2 == 0:
                        wait(pe, s.mi_expert_added, (i - 1) * E + e + 2)
                    for k in range(KD):
                        mm = pe.matmul(pE[:, e // 2, e % 2 * D:(e % 2 + 1) * D], T1[:, k, t * 128:(t + 1) * 128], ew[:, e, k, :],
                                       start=(k == 0), stop=(k == KD - 1))
                    if e % 2:
                        mm.then_inc(s.mi_experts_ready, 1)

            def turn_qk(r, a):
                if a == 0:
                    wait(pe, s.mi_qn, r + 1)
                if a == 1:
                    wait(pe, s.mi_kcat, r + 1)
                if a == 2:
                    wait(pe, s.mi_qk_done, 3 * r + 1)
                src = qn[:, :, :] if a == 0 else kcat[:, :, (a - 1) * ROPE:(a - 1) * ROPE + 128]
                for t in range(R):
                    mm = pe.transpose(pB[:, a % 2, t * 128:(t + 1) * 128], src[:, t, :], m.ident[:, :])
                mm.then_inc(s.mi_qk_turned, 1)

            def turn_gates(r):
                wait(pe, s.mi_gates, r + 1)
                wait(pe, s.mi_qk_done, 3 * r + 2)
                for t in range(R):
                    mm = pe.transpose(pB[0:E, 1, t * 128:(t + 1) * 128], gates[:, t, :], m.ident[:, :])
                mm.then_inc(s.mi_gates_turned, 1)

            def bias(r, more):
                wait(pe, s.mi_gT, r + 1)
                wait(pe, s.mi_gate_biased, r + 1 + more)
                for t in range(R):
                    mm = pe.matmul(pA[:, t // 2, t % 2 * D:(t % 2 + 1) * D], gT[:, t * 128:(t + 1) * 128], eb[:, :], start=True, stop=True)
                mm.then_inc(s.mi_bias_ready, 1)

            def start(r):
                turn0(r)
                gate(r)
                wait(pe, s.mi_weights, 16 * LOADS)

            def body(r, more=True):
                turn1(r)
                if more:
                    turn0(r + 1)
                down(r)
                if more:
                    gate(r + 1)
                experts(r, 0)
                turn_qk(r, 0)
                turn_qk(r, 1)
                experts(r, 1)
                turn_qk(r, 2)
                turn_gates(r)
                experts(r, 2)
                bias(r, 1 if more else 0)
                experts(r, 3)

            wait(pe, s.mi_spread, KD)
            for row in range(B):
                for k in range(KD):
                    mm = pe.transpose(pE[:, row // 2, row % 2 * D + k * 128:row % 2 * D + (k + 1) * 128], spread[:, row, k, :], m.ident[:, :])
            mm.then_inc(s.mi_bc_ready, 1)
            wait(pe, s.mi_half_bc, 2)
            run(pe, start, body, lambda r: body(r, more=False))

        @block.scalar
        def _(act):
            def T0_of(r):
                wait(act, s.mi_turned0, r + 1)
                act.activation(T0[:, :, :], pA[:, :, :], ACT.Copy).then_inc(s.mi_T0, 1)

            def gate(r):
                wait(act, s.mi_gate_biased, r + 1)
                act.activation(th[:, :, :], th[:, :, :], ACT.Tanh, scale=0.5).then_inc(s.mi_tanh, 1)

            def silu(r):
                wait(act, s.mi_hat3, r + 1)
                act.activation(hat[:, :, :], hat[:, :, :], ACT.Silu).then_inc(s.mi_silu, 1)

            def start(r):
                T0_of(r)
                gate(r)
                silu(r)

            def body(r, more=True):
                wait(act, s.mi_turned1, r + 1)
                act.activation(T1[:, :, :], pB[:, :, :], ACT.Copy).then_inc(s.mi_T1, 1)
                if more:
                    T0_of(r + 1)
                wait(act, s.mi_down_ready, r + 1)
                act.activation(dn[:, :, :], pE[:, :, 0:DOWN], ACT.Copy).then_inc(s.mi_dn, 1)
                wait(act, s.mi_dn, r + 1)
                act.activation(sqd[:, :, :], dn[:, :, 0:QR + KVR], ACT.Square).then_inc(s.mi_sq, 1)
                wait(act, s.mi_route_arg, r + 1)
                act.activation(garg[:, :, :], garg[:, :, :], ACT.Tanh).then_inc(s.mi_route_tanh, 1)
                if more:
                    gate(r + 1)
                    silu(r + 1)
                wait(act, s.mi_gates_turned, r + 1)
                act.activation(gT[:, :], pB[0:E, 1, :], ACT.Copy).then_inc(s.mi_gT, 1)

            run(act, start, body, lambda r: body(r, more=False))

        @block.vector
        def _(dve):
            def xn0(r):
                for t in range(R):
                    at = slice(r * R + t, r * R + t + 1) if r.__class__ is int else bass.ds(r * R + t, 1)
                    dve.tensor_scalar(out[:, t, :], x[:, at, :].rearrange("p o d -> p (o d)"), m.mean[:, at], m.rstd[:, at],
                                      ALU.subtract, ALU.mult).then_inc(s.mi_xn0, 1)

            def gate_bias(r):
                wait(dve, s.mi_gate_ready, r + 1)
                dve.tensor_tensor(th[:, :, :], pA[:, :, :].rearrange("p a (b d) -> p (a b) d", b=2), gate_b[:, None, :].to_broadcast([128, R, D]),
                                  ALU.add).then_inc(s.mi_gate_biased, 1)

            def gated(r):
                row = slice(r, r + 1) if r.__class__ is int else bass.ds(r, 1)
                wait(dve, s.mi_tanh, r + 1)
                dve.scalar_tensor_tensor(th[:, :, :], th[:, :, :], 1.0, half_bc[:, row, :].to_broadcast([128, R, D]), ALU.add, ALU.mult)\
                    .then_inc(s.mi_gated, 1)
                wait(dve, s.mi_gated, r + 1)
                dve.tensor_tensor(out[:, :, :], out[:, :, :], th[:, :, :], ALU.add).then_inc(s.mi_out, 1)
                wait(dve, s.mi_out, r + 1)
                moments(0, out, 2 * r)

            def moments(which, src, before):
                for t in range(R):
                    dve.bn_stats(st[:, which, t, :], src[:, t, :]).then_inc(s.mi_stats, 1)
                wait(dve, s.mi_stats, R * (before + 1))
                dve.tensor_copy(idle[:, :], m.minus_half[:, 0:1])
                for t in range(R):
                    dve.bn_aggr(mv[:, which, t, :], st[:, which, t, :]).then_inc(s.mi_aggr, 1)

            def hat_of(r):
                wait(dve, s.mi_rstd, 2 * r + 1)
                for t in range(R):
                    dve.tensor_scalar(hat[:, t, :], out[:, t, :], mv[:, 0, t, 0:1], rs[:, 0, t, :], ALU.subtract, ALU.mult).then_inc(s.mi_hat, 1)
                wait(dve, s.mi_hat, R * (r + 1))
                dve.tensor_tensor(hat[:, :, :], hat[:, :, :], out_g[:, None, :].to_broadcast([128, R, D]), ALU.mult).then_inc(s.mi_hat2, 1)
                wait(dve, s.mi_hat2, r + 1)
                dve.tensor_tensor(hat[:, :, :], hat[:, :, :], out_b[:, None, :].to_broadcast([128, R, D]), ALU.add).then_inc(s.mi_hat3, 1)

            def residual(r):
                wait(dve, s.mi_silu, r + 1)
                dve.tensor_tensor(hat[:, :, :], m.acc[:, tiles(r), :], hat[:, :, :], ALU.mult).then_inc(s.mi_sg, 1)
                wait(dve, s.mi_sg, r + 1)
                dve.tensor_tensor(x1[:, :, :], hat[:, :, :], x[:, tiles(r), :], ALU.add).then_inc(s.mi_x1, 1)
                wait(dve, s.mi_x1, r + 1)
                moments(1, x1, 2 * r + 1)
                dve.tensor_scalar(m.acc[:, tiles(r), :], x1[:, :, :], 1.0, None, ALU.mult).then_inc(s.mi_acc, 1)

            def xn1_of(r):
                wait(dve, s.mi_rstd, 2 * r + 2)
                for t in range(R):
                    dve.tensor_scalar(xn1[:, t, :], x1[:, t, :], mv[:, 1, t, 0:1], rs[:, 1, t, :], ALU.subtract, ALU.mult).then_inc(s.mi_xn1, 1)
                wait(dve, s.mi_xn1, R * (r + 1))

            def route(r):
                lg = dn[:, :, QR + KVR + 2 * ROPE:DOWN]
                n = r * 8
                wide = [128, R, E, E]
                wait(dve, s.mi_dn, r + 1)
                dve.tensor_tensor(gt[:, :, :, :], lg[:, :, None, :].to_broadcast(wide), lg[:, :, :, None].to_broadcast(wide), ALU.is_gt)\
                    .then_inc(s.mi_route, 1)
                dve.tensor_tensor(eq[:, :, :, :], lg[:, :, None, :].to_broadcast(wide), lg[:, :, :, None].to_broadcast(wide), ALU.is_equal)\
                    .then_inc(s.mi_route, 1)
                wait(dve, s.mi_route, n + 2)
                dve.tensor_tensor(eq[:, :, :, :], eq[:, :, :, :], before[:, None, :, :].to_broadcast(wide), ALU.mult).then_inc(s.mi_route, 1)
                wait(dve, s.mi_route, n + 3)
                dve.tensor_tensor(gt[:, :, :, :], gt[:, :, :, :], eq[:, :, :, :], ALU.add).then_inc(s.mi_route, 1)
                wait(dve, s.mi_route, n + 4)
                dve.tensor_reduce(rank[:, :, :], gt[:, :, :, :], AX, ALU.add).then_inc(s.mi_route, 1)
                wait(dve, s.mi_route, n + 5)
                dve.tensor_scalar(flat(sel[:, :, :]), flat(rank[:, :, :]), TOPK - 0.5, None, ALU.is_lt).then_inc(s.mi_route, 1)
                wait(dve, s.mi_route, n + 6)
                dve.tensor_tensor(sl[:, :, :], sel[:, :, :], lg, ALU.mult).then_inc(s.mi_route, 1)
                wait(dve, s.mi_route, n + 7)
                dve.tensor_reduce(hsum[:, :], sl[:, :, :], AX, ALU.add).then_inc(s.mi_route, 1)
                wait(dve, s.mi_route, n + 8)
                dve.scalar_tensor_tensor(garg[:, :, :], hsum[:, :, None].to_broadcast([128, R, E]), -0.5, lg, ALU.mult, ALU.add)\
                    .then_inc(s.mi_route_arg, 1)
                wait(dve, s.mi_sq, r + 1)
                dve.tensor_reduce(ssd[:, :, 0], sqd[:, :, 0:QR], AX, ALU.add).then_inc(s.mi_ssd, 1)
                dve.tensor_reduce(ssd[:, :, 1], sqd[:, :, QR:], AX, ALU.add).then_inc(s.mi_ssd, 1)

            def gates_of(r):
                wait(dve, s.mi_route_tanh, r + 1)
                dve.tensor_scalar(flat(garg[:, :, :]), flat(garg[:, :, :]), 0.5, 0.5, ALU.mult, ALU.add).then_inc(s.mi_route_arg2, 1)
                wait(dve, s.mi_route_arg2, r + 1)
                dve.tensor_tensor(gates[:, :, :], garg[:, :, :], sel[:, :, :], ALU.mult).then_inc(s.mi_gates, 1)

            def latents(r):
                wait(dve, s.mi_rsd, r + 1)
                o = QR + KVR
                dve.tensor_tensor(qn[:, :, :], dn[:, :, 0:QR], rsd[:, :, 0:1].to_broadcast([128, R, QR]), ALU.mult).then_inc(s.mi_scaled, 1)
                dve.tensor_tensor(kvn[:, :, :], dn[:, :, QR:o], rsd[:, :, 1:2].to_broadcast([128, R, KVR]), ALU.mult).then_inc(s.mi_scaled, 1)
                dve.tensor_tensor(kr[:, :, :], dn[:, :, o:o + ROPE], kcos[:, :, :], ALU.mult).then_inc(s.mi_rope, 1)
                dve.tensor_tensor(kcat[:, :, KVR:KVR + ROPE], dn[:, :, o + ROPE:o + 2 * ROPE], ksin[:, :, :], ALU.mult).then_inc(s.mi_rope, 1)
                wait(dve, s.mi_scaled, 2 * r + 2)
                dve.tensor_tensor(qn[:, :, :], qn[:, :, :], norm_w[:, None, 0:QR].to_broadcast([128, R, QR]), ALU.mult).then_inc(s.mi_qn, 1)
                weight = norm_w[:, None, QR:].to_broadcast([128, R, KVR])
                dve.tensor_tensor(kcat[:, :, 0:KVR], kvn[:, :, :], weight, ALU.mult).then_inc(s.mi_kvn, 1)
                dve.tensor_tensor(kcat[:, :, KVR + ROPE:], kvn[:, :, :], weight, ALU.mult).then_inc(s.mi_kvn, 1)
                dve.tensor_tensor(m.kv[:, tiles(r), :], kvn[:, :, :], weight, ALU.mult).then_inc(s.mi_kvn, 1)
                wait(dve, s.mi_rope, 2 * r + 2)
                wait(dve, s.mi_kvn, 3 * r + 3)
                dve.tensor_tensor(kcat[:, :, KVR:KVR + ROPE], kcat[:, :, KVR:KVR + ROPE], kr[:, :, :], ALU.add).then_inc(s.mi_kcat, 1)

            def keep_qk(r, a):
                wait(dve, s.mi_qk_turned, 3 * r + a + 1)
                dve.tensor_scalar(m.qkT[:, a, tokens(r)], pB[:, a % 2, :], 1.0, None, ALU.mult).then_inc(s.mi_qk_done, 1)

            def add_experts(r, t):
                i = r * R + t
                if t == 0:
                    wait(dve, s.mi_gates, r + 1)
                for e in range(E):
                    src = pE[:, e // 2, e % 2 * D:(e % 2 + 1) * D]
                    if e % 2 == 0:
                        wait(dve, s.mi_experts_ready, i * (E // 2) + e // 2 + 1)
                    if e == 0:
                        dve.tensor_scalar(moe[:, t, :], src, gates[:, t, 0:1], None, ALU.mult).then_inc(s.mi_expert_added, 1)
                    else:
                        wait(dve, s.mi_expert_added, i * E + e)
                        dve.scalar_tensor_tensor(moe[:, t, :], src, gates[:, t, e:e + 1], moe[:, t, :], ALU.mult, ALU.add)\
                            .then_inc(s.mi_expert_added, 1)

            def start(r):
                xn0(r)
                gate_bias(r)
                gated(r)
                hat_of(r)
                residual(r)
                xn1_of(r)
                wait(dve, s.mi_weights, 16 * LOADS)

            def body(r, more=True):
                if more:
                    xn0(r + 1)
                route(r)
                if more:
                    gate_bias(r + 1)
                gates_of(r)
                if more:
                    gated(r + 1)
                latents(r)
                add_experts(r, 0)
                keep_qk(r, 0)
                keep_qk(r, 1)
                if more:
                    hat_of(r + 1)
                add_experts(r, 1)
                keep_qk(r, 2)
                if more:
                    residual(r + 1)
                add_experts(r, 2)
                if more:
                    xn1_of(r + 1)
                add_experts(r, 3)
                wait(dve, s.mi_bias_ready, r + 1)
                wait(dve, s.mi_expert_added, (r + 1) * R * E)
                dve.tensor_tensor(m.moe[:, tiles(r), :], moe[:, :, :], pA[:, :, :].rearrange("p a (b d) -> p (a b) d", b=2), ALU.add)\
                    .then_inc(s.mi_moe, 1)
                wait(dve, s.mi_moe, r + 1)

            for k in range(KD):
                dve.tensor_copy(spread[:, :, k, :], m.bcT[:, k, :, None].to_broadcast([128, B, 128])).then_inc(s.mi_spread, 1)
            wait(dve, s.mi_bc_ready, 1)
            for i in range(2):
                dve.tensor_scalar(half_bc[:, 2 * i:2 * i + 2, :].rearrange("p b d -> p (b d)"), pE[:, i, :], 0.5, None, ALU.mult).then_inc(s.mi_half_bc, 1)
            wait(dve, s.mi_half_bc, 2)
            run(dve, start, body, lambda r: body(r, more=False))

        @block.gpsimd
        def _(pool):
            def rstd(which, n):
                wait(pool, s.mi_aggr, R * (n + 1))
                pool.tensor_tensor(rs[:, which, :, :], mv[:, which, :, 1:2], eps[:, which:which + 1, None].to_broadcast([128, R, 1]), ALU.add)\
                    .then_inc(s.mi_eps, 1)
                wait(pool, s.mi_eps, n + 1)
                pool.tensor_tensor(rs[:, which, :, :], rs[:, which, :, :], m.minus_half[:, 0:R, None], ALU.pow).then_inc(s.mi_rstd, 1)

            def start(r):
                rstd(0, 2 * r)
                rstd(1, 2 * r + 1)

            def body(r, more=True):
                wait(pool, s.mi_ssd, 2 * r + 2)
                pool.tensor_tensor(rsd[:, :, :], ssd[:, :, :], inv[:, :, :], ALU.mult).then_inc(s.mi_rsd_chain, 1)
                wait(pool, s.mi_rsd_chain, 2 * r + 1)
                pool.tensor_tensor(rsd[:, :, :], rsd[:, :, :], eps[:, 0:1, None].to_broadcast([128, R, 2]), ALU.add).then_inc(s.mi_rsd_chain, 1)
                wait(pool, s.mi_rsd_chain, 2 * r + 2)
                pool.tensor_tensor(rsd[:, :, :], rsd[:, :, :], m.minus_half[:, 0:2 * R].rearrange("p (t a) -> p t a", a=2), ALU.pow).then_inc(s.mi_rsd, 1)
                if more:
                    start(r + 1)

            pool.memset(inv[:, :, 0], 1.0 / QR).then_inc(s.mi_const, 1)
            pool.memset(inv[:, :, 1], 1.0 / KVR).then_inc(s.mi_const, 1)
            pool.memset(eps[:, 0:1], 1e-6).then_inc(s.mi_const, 1)
            pool.memset(eps[:, 1:2], 1e-5).then_inc(s.mi_const, 1)
            wait(pool, s.mi_const, 4)
            run(pool, start, body, lambda r: body(r, more=False))


def attention(nc, m, io):
    SCALE = 1.0 / float(np.sqrt(NOPE + ROPE))
    UNITS = AH * CH
    with ExitStack() as ctx:
        def sb(name, shape, dt=F32):
            return ctx.enter_context(nc.sbuf_tensor(name, shape, dt))

        def split(name, shape):
            return [sb(f"{name}_hi", shape, F32R), sb(f"{name}_lo", shape, F32R)]

        up_q, up_kv = m.up_q, m.up_kv
        woT = m.wide.rearrange("p (h n) -> p h n", h=AH)
        oT = m.wide.rearrange("p (a t) -> p a t", a=APAIRS)
        wq, wqs = sb("at_wq", [128, AH, KVR + ROPE]), sb("at_wqs", [128, APAIRS, 2 * ROPE])
        wq2, wqs2 = split("at_wq2", [128, AH, KVR + ROPE]), split("at_wqs2", [128, APAIRS, 2 * ROPE])
        wvo = sb("at_wvo", [128, APAIRS, D])
        qcos = [sb(f"at_cos{i}", [128, T]) for i in range(2)]
        qsin = sb("at_sin", [128, T])
        qin, kin = split("at_qin", [128, T]), [split(f"at_kin{i}", [128, T]) for i in range(2)]
        vin = sb("at_vin", [128, CH, KVR])
        g1 = m.x[:, 0:CH, :]
        q, qsw = sb("at_q", [128, T]), sb("at_qsw", [128, T])
        qT = [split(f"at_qT{i}", [128, T]) for i in range(2)]
        PR = [sb(f"at_P{i}", [128, T]) for i in range(3)]
        PT = [sb(f"at_PT{i}", [128, T]) for i in range(3)]
        nm, sm, rc = (sb(f"at_{n}", [128, 2, 2, CH]) for n in ("nm", "sm", "rc"))
        o = sb("at_o", [128, CH, 2, KVR])
        psS = [ctx.enter_context(nc.psum_tensor(f"at_S{i}", [128, 512], F32)) for i in range(3)]
        psT = [ctx.enter_context(nc.psum_tensor(f"at_T{i}", [128, 512], F32)) for i in range(2)]
        psQ = [ctx.enter_context(nc.psum_tensor(f"at_Q{i}", [128, 512], F32)) for i in range(2)]
        psO = ctx.enter_context(nc.psum_tensor("at_O", [128, 512], F32))
        s = sems(nc, ctx, "at_loaded", "at_w_ready0", "at_w_ready1", "at_w_done0", "at_w_done1", "at_w_hi", "at_w_split", "at_in",
                 "at_g1", "at_q_ready", "at_cos", "at_sin", "at_qsum", "at_q_hi", "at_qT", "at_s_ready",
                 "at_nm", "at_exp", "at_turned", "at_evA", "at_evD", "at_pv", "at_rc", "at_o",
                 "at_oT_ready", "at_oT", "at_out_ready", "at_sg", "at_fin", "at_stored")
        block = ctx.enter_context(nc.Block())
        LOADS = 6

        def steps():
            def unit(n):
                return n if 0 <= n < UNITS else None

            divide = {8 * pr + 7 + CH: pr for pr in range(APAIRS)}
            turn_out = {min(8 * pr + 10 + CH, UNITS + CH): pr for pr in range(APAIRS)}
            for n in range(UNITS + CH + 1):
                yield n, unit(n), unit(n - 2), unit(n - 3), unit(n - 4), divide.get(n), turn_out.get(n)

        STEPS = list(steps())
        AHEAD = 2

        def of_pair(t, n):
            return t[:, n // 8 % 2, n // 4 % 2, n % 4:n % 4 + 1]

        @block.sync
        def _(sp):
            for par in range(2):
                at = ROPE * (1 - par)
                sp.dma_start(wq[:, par::2, at:at + ROPE], io.wq_ropeT[:, par::2, :]).then_inc(s.at_loaded, 16)
                sp.dma_start(qcos[par][:, :], io.c_qcos[par]).then_inc(s.at_loaded, 16)
            sp.dma_start(wqs[:, :, :], io.wq_swapT).then_inc(s.at_loaded, 16)
            sp.dma_start(qsin[:, :], io.c_qsin).then_inc(s.at_loaded, 16)
            sp.wait_ge(s.at_loaded, 16 * LOADS)
            out = io.out.rearrange("b (c p) d -> b p c d", p=128)
            for b in range(B):
                sp.wait_ge(s.at_fin, b + 1)
                sp.dma_start(out[b], m.acc[:, b * CH:(b + 1) * CH, :]).then_inc(s.at_stored, 16)
            sp.wait_ge(s.at_stored, 16 * B)

        @block.tensor
        def _(pe):
            def queries(b, h):
                wait(pe, s.at_cos, b * AH + h)
                mm = split_matmul(pe, psQ[0][:, :], [w[:, h, :] for w in wq2], [x[:, :] for x in qin])
                mm.then_inc(s.at_q_ready, 1)
                if h % 2 == 0:
                    pr = h // 2
                    wait(pe, s.at_sin, b * APAIRS + pr)
                    if pr >= 3:
                        pe.wait_ge(s.at_oT, b * APAIRS + pr - 2)
                    mm = split_matmul(pe, psQ[1][:, :], [w[:, pr, :] for w in wqs2], [x[:, :] for x in qin])
                    mm.then_inc(s.at_q_ready, 1)

            def scores(b, n):
                h, i = n // CH, n % CH
                if i == 0:
                    pe.wait_ge(s.at_qT, b * AH + h + 1)
                if n >= 3:
                    pe.wait_ge(s.at_exp, b * UNITS + n - 2)
                w = (i + 1) * 128
                split_matmul(pe, psS[n % 3][:, 0:w], [x[:, i * 128:(i + 1) * 128] for x in qT[h % 2]],
                             [x[:, 0:w] for x in kin[h % 2]], last=False)
                pe.matmul(psS[n % 3][:, w - 128:w], m.identb[:, :], m.maskb[:, 1, :], start=False, stop=True)\
                    .then_inc(s.at_s_ready, 1)

            def evacuated(b, n):
                if n % CH == CH - 1:
                    pe.wait_ge(s.at_evD, b * AH + n // CH + 1)
                else:
                    pe.wait_ge(s.at_evA, b * AH * (CH - 1) + n // CH * (CH - 1) + n % CH + 1)

            def turn(b, n):
                pe.wait_ge(s.at_exp, b * UNITS + n + 1)
                if n >= 2:
                    evacuated(b, n - 2)
                for j in range(n % CH + 1):
                    mm = pe.transpose(psT[n % 2][:, j * 128:(j + 1) * 128], PR[n % 3][:, j * 128:(j + 1) * 128], m.ident[:, :])
                mm.then_inc(s.at_turned, 1)

            def values(b, n):
                evacuated(b, n)
                if n % 8 == 0 and n:
                    pe.wait_ge(s.at_o, b * APAIRS + n // 8)
                i = n % CH
                at = n % 8 * KVR
                for j in range(i + 1):
                    mm = pe.matmul(psO[:, at:at + KVR], PT[n % 3][:, j * 128:(j + 1) * 128], vin[:, j, :],
                                   start=(j == 0), stop=(j == i))
                mm.then_inc(s.at_pv, 1)

            def turn_out(b, pr):
                pe.wait_ge(s.at_o, b * APAIRS + pr + 1)
                pe.wait_ge(s.at_sin, b * APAIRS + min(pr + 3, APAIRS))
                for i in range(CH):
                    mm = pe.transpose(psQ[1][:, i * 128:(i + 1) * 128], o[:, i, :, :].rearrange("p h r -> p (h r)"), m.ident[:, :])
                mm.then_inc(s.at_oT_ready, 1)

            for h in range(AH):
                at = h // 2 * KVR
                pe.matmul(psS[h % 2][:, at:at + KVR], up_q[:, h, :], up_kv[:, h, 0, :], start=True, stop=True)\
                    .then_inc(s.at_w_ready0, 1)
            for pr in range(APAIRS):
                if pr >= 2:
                    pe.wait_ge(s.at_w_done1, pr - 1)
                for hh in range(2):
                    h = 2 * pr + hh
                    mm = pe.matmul(psT[pr % 2][hh * KVR:(hh + 1) * KVR, 0:D], up_kv[:, h, 1, :], woT[:, h, :], start=True, stop=True)
                mm.then_inc(s.at_w_ready1, 1)
            pe.wait_ge(s.at_w_done1, APAIRS)
            pe.wait_ge(s.at_w_split, 3)
            def first_queries(b):
                pe.wait_ge(s.at_in, b * 7 + 7)
                queries(b, 0)
                queries(b, 1)

            def step(b, n, made, turned, _, applied, __, turned_out):
                if n % CH == CH - 1 and n // CH + 2 < AH:
                    queries(b, n // CH + 2)
                if made is not None:
                    scores(b, made)
                if turned is not None:
                    turn(b, turned)
                if turned_out is not None:
                    turn_out(b, turned_out)
                if applied is not None:
                    values(b, applied)

            def output(half):
                for c in range(2):
                    for pr in range(APAIRS):
                        at = (2 * half + c) * 128
                        mm = pe.matmul(psT[half][:, c * D:(c + 1) * D], oT[:, pr, at:at + 128], wvo[:, pr, :],
                                       start=(pr == 0), stop=(pr == APAIRS - 1))
                mm.then_inc(s.at_out_ready, 1)

            def row(b, last=False):
                for st in STEPS[AHEAD:]:
                    step(b, *st)
                pe.wait_ge(s.at_oT, (b + 1) * APAIRS)
                if last:
                    output(0)
                    output(1)
                    return
                first_queries(b + 1)
                output(0)
                for st in STEPS[:AHEAD]:
                    step(b + 1, *st)
                output(1)
                pe.wait_ge(s.at_sg, 2 * b + 2)

            first_queries(0)
            for st in STEPS[:AHEAD]:
                step(0, *st)
            with pe.Fori(0, B - 1) as b:
                row(b)
            row(B - 1, last=True)

        @block.scalar
        def _(act):
            def high(b, h):
                act.wait_ge(s.at_qsum, b * AH + h + 1)
                act.activation(qT[h % 2][0][:, :], q[:, :], ACT.Copy).then_inc(s.at_q_hi, 1)

            act.activation(m.moe[:, :, :], m.moe[:, :, :], ACT.Silu).then_inc(s.at_g1, 1)
            act.wait_ge(s.at_loaded, 16 * LOADS)
            for par in range(2):
                at = ROPE * (1 - par)
                act.activation(wq[:, par::2, at:at + ROPE], wq[:, par::2, at:at + ROPE], ACT.Copy, scale=SCALE).then_inc(s.at_w_done0, 1)
            act.activation(wqs[:, :, :], wqs[:, :, :], ACT.Copy, scale=SCALE).then_inc(s.at_w_done0, 1)
            for par in range(2):
                act.wait_ge(s.at_w_ready0, AH - 1 + par)
                at = ROPE * par
                act.activation(wq[:, par::2, at:at + KVR], psS[par][:, :].rearrange("p (h r) -> p h r", r=KVR), ACT.Copy, scale=SCALE)\
                    .then_inc(s.at_w_done0, 1)
                act.wait_ge(s.at_w_done0, 4 + par)
                act.activation(wq2[0][:, par::2, :], wq[:, par::2, :], ACT.Copy).then_inc(s.at_w_hi, 1)
            act.activation(wqs2[0][:, :, :], wqs[:, :, :], ACT.Copy).then_inc(s.at_w_hi, 1)

            def step(b, n, made, _, left, __, ___, turned_out):
                if left is not None and left % CH < CH - 1:
                    w = (left % CH + 1) * 128
                    act.wait_ge(s.at_turned, b * UNITS + left + 1)
                    act.activation(PT[left % 3][:, 0:w], psT[left % 2][:, 0:w], ACT.Copy).then_inc(s.at_evA, 1)
                if made is not None:
                    w = (n % CH + 1) * 128
                    act.wait_ge(s.at_nm, b * UNITS + n + 1)
                    act.activation(PR[n % 3][:, 0:w], psS[n % 3][:, 0:w], ACT.Exp, bias=of_pair(nm, n),
                                   accum_out=of_pair(sm, n)).then_inc(s.at_exp, 1)
                    if n % CH == 1 and n // CH < AH - 1:
                        high(b, n // CH + 1)
                if turned_out is not None:
                    act.wait_ge(s.at_oT_ready, b * APAIRS + turned_out + 1)
                    act.activation(oT[:, turned_out, :], psQ[1][:, :], ACT.Copy).then_inc(s.at_oT, 1)

            def begin(b):
                high(b, 0)
                for st in STEPS[:AHEAD]:
                    step(b, *st)

            def row(b, last=False):
                for st in STEPS[AHEAD:]:
                    step(b, *st)
                if not last:
                    begin(b + 1)

            begin(0)
            with act.Fori(0, B - 1) as b:
                row(b)
            row(B - 1, last=True)

        @block.vector
        def _(dve):
            def rope(b, h):
                k = b * (AH + APAIRS) + h + (h + 1) // 2
                dve.wait_ge(s.at_q_ready, k + 1)
                wait(dve, s.at_qT, b * AH + h)
                dve.tensor_tensor(q[:, :], psQ[0][:, :], qcos[h % 2][:, :], ALU.mult).then_inc(s.at_cos, 1)
                if h % 2 == 0:
                    dve.wait_ge(s.at_q_ready, k + 2)
                    dve.tensor_tensor(qsw[:, :], psQ[1][:, :], qsin[:, :], ALU.mult).then_inc(s.at_sin, 1)

            def split_part(b, i):
                part = ([qin] + kin)[i]
                src = m.qkT[:, i, bass.ds(b * T, T)]
                dve.tensor_scalar(part[0][:, :], src, 1.0, None, ALU.mult).then_inc(s.at_in, 1)
                dve.wait_ge(s.at_in, b * 7 + 2 * i + 1)
                dve.tensor_tensor(part[1][:, :], src, part[0][:, :].bitcast(F32), ALU.subtract).then_inc(s.at_in, 1)

            def values_of(b):
                dve.tensor_scalar(vin[:, :, :], m.kv[:, bass.ds(b * CH, CH), :], 1.0, None, ALU.mult).then_inc(s.at_in, 1)

            def step(b, n, made, _, left, __, divided, ___):
                if left is not None and left % CH == CH - 1:
                    dve.wait_ge(s.at_turned, b * UNITS + left + 1)
                    dve.tensor_copy(PT[left % 3][:, :], psT[left % 2][:, :]).then_inc(s.at_evD, 1)
                if made is not None:
                    w = (n % CH + 1) * 128
                    dve.wait_ge(s.at_s_ready, b * UNITS + n + 1)
                    dve.tensor_reduce(of_pair(nm, n), psS[n % 3][:, 0:w], AX, ALU.max, negate=True).then_inc(s.at_nm, 1)
                    if n % CH == 0 and n // CH < AH - 1:
                        rope(b, n // CH + 1)
                if divided is not None:
                    par = divided % 2
                    dve.wait_ge(s.at_exp, b * UNITS + divided * 8 + 8)
                    dve.reciprocal(rc[:, par, :, :], sm[:, par, :, :]).then_inc(s.at_rc, 1)
                    dve.wait_ge(s.at_rc, b * APAIRS + divided + 1)
                    dve.wait_ge(s.at_pv, b * UNITS + divided * 8 + 8)
                    if divided:
                        dve.wait_ge(s.at_oT_ready, b * APAIRS + divided)
                    dve.tensor_tensor(o[:, :, :, :].rearrange("p i h r -> p h i r"),
                                      psO[:, :].rearrange("p (h i r) -> p h i r", h=2, i=CH),
                                      rc[:, par, :, :, None].to_broadcast([128, 2, CH, KVR]), ALU.mult).then_inc(s.at_o, 1)

            def gated(b, half):
                dve.wait_ge(s.at_out_ready, 2 * b + half + 1)
                dve.tensor_tensor(g1[:, 2 * half:2 * half + 2, :], psT[half][:, :].rearrange("p (c d) -> p c d", d=D),
                                  m.moe[:, bass.ds(b * CH + 2 * half, 2), :], ALU.mult).then_inc(s.at_sg, 1)

            def row(b, last=False):
                for st in STEPS[AHEAD:]:
                    step(b, *st)
                    if not last and 0 <= st[0] - UNITS < 3:
                        split_part(b + 1, st[0] - UNITS)
                tiles = bass.ds(b * CH, CH)
                if not last:
                    values_of(b + 1)
                    rope(b + 1, 0)
                dve.wait_ge(s.at_g1, 1)
                gated(b, 0)
                if not last:
                    for st in STEPS[:AHEAD]:
                        step(b + 1, *st)
                gated(b, 1)
                dve.wait_ge(s.at_sg, 2 * b + 2)
                dve.tensor_tensor(m.acc[:, tiles, :], g1[:, :, :], m.acc[:, tiles, :], ALU.add).then_inc(s.at_fin, 1)
                if not last:
                    dve.wait_ge(s.at_fin, b + 1)

            for i in range(3):
                split_part(0, i)
            values_of(0)
            dve.wait_ge(s.at_loaded, 16 * LOADS)
            low_parts = [(wq2, wq, slice(par, None, 2)) for par in range(2)] + [(wqs2, wqs, slice(None))]
            for pr in range(APAIRS):
                dve.wait_ge(s.at_w_ready1, pr + 1)
                dve.tensor_copy(wvo[:, pr, :], psT[pr % 2][:, 0:D]).then_inc(s.at_w_done1, 1)
                if pr < 3:
                    split, whole, heads = low_parts[pr]
                    dve.wait_ge(s.at_w_hi, pr + 1)
                    dve.tensor_tensor(split[1][:, heads, :], whole[:, heads, :], split[0][:, heads, :].bitcast(F32), ALU.subtract)\
                        .then_inc(s.at_w_split, 1)
            rope(0, 0)
            for st in STEPS[:AHEAD]:
                step(0, *st)
            with dve.Fori(0, B - 1) as b:
                row(b)
            row(B - 1, last=True)

        @block.gpsimd
        def _(pool):
            with pool.Fori(0, B) as b:
                for h in range(AH):
                    n = b * AH + h
                    half = slice(KVR * (1 - h % 2), KVR * (2 - h % 2))
                    pool.wait_ge(s.at_cos, n + 1)
                    pool.wait_ge(s.at_sin, b * APAIRS + h // 2 + 1)
                    pool.tensor_tensor(q[half, :], q[half, :], qsw[half, :], ALU.add).then_inc(s.at_qsum, 1)
                    pool.wait_ge(s.at_q_hi, n + 1)
                    pool.tensor_tensor(qT[h % 2][1][:, :], q[:, :], qT[h % 2][0][:, :].bitcast(F32), ALU.subtract).then_inc(s.at_qT, 1)


def constants():
    q = np.arange(128)
    keep_up = q[:, None] <= q[None, :]
    c = {"c_ident": np.eye(128, dtype=np.float32), "c_triu": keep_up.astype(np.float32),
         "c_identb": np.eye(128).astype(mybir.dt.np(BF16)),
         "c_maskb": np.stack([np.where(keep_up, 0.0, MASKED), np.where(keep_up.T, 0.0, MASKED)], 1).astype(mybir.dt.np(BF16)),
         "c_onehot": np.stack([np.tile(np.eye(H), (3, 1)), -np.tile(np.eye(H), (3, 1))], 1).astype(mybir.dt.np(BF16))}
    f = (1.0 / 10000.0 ** (np.arange(0, ROPE, 2, dtype=np.float32) / ROPE)).astype(np.float32)
    ang = np.outer(np.arange(T, dtype=np.float32), f)
    cos = np.concatenate([np.cos(ang), np.cos(ang)], 1).astype(np.float32)
    sin = np.concatenate([-np.sin(ang), np.sin(ang)], 1).astype(np.float32)
    c["c_kcos"] = np.ascontiguousarray(cos.reshape(CH, 128, ROPE).transpose(1, 0, 2))
    c["c_ksin"] = np.ascontiguousarray(sin.reshape(CH, 128, ROPE).transpose(1, 0, 2))
    one = np.ones((KVR, T), np.float32)
    c["c_qcos"] = np.stack([np.concatenate([one, cos.T]), np.concatenate([cos.T, one])])
    c["c_qsin"] = np.concatenate([sin.T, sin.T])
    e = np.arange(E)
    c["c_before"] = np.ascontiguousarray(np.broadcast_to((e[None, :] < e[:, None]).astype(np.float32), (128, E, E)))
    return c


def layouts(i):
    win = i["L0_attn_Win"]
    x0, z0, b0, c0 = 0, H * P, 2 * H * P, 2 * H * P + H * N
    a = {"x": i["L0_attn_x"], "A_log": i["L0_attn_A_log"], "dt_bias": i["L0_attn_dt_bias"],
         "w_dt": np.ascontiguousarray(win[c0 + H * N:].T)}
    pack = np.empty((PAIRS, 128, PACK), np.float32)
    for p in range(PAIRS):
        rows = [win[x0 + p * 128:x0 + (p + 1) * 128], win[z0 + p * 128:z0 + (p + 1) * 128]]
        taps = [i["L0_attn_conv_w_x"][2 * p:2 * p + 2].reshape(128, TAPS)]
        for h in (2 * p, 2 * p + 1):
            rows += [win[b0 + h * N:b0 + (h + 1) * N], win[c0 + h * N:c0 + (h + 1) * N]]
            taps += [i["L0_attn_conv_w_b"][h], i["L0_attn_conv_w_c"][h]]
        w = np.concatenate(rows).T
        pack[p, :, 0:PACK_CONV] = w.reshape(KD, 128, CHANNELS).transpose(1, 0, 2).reshape(128, -1)
        pack[p, :, PACK_CONV:] = np.concatenate(taps, 1)
    a["w_pack"] = pack
    a["w_out"] = np.ascontiguousarray(i["L0_attn_Wout"].T.reshape(PAIRS, 128, D))
    for n in ("in_gamma", "in_beta", "agg_w", "agg_b", "pn_gamma", "pn_beta", "d1_w", "d2_w", "d2_b", "bc_w",
              "gate_w", "gate_b", "out_gamma", "out_beta"):
        a[n] = i["L0_ffn_" + n]
    a["bc_b"] = np.ascontiguousarray(i["L0_ffn_bc_b"].reshape(KD, 128).T)
    a["d1_b"] = np.ascontiguousarray(i["L0_ffn_d1_b"].reshape(HID // 128, 128).T)
    turned = np.concatenate([np.arange(0, ROPE, 2), np.arange(1, ROPE, 2)])
    swapped = np.roll(turned, ROPE // 2)
    wk = i["L1_attn_wk_rope"]
    a["w_down"] = np.ascontiguousarray(np.concatenate(
        [i["L1_attn_wq_down"], i["L1_attn_wkv_down"], wk[turned], wk[swapped], i["L1_ffn_gate_w"]]).T)
    a["q_norm_w"], a["kv_norm_w"] = i["L1_attn_q_norm_w"], i["L1_attn_kv_norm_w"]
    a["wq_up"] = np.ascontiguousarray(i["L1_attn_wq_up"].reshape(AH, NOPE, QR).transpose(1, 0, 2))
    a["wkv_up"] = np.ascontiguousarray(i["L1_attn_wkv_up"].reshape(AH, 2, NOPE, KVR).transpose(2, 0, 1, 3))
    wr = i["L1_attn_wq_rope"].reshape(AH, ROPE, QR)
    a["wq_ropeT"] = np.ascontiguousarray(wr[:, turned].transpose(2, 0, 1))
    swap = wr[:, swapped].reshape(APAIRS, 2, ROPE, QR)[:, ::-1]
    a["wq_swapT"] = np.ascontiguousarray(swap.transpose(3, 0, 1, 2).reshape(QR, APAIRS, 2 * ROPE))
    a["woT"] = np.ascontiguousarray(i["L1_attn_wo"].T)
    a["expert_w"], a["expert_b"] = i["L1_ffn_expert_w"], i["L1_ffn_expert_b"]
    return a


def program(nc, io):
    m = Buffers()
    with ExitStack() as whole:
        def sb_in(ctx):
            return lambda name, shape, dt=F32: ctx.enter_context(nc.sbuf_tensor(name, shape, dt))

        shared(m, sb_in(whole))
        with ExitStack() as part:
            mixer_buffers(m, sb_in(part))
            norm_and_decay(nc, m, io)
            mixer(nc, m, io)
        sb = sb_in(whole)
        m.moe = sb("moe", [128, TILES, D])
        m.kv = sb("kv", [128, TILES, KVR])
        m.qkT = sb("qkT", [128, 3, TOK])
        middle(nc, m, io)
        attention(nc, m, io)


def kernel(**inputs):
    import concourse.bacc as bacc
    from concourse.bass_utils import run_bass_kernel_spmd

    nc = bacc.Bacc("TRN2", target_bir_lowering=False, num_devices=1)
    arrays = {**layouts({k: np.asarray(v) for k, v in inputs.items()}), **constants()}
    aps = {k: nc.dram_tensor("in_" + k, a.shape, mybir.dt.from_np(a.dtype), kind="ExternalInput").ap()
           for k, a in arrays.items()}
    aps["out"] = nc.dram_tensor("out_0", (B, T, D), F32, kind="ExternalOutput").ap()
    program(nc, namedtuple("Arrays", aps)(**aps))
    r = run_bass_kernel_spmd(nc, [{"in_" + k: np.ascontiguousarray(a) for k, a in arrays.items()}], core_ids=[0])
    return r.results[0]["out_0"]
```
